# Optimizing a Trainium2 kernel written in Bass

```python
import numpy as np
import jax
import jax.numpy as jnp

def _softmax(x, axis=-1):
    return jax.nn.softmax(x, axis=axis)

def _gelu(x):
    return jax.nn.gelu(x, approximate=True)

def _silu(x):
    return jax.nn.silu(x)

def _sigmoid(x):
    return jax.nn.sigmoid(x)

def _layernorm(x, axis=-1, eps=1e-05):
    m = jnp.mean(x, axis=axis, keepdims=True)
    v = jnp.var(x, axis=axis, keepdims=True)
    return (x - m) / jnp.sqrt(v + eps)

def _scatter_add(tgt, idx, src, axis=0):
    return tgt.at[idx].add(src)

def _segment_sum(src, seg, n):
    return jax.ops.segment_sum(src, seg, n)
kernel_name = 'mk_flamingo_gated_d2_seqx_r8_cd1fb4'

def setup_inputs(seed: int=0):
    np.random.seed(seed)
    _w = jnp.asarray

    def _rec_inputs():
        import jax
        import jax.numpy as jnp
        _rk = jax.random.key(seed)
        x = 0.0003765 + 1 * jax.random.normal(jax.random.fold_in(_rk, 1), (16, 128, 256), jnp.float32)
        _lenS = 128 - jax.random.randint(jax.random.fold_in(_rk, 7), (16,), 0, max(1, 128 // 4) + 1, jnp.int32)
        _lenS2 = 128 - jax.random.randint(jax.random.fold_in(_rk, 8), (16,), 0, max(1, 128 // 4) + 1, jnp.int32)
        _ctx_2048P = jax.random.normal(jax.random.fold_in(_rk, 11), (16, 16, 256), jnp.float32)
        _ctx_2048c = jax.random.dirichlet(jax.random.fold_in(_rk, 511), 0.3 * jnp.ones((16,), jnp.float32), (16, 128))
        _ctx_2048t = jnp.einsum('bsk,bkd->bsd', _ctx_2048c, _ctx_2048P)
        _ctx_2048t = _ctx_2048t * jax.lax.rsqrt(jnp.mean(jnp.square(_ctx_2048t)) + 1e-12) * 0.953939
        ctx_2048 = -0.000292821 + 1.00034 * (_ctx_2048t + 0.3 * jax.random.normal(jax.random.fold_in(_rk, 611), (16, 128, 256), jnp.float32))
        _validS = jnp.arange(128)[None, :] < _lenS[:, None]
        _validS2 = jnp.arange(128)[None, :] < _lenS2[:, None]
        _causal = jnp.tril(jnp.ones((128, 128), dtype=bool))
        mask_BxS2_if1 = jnp.where(jnp.ones((16, 128), dtype=bool), 1, 0).astype(jnp.int32)
        _g = jax.random.normal(jax.random.fold_in(_rk, 9001), (2, 2), jnp.float32)
        _g = jnp.sign(_g) * jnp.maximum(jnp.abs(_g), 1.0) + (_g == 0) * 1.0
        g_xattn = _g[0]
        g_ffn = _g[1]
        return (x, ctx_2048, mask_BxS2_if1, g_xattn, g_ffn)
    x, ctx_2048, mask_BxS2_if1, g_xattn, g_ffn = _rec_inputs()

    def _L0_xattn_setup():
        import jax, jax.numpy as jnp
        import numpy as np
        key = jax.random.key(seed)
        k1, k2, k3, k4, k5 = jax.random.split(key, 5)
        B, D_MODEL, L = (2, 128, 256)
        HEAD_DIM = 8
        H = D_MODEL // HEAD_DIM
        return {'k': jax.random.normal(k1, (B, D_MODEL, L), dtype=jnp.float32), 'v': jax.random.normal(k2, (B, D_MODEL, L), dtype=jnp.float32), 'q': jax.random.normal(k3, (B, D_MODEL, L), dtype=jnp.float32), 'ssm_kernel': jax.random.normal(k4, (H, L), dtype=jnp.float32), 'D': jax.random.normal(k5, (H,), dtype=jnp.float32), 'head_dim': HEAD_DIM}
    _L0_xattn_all = _L0_xattn_setup()
    _L0_xattn_in = {k: v for k, v in _L0_xattn_all.items() if k in ('ssm_kernel', 'D')}
    del _L0_xattn_all

    def _L0_ffn_setup():
        import jax, jax.numpy as jnp
        import numpy as np
        H = 256
        I_MOE = 176
        I_SH = 704
        E = 8
        TOP_K = 2
        B, S = (1, 256)

        def _silu_and_mul(gu, inter):
            return jax.nn.silu(gu[..., :inter]) * gu[..., inter:]
        key = jax.random.key(seed)
        ks = jax.random.split(key, 7)
        sc = 0.02
        return {'hidden_states': jax.random.normal(ks[0], (B, S, H), jnp.float32), 'W_router': jax.random.normal(ks[1], (E, H), jnp.float32) * sc, 'W_sgate': jax.random.normal(ks[2], (1, H), jnp.float32) * sc, 'Ws_gate_up': jax.random.normal(ks[3], (H, 2 * I_SH), jnp.float32) * sc, 'Ws_down': jax.random.normal(ks[4], (I_SH, H), jnp.float32) * sc, 'We_gate_up': jax.random.normal(ks[5], (E, H, 2 * I_MOE), jnp.float32) * sc, 'We_down': jax.random.normal(ks[6], (E, I_MOE, H), jnp.float32) * sc}
    _L0_ffn_all = _L0_ffn_setup()
    _L0_ffn_in = {k: v for k, v in _L0_ffn_all.items() if k in ('W_router', 'W_sgate', 'Ws_gate_up', 'Ws_down', 'We_gate_up', 'We_down')}
    del _L0_ffn_all

    def _L1_xattn_setup():
        import jax, jax.numpy as jnp
        import numpy as np
        D_MODEL = 256
        N_HEADS = 32
        N_GROUPS = 8
        HEAD_DIM = D_MODEL // N_HEADS
        BATCH, SEQ = (2, 128)
        NEG_INF = float('-inf')
        key = jax.random.key(seed)
        ks = jax.random.split(key, 9)
        s = 0.02
        return {'Q': jax.random.normal(ks[0], (BATCH, SEQ, D_MODEL), jnp.float32), 'K': jax.random.normal(ks[1], (BATCH, SEQ, D_MODEL), jnp.float32), 'V': jax.random.normal(ks[2], (BATCH, SEQ, D_MODEL), jnp.float32), 'attention_mask': jnp.ones((BATCH, SEQ), jnp.int32), 'w_q': jax.random.normal(ks[3], (D_MODEL, D_MODEL), jnp.float32) * s, 'w_k': jax.random.normal(ks[4], (HEAD_DIM * N_GROUPS, D_MODEL), jnp.float32) * s, 'w_v': jax.random.normal(ks[5], (HEAD_DIM * N_GROUPS, D_MODEL), jnp.float32) * s, 'w_o': jax.random.normal(ks[6], (D_MODEL, D_MODEL), jnp.float32) * s, 'b_o': jnp.zeros((D_MODEL,), jnp.float32)}
    _L1_xattn_all = _L1_xattn_setup()
    _L1_xattn_in = {k: v for k, v in _L1_xattn_all.items() if k in ('w_q', 'w_k', 'w_v', 'w_o', 'b_o')}
    del _L1_xattn_all

    def _L1_ffn_setup():
        import jax, jax.numpy as jnp
        import numpy as np
        B, S, D = (4, 512, 256)
        E, K, I, J = (8, 2, 176, 704)
        CAP_FACTOR = 1.25
        STD = 0.02

        def _moe_routed(x_flat, router, w_up_gate, w_down):
            T, d = x_flat.shape
            logits = jnp.einsum('td,de->te', x_flat, router)
            topk_logits, sel = jax.lax.top_k(logits, K)
            cw = jax.nn.softmax(topk_logits, axis=-1).astype(x_flat.dtype)
            C = int(np.ceil(T * K / E * CAP_FACTOR))
            e_flat = sel.reshape(-1)
            oh = jax.nn.one_hot(e_flat, E, dtype=jnp.int32)
            pos_all = jnp.cumsum(oh, axis=0) - oh
            pos = jnp.take_along_axis(pos_all, e_flat[:, None], axis=1)[:, 0]
            valid = pos < C
            safe_pos = jnp.where(valid, pos, C)
            tok = jnp.repeat(jnp.arange(T), K)
            buf = jnp.zeros((E, C, d), x_flat.dtype).at[e_flat, safe_pos].set(x_flat[tok], mode='drop')
            gate_up = jnp.einsum('ecd,edm->ecm', buf, w_up_gate)
            gate, up = jnp.split(gate_up, [I], axis=-1)
            h = jax.nn.silu(gate) * up
            out_buf = jnp.einsum('eci,eid->ecd', h, w_down)
            gathered = out_buf[e_flat, jnp.minimum(safe_pos, C - 1)]
            gathered = gathered * valid[:, None].astype(x_flat.dtype)
            w = cw.reshape(-1)
            y = jnp.zeros((T, d), x_flat.dtype).at[tok].add(w[:, None] * gathered)
            return y

        def _shared_mlp(x_flat, shared_w_up_gate, shared_w_down):
            gu = jnp.einsum('td,dm->tm', x_flat, shared_w_up_gate)
            gate, up = jnp.split(gu, [J], axis=-1)
            return jnp.einsum('tm,md->td', jax.nn.silu(gate) * up, shared_w_down)
        key = jax.random.key(seed)
        kx, kr, ku, kd, ksu, ksd = jax.random.split(key, 6)
        x = jax.random.normal(kx, (B, S, D), dtype=jnp.float32)
        router = STD * jax.random.truncated_normal(kr, -3, 3, (D, E), dtype=jnp.float32)
        w_up_gate = STD * jax.random.truncated_normal(ku, -3, 3, (E, D, 2 * I), dtype=jnp.float32)
        w_down = STD * jax.random.truncated_normal(kd, -3, 3, (E, I, D), dtype=jnp.float32)
        shared_w_up_gate = STD * jax.random.truncated_normal(ksu, -3, 3, (D, 2 * J), dtype=jnp.float32)
        shared_w_down = STD * jax.random.truncated_normal(ksd, -3, 3, (J, D), dtype=jnp.float32)
        return {'x': x, 'router': router, 'w_up_gate': w_up_gate, 'w_down': w_down, 'shared_w_up_gate': shared_w_up_gate, 'shared_w_down': shared_w_down}
    _L1_ffn_all = _L1_ffn_setup()
    _L1_ffn_in = {k: v for k, v in _L1_ffn_all.items() if k in ('router', 'w_up_gate', 'w_down', 'shared_w_up_gate', 'shared_w_down')}
    del _L1_ffn_all
    return {'x': x, 'ctx_2048': ctx_2048, 'mask_BxS2_if1': mask_BxS2_if1, 'g_xattn': g_xattn, 'g_ffn': g_ffn, 'L0_xattn_ssm_kernel': _L0_xattn_in['ssm_kernel'], 'L0_xattn_D': _L0_xattn_in['D'], 'L0_ffn_W_router': _L0_ffn_in['W_router'], 'L0_ffn_W_sgate': _L0_ffn_in['W_sgate'], 'L0_ffn_Ws_gate_up': _L0_ffn_in['Ws_gate_up'], 'L0_ffn_Ws_down': _L0_ffn_in['Ws_down'], 'L0_ffn_We_gate_up': _L0_ffn_in['We_gate_up'], 'L0_ffn_We_down': _L0_ffn_in['We_down'], 'L1_xattn_w_q': _L1_xattn_in['w_q'], 'L1_xattn_w_k': _L1_xattn_in['w_k'], 'L1_xattn_w_v': _L1_xattn_in['w_v'], 'L1_xattn_w_o': _L1_xattn_in['w_o'], 'L1_xattn_b_o': _L1_xattn_in['b_o'], 'L1_ffn_router': _L1_ffn_in['router'], 'L1_ffn_w_up_gate': _L1_ffn_in['w_up_gate'], 'L1_ffn_w_down': _L1_ffn_in['w_down'], 'L1_ffn_shared_w_up_gate': _L1_ffn_in['shared_w_up_gate'], 'L1_ffn_shared_w_down': _L1_ffn_in['shared_w_down']}

def reference(x, ctx_2048, mask_BxS2_if1, g_xattn, g_ffn, L0_xattn_ssm_kernel, L0_xattn_D, L0_ffn_W_router, L0_ffn_W_sgate, L0_ffn_Ws_gate_up, L0_ffn_Ws_down, L0_ffn_We_gate_up, L0_ffn_We_down, L1_xattn_w_q, L1_xattn_w_k, L1_xattn_w_v, L1_xattn_w_o, L1_xattn_b_o, L1_ffn_router, L1_ffn_w_up_gate, L1_ffn_w_down, L1_ffn_shared_w_up_gate, L1_ffn_shared_w_down):
    import jax
    import jax.numpy as jnp

    def _L0_xattn_ref(k, v, q, ssm_kernel, D, head_dim):
        import jax, jax.numpy as jnp
        import numpy as np
        B, HD, L = k.shape
        H = HD // head_dim
        fft_size = 2 * L
        k_ = k.reshape(B, H, head_dim, L)
        v_ = v.reshape(B, H, head_dim, L)
        q_ = q.reshape(B, H, head_dim, L)
        kv = jnp.einsum('bhil,bhjl->bijhl', k_, v_)
        kv_f = jnp.fft.rfft(kv, n=fft_size)
        kernel_f = jnp.fft.rfft(ssm_kernel, n=fft_size)
        y = jnp.fft.irfft(kv_f * kernel_f, n=fft_size)[..., :L]
        out = y + kv * D[None, None, None, :, None]
        out = jnp.einsum('bijhl,bhil->bjhl', out, q_)
        out = jnp.transpose(out, (0, 2, 1, 3)).reshape(B, H * head_dim, L)
        return out.astype(k.dtype)

    def _L0_ffn_ref(hidden_states, W_router, W_sgate, Ws_gate_up, Ws_down, We_gate_up, We_down):
        import jax, jax.numpy as jnp
        import numpy as np
        H = 256
        I_MOE = 176
        I_SH = 704
        E = 8
        TOP_K = 2
        B, S = (1, 256)

        def _silu_and_mul(gu, inter):
            return jax.nn.silu(gu[..., :inter]) * gu[..., inter:]
        orig_shape = hidden_states.shape
        x = hidden_states.reshape(-1, H)
        T = x.shape[0]
        logits = x @ W_router.T
        probs = jax.nn.softmax(logits.astype(jnp.float32), axis=-1)
        rw, sel = jax.lax.top_k(probs, TOP_K)
        rw = rw.astype(x.dtype)
        combine = jnp.zeros((T, E), x.dtype).at[jnp.arange(T)[:, None], sel].add(rw)
        sh = _silu_and_mul(x @ Ws_gate_up, I_SH) @ Ws_down
        shared_out = sh * jax.nn.sigmoid(x @ W_sgate.T)
        gu = jnp.einsum('th,ehi->eti', x, We_gate_up)
        h = _silu_and_mul(gu, I_MOE)
        eo = jnp.einsum('eti,eih->eth', h, We_down)
        sparse_out = jnp.einsum('eth,te->th', eo, combine)
        return (shared_out + sparse_out).reshape(orig_shape)

    def _L1_xattn_ref(Q, K, V, attention_mask, w_q, w_k, w_v, w_o, b_o):
        import jax, jax.numpy as jnp
        import numpy as np
        D_MODEL = 256
        N_HEADS = 32
        N_GROUPS = 8
        HEAD_DIM = D_MODEL // N_HEADS
        BATCH, SEQ = (2, 128)
        NEG_INF = float('-inf')
        B, S, D = Q.shape
        G, HG, HD = (N_GROUPS, N_HEADS // N_GROUPS, HEAD_DIM)
        q = (Q @ w_q.T).reshape(B, S, G, HG, HD)
        k = (K @ w_k.T).reshape(B, S, G, HD)
        v = (V @ w_v.T).reshape(B, S, G, HD)
        scale = jnp.sqrt(jnp.float32(HD))
        scores = jnp.einsum('bnghd,bmgd->bnghm', q, k) / scale
        pad = (attention_mask == 0)[:, None, None, None, :]
        scores = jnp.where(pad, NEG_INF, scores)
        causal = jnp.tril(jnp.ones((S, S), bool))[None, :, None, None, :]
        scores = jnp.where(causal, scores, NEG_INF)
        attn = jax.nn.softmax(scores, axis=-1)
        out = jnp.einsum('bnghm,bmgd->bnghd', attn, v).reshape(B, S, D)
        return out @ w_o.T + b_o

    def _L1_ffn_ref(x, router, w_up_gate, w_down, shared_w_up_gate, shared_w_down):
        import jax, jax.numpy as jnp
        import numpy as np
        B, S, D = (4, 512, 256)
        E, K, I, J = (8, 2, 176, 704)
        CAP_FACTOR = 1.25
        STD = 0.02

        def _moe_routed(x_flat, router, w_up_gate, w_down):
            T, d = x_flat.shape
            logits = jnp.einsum('td,de->te', x_flat, router)
            topk_logits, sel = jax.lax.top_k(logits, K)
            cw = jax.nn.softmax(topk_logits, axis=-1).astype(x_flat.dtype)
            C = int(np.ceil(T * K / E * CAP_FACTOR))
            e_flat = sel.reshape(-1)
            oh = jax.nn.one_hot(e_flat, E, dtype=jnp.int32)
            pos_all = jnp.cumsum(oh, axis=0) - oh
            pos = jnp.take_along_axis(pos_all, e_flat[:, None], axis=1)[:, 0]
            valid = pos < C
            safe_pos = jnp.where(valid, pos, C)
            tok = jnp.repeat(jnp.arange(T), K)
            buf = jnp.zeros((E, C, d), x_flat.dtype).at[e_flat, safe_pos].set(x_flat[tok], mode='drop')
            gate_up = jnp.einsum('ecd,edm->ecm', buf, w_up_gate)
            gate, up = jnp.split(gate_up, [I], axis=-1)
            h = jax.nn.silu(gate) * up
            out_buf = jnp.einsum('eci,eid->ecd', h, w_down)
            gathered = out_buf[e_flat, jnp.minimum(safe_pos, C - 1)]
            gathered = gathered * valid[:, None].astype(x_flat.dtype)
            w = cw.reshape(-1)
            y = jnp.zeros((T, d), x_flat.dtype).at[tok].add(w[:, None] * gathered)
            return y

        def _shared_mlp(x_flat, shared_w_up_gate, shared_w_down):
            gu = jnp.einsum('td,dm->tm', x_flat, shared_w_up_gate)
            gate, up = jnp.split(gu, [J], axis=-1)
            return jnp.einsum('tm,md->td', jax.nn.silu(gate) * up, shared_w_down)
        b, s, d = x.shape
        x_flat = x.reshape(b * s, d)
        routed = _moe_routed(x_flat, router, w_up_gate, w_down)
        shared = _shared_mlp(x_flat, shared_w_up_gate, shared_w_down)
        return (routed + shared).reshape(b, s, d)
    x = x + jnp.tanh(g_xattn[0]) * _L0_xattn_ref(ctx_2048, ctx_2048, _layernorm(x, axis=-1), L0_xattn_ssm_kernel, L0_xattn_D, 8)
    x = x + jnp.tanh(g_ffn[0]) * _L0_ffn_ref(_layernorm(x, axis=-1), L0_ffn_W_router, L0_ffn_W_sgate, L0_ffn_Ws_gate_up, L0_ffn_Ws_down, L0_ffn_We_gate_up, L0_ffn_We_down)
    x = x + jnp.tanh(g_xattn[1]) * _L1_xattn_ref(_layernorm(x, axis=-1), ctx_2048, ctx_2048, mask_BxS2_if1, L1_xattn_w_q, L1_xattn_w_k, L1_xattn_w_v, L1_xattn_w_o, L1_xattn_b_o)
    x = x + jnp.tanh(g_ffn[1]) * _L1_ffn_ref(_layernorm(x, axis=-1), L1_ffn_router, L1_ffn_w_up_gate, L1_ffn_w_down, L1_ffn_shared_w_up_gate, L1_ffn_shared_w_down)
    return x

_drawn_inputs = setup_inputs


def setup_inputs(seed=0):
    import zlib

    import numpy as np

    out = dict(_drawn_inputs(seed))
    spreads = {'g_ffn': (-1.0, 0.6), 'L1_xattn_b_o': (0.0, 0.8)}
    factors = {'L0_ffn_W_router': 8.0,
     'L0_ffn_W_sgate': 8.0,
     'L0_ffn_Ws_gate_up': 8.0,
     'L0_ffn_Ws_down': 8.0,
     'L0_ffn_We_gate_up': 8.0,
     'L0_ffn_We_down': 8.0,
     'L1_xattn_w_q': 8.0,
     'L1_xattn_w_k': 8.0,
     'L1_xattn_w_v': 8.0,
     'L1_xattn_w_o': 8.0,
     'L1_ffn_router': 8.0,
     'L1_ffn_w_up_gate': 8.0,
     'L1_ffn_w_down': 8.0,
     'L1_ffn_shared_w_up_gate': 8.0,
     'L1_ffn_shared_w_down': 8.0}
    for name, (base, spread) in spreads.items():
        noise = np.random.default_rng([zlib.crc32(name.encode()), seed]).standard_normal(out[name].shape)
        drawn = base * np.exp(spread * noise) if base else spread * noise
        out[name] = jnp.asarray(drawn.astype(out[name].dtype))
    for name, factor in factors.items():
        out[name] = (out[name] * factor).astype(out[name].dtype)
    return out
```

```python
from contextlib import ExitStack

import concourse.bass as bass
from concourse import mybir

F32 = mybir.dt.float32
F32R = mybir.dt.float32r
BF16 = mybir.dt.bfloat16
ALU = mybir.AluOpType
ACT = mybir.ActivationFunctionType
AX = mybir.AxisListType.X

P = 128
B = 16
D = 256
DT = D // P
E = 8
UNIT = 176
SHARED = 4
UNITS = SHARED + E
GU = 2 * UNIT
HID = UNITS * UNIT
KT = (HID + P - 1) // P
WCOLS = DT * UNITS * GU + KT * D
WCHUNK = WCOLS // 25
CAPACITY = 640
HC = 16
DC = 8
G, HG, HD = 8, 4, 8
SLOT = 32
EPS = 1e-5
NEG = -1.0e30


def steps(eng, body, first, end, peel=2):
    for s in range(first, first + peel):
        body(s, s % 2)
    pairs = (end - first - peel) // 2 * 2
    if pairs:
        with eng.Fori(0, pairs // 2) as pair:
            for j in range(2):
                body(pair * 2 + (first + peel + j), (first + peel + j) % 2)
    for s in range(first + peel + pairs, end):
        body(s, s % 2)


def late(step, n):
    return not isinstance(step, int) or step >= n


class Kernel:

    def __init__(self, nc, ctx, io):
        self.nc, self.io = nc, io
        self.sb_in(ctx)

    def sb(self, ctx, name, shape, dt=F32):
        return ctx.enter_context(self.nc.sbuf_tensor(name, shape, dt))

    def ps(self, ctx, name, shape, dt=F32):
        return ctx.enter_context(self.nc.psum_tensor(name, shape, dt))

    def sem(self, ctx, name):
        return ctx.enter_context(self.nc.semaphore(name))

    def after(self, eng, sem, value):
        eng.wait_ge(self.begun, 1)
        eng.wait_ge(sem, value)

    def sb_in(self, ctx):
        self.x = self.sb(ctx, "x_res", [P, B, D])
        self.ctxT = self.sb(ctx, "ctxT", [P, DT, B, P])
        self.actT = self.sb(ctx, "actT", [P, DT, B, P])
        self.w_hi = self.sb(ctx, "w_hi", [P, WCOLS], F32R)
        self.w_lo = self.sb(ctx, "w_lo", [P, WCOLS], F32R)
        self.ident = self.sb(ctx, "ident", [P, P])
        self.gates = self.sb(ctx, "gates", [P, 4])
        self.stats = self.sb(ctx, "stats", [P, B, 6])
        self.mean = self.sb(ctx, "mean", [P, B])
        self.rstd = self.sb(ctx, "rstd", [P, B])
        self.w_unit = self.sb(ctx, "w_unit", [P, B, UNITS])
        self.begun = self.sem(ctx, "begun")
        self.w_router = self.sb(ctx, "w_router", [P, 2, DT, E + 1])


def split_weights(k, layer, ctx):
    nc = k.nc
    raw = k.sb(ctx, f"raw{layer}", [P, 2, WCHUNK])
    raw_in = [k.sem(ctx, f"raw_in{layer}_{j}") for j in range(2)]
    hi_done, lo_done = k.sem(ctx, f"hi_done{layer}"), k.sem(ctx, f"lo_done{layer}")
    src = k.io[f"w{layer}"]
    n = WCOLS // WCHUNK

    def emit(pool):
        def load(c):
            pool.dma_start(raw[:, c % 2], src[:, c * WCHUNK:(c + 1) * WCHUNK]).then_inc(raw_in[c % 2], 16)
        load(0)
        load(1)
        for c in range(n):
            cols = slice(c * WCHUNK, (c + 1) * WCHUNK)
            pool.wait_ge(raw_in[c % 2], 16 * (c // 2 + 1))
            nc.gpsimd.tensor_copy(k.w_hi[:, cols], raw[:, c % 2]).then_inc(hi_done, 1)
            pool.wait_ge(hi_done, c + 1)
            nc.gpsimd.tensor_tensor(k.w_lo[:, cols], raw[:, c % 2], k.w_hi[:, cols].bitcast(F32),
                                    ALU.subtract).then_inc(lo_done, 1)
            if c + 2 < n:
                pool.wait_ge(lo_done, c + 1)
                load(c + 2)
    return emit


def phase_setup(k):
    nc, io = k.nc, k.io
    with ExitStack() as ctx:
        x_in, small_in, made = (k.sem(ctx, n) for n in ("x_in", "small_in", "made"))
        stat_done, tanh_done = k.sem(ctx, "stat_done0"), k.sem(ctx, "tanh_done")
        raw_gates = k.sb(ctx, "raw_gates", [P, 4])
        with nc.Block() as block:
            @block.sync
            def _(sp):
                sp.dma_start(k.x[:], io["x"].rearrange("b t d -> t b d")).then_inc(x_in, 16)
                sp.dma_start(raw_gates[:, 0:4], bass.AP(io["gates"].tensor, 0, [[0, P], [1, 4]])).then_inc(small_in, 16)
                sp.dma_start(k.w_router[:], io["routers"]).then_inc(small_in, 16)
                sp.wait_ge(small_in, 32)

            @block.gpsimd
            def _(pool):
                nc.gpsimd.memset(k.ident[:], 0.0).then_inc(made, 1)
                pool.wait_ge(made, 1)
                nc.gpsimd.affine_select(out=k.ident[:], in_=k.ident[:], compare_op=ALU.not_equal, fill=1.0,
                                        base=0, pattern=[[-1, P]], channel_multiplier=1).then_inc(k.begun, 1)

            @block.scalar
            def _(act):
                act.wait_ge(small_in, 32)
                nc.scalar.activation(k.gates[:], raw_gates[:], ACT.Tanh).then_inc(tanh_done, 1)

            @block.vector
            def _(dve):
                dve.wait_ge(x_in, 16)
                with dve.Fori(0, B) as b:
                    nc.vector.bn_stats(k.stats[:, b], k.x[:, b]).then_inc(stat_done, 1)


def norm_coefficients(k, ctx, tag):
    nc = k.nc
    coef = k.sem(ctx, f"coef{tag}")
    dist = k.sb(ctx, f"dist{tag}", [P, B])
    var = k.sb(ctx, f"var{tag}", [P, B])
    expo = k.sb(ctx, f"expo{tag}", [P, B])

    def emit(pool):
        done = [0]

        def link(ins):
            done[0] += 1
            ins.then_inc(coef, 1)
            pool.wait_ge(coef, done[0])
        link(nc.gpsimd.memset(expo[:], -0.5))
        link(nc.gpsimd.tensor_tensor(k.mean[:], k.stats[:, :, 1], k.stats[:, :, 4], ALU.add))
        link(nc.gpsimd.tensor_scalar(k.mean[:], k.mean[:], 0.5, 0.0, ALU.mult, ALU.add))
        link(nc.gpsimd.tensor_tensor(dist[:], k.mean[:], k.stats[:, :, 1], ALU.subtract))
        link(nc.gpsimd.tensor_tensor(dist[:], dist[:], dist[:], ALU.mult))
        link(nc.gpsimd.tensor_tensor(var[:], k.stats[:, :, 2], k.stats[:, :, 5], ALU.add))
        link(nc.gpsimd.tensor_scalar(var[:], var[:], 1.0 / D, EPS, ALU.mult, ALU.add))
        link(nc.gpsimd.tensor_tensor(var[:], var[:], dist[:], ALU.add))
        link(nc.gpsimd.tensor_tensor(k.rstd[:], var[:], expo[:], ALU.pow))
    return emit, coef


def phase_turn(k):
    nc, io = k.nc, k.io
    with ExitStack() as ctx:
        xn = k.sb(ctx, "xn_a", [P, 2, D])
        cx = k.sb(ctx, "cx_a", [P, 2, D])
        turned = k.ps(ctx, "turned_a", [P, 2, 2 * DT, P])
        pool_coef, coef = norm_coefficients(k, ctx, "a")
        cx_in = [k.sem(ctx, f"cx_in{j}") for j in range(2)]
        normed, turned_full, copied = (k.sem(ctx, n) for n in ("normed_a", "turned_full_a", "copied_a"))
        pool_weights = split_weights(k, 0, ctx)
        with nc.Block() as block:
            @block.gpsimd
            def _(pool):
                pool_coef(pool)
                pool_weights(pool)

            @block.sync
            def _(sp):
                def body(b, j):
                    if late(b, 2):
                        sp.wait_ge(turned_full, b - 1)
                    sp.dma_start(cx[:, j], io["ctx"][b]).then_inc(cx_in[j], 16)
                steps(sp, body, 0, B)

            @block.vector
            def _(dve):
                dve.wait_ge(coef, 9)

                def body(b, j):
                    if late(b, 2):
                        dve.wait_ge(turned_full, b - 1)
                    nc.vector.tensor_scalar(xn[:, j], k.x[:, b], k.mean[:, bass.ds(b, 1)], k.rstd[:, bass.ds(b, 1)],
                                            ALU.subtract, ALU.mult).then_inc(normed, 1)
                steps(dve, body, 0, B)

            @block.tensor
            def _(pe):
                def body(b, j):
                    pe.wait_ge(normed, b + 1)
                    pe.wait_ge(cx_in[j], 8 * (b - j) + 16)
                    if late(b, 2):
                        pe.wait_ge(copied, 2 * b - 2)
                    for t in range(DT):
                        pe.transpose(turned[:, j, t], xn[:, j, t * P:(t + 1) * P], k.ident[:])
                    for t in range(DT):
                        mm = pe.transpose(turned[:, j, DT + t], cx[:, j, t * P:(t + 1) * P], k.ident[:])
                    mm.then_inc(turned_full, 1)
                steps(pe, body, 0, B)

            @block.scalar
            def _(act):
                def body(b, j):
                    act.wait_ge(turned_full, b + 1)
                    nc.scalar.copy(k.actT[:, :, b], turned[:, j, 0:DT]).then_inc(copied, 1)
                    nc.scalar.copy(k.ctxT[:, :, b], turned[:, j, DT:2 * DT]).then_inc(copied, 1)
                steps(act, body, 0, B)


def phase_conv(k):
    nc, io = k.nc, k.io
    NB2 = B // 2
    W = B * DC * DC
    with ExitStack() as ctx:
        kv = k.sb(ctx, "kv", [P, 2, DT, W])
        toep = k.sb(ctx, "toep", [P, 2, D])
        skip = k.sb(ctx, "skip", [P, HC])
        prod = k.sb(ctx, "prod", [P, 2, W])
        conv = k.ps(ctx, "conv", [P, 4, W])
        toep_in = [k.sem(ctx, f"toep_in{j}") for j in range(2)]
        skip_in, toep_full, kv_full, conv_full = (k.sem(ctx, n) for n in ("skip_in", "toep_full", "kv_full", "conv_full"))
        prod_done, summed = k.sem(ctx, "prod_done"), k.sem(ctx, "summed")

        def head(buf, t, h):
            return buf[:, t, :, bass.ds(h * DC, DC)]

        with nc.Block() as block:
            @block.sync
            def _(sp):
                sp.dma_start(skip[:], bass.AP(io["skip"].tensor, 0, [[0, P], [1, HC]])).then_inc(skip_in, 16)

                def body(h, j):
                    if late(h, 2):
                        sp.wait_ge(conv_full, 2 * h - 2)
                    sp.dma_start(toep[:, j], io["taps"][h]).then_inc(toep_in[j], 16)
                steps(sp, body, 0, HC)

            @block.gpsimd
            def _(pool):
                def body(h, j):
                    if late(h, 2):
                        pool.wait_ge(conv_full, 2 * h - 2)
                    for t in range(DT):
                        c = head(k.ctxT, t, h)
                        nc.gpsimd.tensor_tensor(
                            kv[:, j, t].rearrange("p (b j i) -> p b j i", j=DC, i=DC),
                            c.unsqueeze(3).broadcast_to([P, B, DC, DC]),
                            c.unsqueeze(2).broadcast_to([P, B, DC, DC]), ALU.mult).then_inc(kv_full, 1)
                steps(pool, body, 0, HC)

            @block.tensor
            def _(pe):
                def body(h, j):
                    pe.wait_ge(toep_full, h + 1)
                    pe.wait_ge(kv_full, 2 * h + 2)
                    for t in range(DT):
                        bank = 2 * j + t
                        if late(h, 2):
                            pe.wait_ge(prod_done, 2 * h - 3 + t)
                        for half in range(2):
                            cols = slice(half * (W // 2), (half + 1) * (W // 2))
                            for s in range(t + 1):
                                mm = pe.matmul(conv[:, bank, cols], toep[:, j, (t - s) * P:(t - s + 1) * P],
                                               kv[:, j, s, cols], start=(s == 0), stop=(s == t))
                        mm.then_inc(conv_full, 1)
                steps(pe, body, 0, HC)

            @block.vector
            def _(dve):
                dve.wait_ge(skip_in, 16)

                def body(h, j):
                    dve.wait_ge(toep_in[j], 8 * (h - j) + 16)
                    nc.vector.scalar_tensor_tensor(toep[:, j, 0:P], k.ident[:], skip[:, bass.ds(h, 1)],
                                                   toep[:, j, 0:P], ALU.mult, ALU.add).then_inc(toep_full, 1)
                    for t in range(DT):
                        dve.wait_ge(conv_full, 2 * h + t + 1)
                        if late(h, 1):
                            dve.wait_ge(summed, 2 * h - 1 + t)
                        q = head(k.actT, t, h)
                        nc.vector.tensor_tensor(
                            prod[:, t].rearrange("p (b j i) -> p b j i", j=DC, i=DC),
                            conv[:, 2 * j + t].rearrange("p (b j i) -> p b j i", j=DC, i=DC),
                            q.unsqueeze(2).broadcast_to([P, B, DC, DC]), ALU.mult).then_inc(prod_done, 1)
                        k.after(dve, prod_done, 2 * h + t + 1)
                        nc.vector.tensor_reduce(q, prod[:, t].rearrange("p (b j i) -> p b j i", j=DC, i=DC),
                                                AX, ALU.add).then_inc(summed, 1)
                steps(dve, body, 0, HC)


def phase_residual(k):
    nc = k.nc
    with ExitStack() as ctx:
        stage = k.sb(ctx, "stage_c", [P, 2, DT, P])
        back = k.ps(ctx, "back_c", [P, 2, 512])
        staged, turned, added = (k.sem(ctx, n) for n in ("staged_c", "turned_c", "added_c"))
        with nc.Block() as block:
            @block.scalar
            def _(act):
                def body(b, j):
                    if late(b, 2):
                        act.wait_ge(turned, b - 1)
                    nc.scalar.copy(stage[:, j], k.actT[:, :, b]).then_inc(staged, 1)
                steps(act, body, 0, B)

            @block.tensor
            def _(pe):
                def body(b, j):
                    pe.wait_ge(staged, b + 1)
                    if late(b, 2):
                        pe.wait_ge(added, b - 1)
                    for t in range(DT):
                        mm = pe.transpose(back[:, j, t * P:(t + 1) * P], stage[:, j, t], k.ident[:])
                    mm.then_inc(turned, 1)
                steps(pe, body, 0, B)

            @block.vector
            def _(dve):
                def body(b, j):
                    dve.wait_ge(turned, b + 1)
                    nc.vector.scalar_tensor_tensor(k.x[:, b], back[:, j, 0:D], k.gates[:, 0:1], k.x[:, b],
                                                   ALU.mult, ALU.add).then_inc(added, 1)
                    k.after(dve, added, b + 1)
                    nc.vector.bn_stats(k.stats[:, b], k.x[:, b])
                steps(dve, body, 0, B)


def phase_route(k, layer):
    nc = k.nc
    cols = E + 1 if layer == 0 else E
    with ExitStack() as ctx:
        xn = k.sb(ctx, f"xn_r{layer}", [P, 2, D])
        logT = k.sb(ctx, f"logT{layer}", [E + 1, B * P])
        lg = k.sb(ctx, f"lg{layer}", [P, B, E + 1])
        rev = k.sb(ctx, f"rev{layer}", [P, B, E])
        tmp = {n: k.sb(ctx, f"{n}{layer}", [P, B, E]) for n in ("eq", "rank", "one1", "one2", "lg2", "ex", "sel", "valid")}
        row = {n: k.sb(ctx, f"{n}_row{layer}", [P, B]) for n in ("m1", "m2", "r1", "r2", "gap", "e2", "den", "inv")}
        gate9 = k.sb(ctx, f"gate9{layer}", [P, B])
        sel_pad = k.sb(ctx, f"sel_pad{layer}", [P, 2 * B, E], BF16)
        sel16 = sel_pad[:, B:]
        ones16 = k.sb(ctx, f"ones16{layer}", [P, P], BF16)
        tri16 = k.sb(ctx, f"tri16{layer}", [P, P], BF16)
        turned = k.ps(ctx, f"turned_r{layer}", [P, 2, 512])
        logP = k.ps(ctx, f"logP{layer}", [P, 2, 512])
        lgP = k.ps(ctx, f"lgP{layer}", [P, B * (E + 1)])
        posP = k.ps(ctx, f"posP{layer}", [P, B, E])
        pool_coef, coef = norm_coefficients(k, ctx, f"r{layer}")
        normed, turned_full, copied = (k.sem(ctx, f"{n}_r{layer}") for n in ("normed", "turned_full", "copied"))
        logits_full, logits_out, back_full, chain = (k.sem(ctx, f"{n}_r{layer}") for n in
                                                     ("logits_full", "logits_out", "back_full", "chain"))
        consts, ex_in, ex_out, pos_in, pos_out = (k.sem(ctx, f"{n}_r{layer}") for n in
                                                  ("consts", "ex_in", "ex_out", "pos_in", "pos_out"))
        with nc.Block() as block:
            @block.gpsimd
            def _(pool):
                pool_coef(pool)
                for e in range(E):
                    nc.gpsimd.memset(rev[:, :, e], float(E - e)).then_inc(consts, 1)
                nc.gpsimd.memset(ones16[:], 1.0).then_inc(consts, 1)
                pool.wait_ge(consts, E + 1)
                nc.gpsimd.affine_select(out=tri16[:], in_=ones16[:], compare_op=ALU.is_gt, fill=0.0,
                                        base=0, pattern=[[1, P]], channel_multiplier=-1).then_inc(consts, 1)

            @block.vector
            def _(dve):
                dve.wait_ge(coef, 9)

                def body(b, j):
                    if late(b, 2):
                        dve.wait_ge(turned_full, b - 1)
                    nc.vector.tensor_scalar(xn[:, j], k.x[:, b], k.mean[:, bass.ds(b, 1)], k.rstd[:, bass.ds(b, 1)],
                                            ALU.subtract, ALU.mult).then_inc(normed, 1)
                steps(dve, body, 0, B)
                count = [0]

                def link(ins):
                    count[0] += 1
                    ins.then_inc(chain, 1)
                    dve.wait_ge(chain, count[0])

                def bc(r):
                    return r[:].unsqueeze(2).broadcast_to([P, B, E])

                def best(logits, m, r, one):
                    link(nc.vector.tensor_reduce(row[m][:], logits, AX, ALU.max))
                    link(nc.vector.tensor_tensor(tmp["eq"][:], logits, bc(row[m]), ALU.is_equal))
                    link(nc.vector.tensor_tensor(tmp["rank"][:], tmp["eq"][:], rev[:], ALU.mult))
                    link(nc.vector.tensor_reduce(row[r][:], tmp["rank"][:], AX, ALU.max))
                    link(nc.vector.tensor_tensor(tmp[one][:], tmp["rank"][:], bc(row[r]), ALU.is_equal))

                dve.wait_ge(back_full, 1)
                dve.wait_ge(consts, E + 2)
                link(nc.vector.tensor_copy(lg[:, :, 0:cols], lgP[:, 0:B * cols].rearrange("p (b e) -> p b e", e=cols)))
                logits = lg[:, :, 0:E]
                best(logits, "m1", "r1", "one1")
                link(nc.vector.scalar_tensor_tensor(tmp["lg2"][:], tmp["one1"][:], NEG, logits, ALU.mult, ALU.add))
                best(tmp["lg2"][:], "m2", "r2", "one2")
                if layer == 0:
                    link(nc.vector.tensor_tensor(tmp["ex"][:], logits, bc(row["m1"]), ALU.subtract))
                    nc.vector.tensor_copy(gate9[:], lg[:, :, E]).then_inc(ex_in, 1)
                    dve.wait_ge(ex_out, 2)
                    link(nc.vector.tensor_reduce(row["den"][:], tmp["ex"][:], AX, ALU.add))
                    link(nc.vector.reciprocal(row["inv"][:], row["den"][:]))
                    link(nc.vector.tensor_tensor(tmp["sel"][:], tmp["one1"][:], tmp["one2"][:], ALU.add))
                    link(nc.vector.tensor_tensor(tmp["ex"][:], tmp["ex"][:], tmp["sel"][:], ALU.mult))
                    link(nc.vector.tensor_tensor(k.w_unit[:, :, SHARED:], tmp["ex"][:], bc(row["inv"]), ALU.mult))
                    link(nc.vector.tensor_scalar(gate9[:], gate9[:], 1.0, None, ALU.add))
                    link(nc.vector.reciprocal(row["gap"][:], gate9[:]))
                    link(nc.vector.tensor_copy(k.w_unit[:, :, 0:SHARED],
                                               row["gap"][:].unsqueeze(2).broadcast_to([P, B, SHARED])))
                else:
                    link(nc.vector.tensor_tensor(sel16, tmp["one1"][:], tmp["one2"][:], ALU.add))
                    nc.vector.memset(sel_pad[:, 0:B], 0.0).then_inc(pos_in, 1)
                    nc.vector.tensor_tensor(row["gap"][:], row["m2"][:], row["m1"][:], ALU.subtract).then_inc(ex_in, 1)
                    dve.wait_ge(ex_out, 1)
                    link(nc.vector.tensor_scalar(row["den"][:], row["e2"][:], 1.0, None, ALU.add))
                    link(nc.vector.reciprocal(row["inv"][:], row["den"][:]))
                    link(nc.vector.tensor_tensor(tmp["ex"][:], tmp["one2"][:], bc(row["e2"]), ALU.mult))
                    link(nc.vector.tensor_tensor(tmp["ex"][:], tmp["ex"][:], tmp["one1"][:], ALU.add))
                    link(nc.vector.tensor_tensor(tmp["ex"][:], tmp["ex"][:], bc(row["inv"]), ALU.mult))
                    dve.wait_ge(pos_out, 1)
                    link(nc.vector.tensor_scalar(tmp["valid"][:], posP[:], float(CAPACITY), None, ALU.is_lt))
                    link(nc.vector.tensor_tensor(k.w_unit[:, :, SHARED:], tmp["ex"][:], tmp["valid"][:], ALU.mult))
                    link(nc.vector.memset(k.w_unit[:, :, 0:SHARED], 1.0))

            @block.scalar
            def _(act):
                def body(b, j):
                    act.wait_ge(turned_full, b + 1)
                    nc.scalar.copy(k.actT[:, :, b], turned[:, j, 0:D].rearrange("p (t n) -> p t n", t=DT)).then_inc(copied, 1)
                steps(act, body, 0, B)
                for c in range(4):
                    act.wait_ge(logits_full, c + 1)
                    nc.scalar.copy(logT[0:cols, c * 512:(c + 1) * 512], logP[0:cols, c % 2]).then_inc(logits_out, 1)
                act.wait_ge(ex_in, 1)
                if layer == 0:
                    act.wait_ge(chain, 13)
                    nc.scalar.activation(tmp["ex"][:], tmp["ex"][:], ACT.Exp).then_inc(ex_out, 1)
                    nc.scalar.activation(gate9[:], gate9[:], ACT.Exp, scale=-1.0).then_inc(ex_out, 1)
                else:
                    nc.scalar.activation(row["e2"][:], row["gap"][:], ACT.Exp).then_inc(ex_out, 1)

            @block.tensor
            def _(pe):
                def body(b, j):
                    pe.wait_ge(normed, b + 1)
                    if late(b, 2):
                        pe.wait_ge(copied, b - 1)
                    for t in range(DT):
                        mm = pe.transpose(turned[:, j, t * P:(t + 1) * P], xn[:, j, t * P:(t + 1) * P], k.ident[:])
                    mm.then_inc(turned_full, 1)
                steps(pe, body, 0, B)
                pe.wait_ge(copied, B)
                for c in range(4):
                    if c >= 2:
                        pe.wait_ge(logits_out, c - 1)
                    for t in range(DT):
                        mm = pe.matmul(logP[0:cols, c % 2], k.w_router[:, layer, t, 0:cols],
                                       k.actT[:, t, 4 * c:4 * c + 4], start=(t == 0), stop=(t == DT - 1))
                    mm.then_inc(logits_full, 1)
                pe.wait_ge(logits_out, 4)
                for b in range(B):
                    mm = pe.transpose(lgP[:, b * cols:(b + 1) * cols], logT[0:cols, b * P:(b + 1) * P],
                                      k.ident[0:cols, 0:cols])
                mm.then_inc(back_full, 1)
                if layer == 1:
                    pe.wait_ge(pos_in, 1)
                    pe.wait_ge(consts, E + 2)
                    for back in range(1, B):
                        pe.matmul(posP[:], ones16[:], sel_pad[:, B - back:2 * B - back], start=(back == 1), stop=False)
                    mm = pe.matmul(posP[:], tri16[:], sel16, start=False, stop=True)
                    mm.then_inc(pos_out, 1)


def phase_experts(k, layer):
    nc, io = k.nc, k.io
    GW = DT * UNITS * GU
    RING = 4
    NG = (KT + 3) // 4
    with ExitStack() as ctx:
        t_ = f"_e{layer}"
        xs_hi = k.sb(ctx, "xs_hi" + t_, [P, 2, DT, P], F32R)
        xs_lo = k.sb(ctx, "xs_lo" + t_, [P, 2, DT, P], F32R)
        silu = k.sb(ctx, "silu" + t_, [P, RING, UNIT])
        h = k.sb(ctx, "h" + t_, [P, 2, HID])
        hT_hi = k.sb(ctx, "hT_hi" + t_, [P, 2, 4, P], F32R)
        hT_lo = k.sb(ctx, "hT_lo" + t_, [P, 2, 4, P], F32R)
        gu = k.ps(ctx, "gu" + t_, [P, RING, 512])
        turned = k.ps(ctx, "turned" + t_, [P, 2, 512])
        out = k.ps(ctx, "out" + t_, [P, 2, 512])
        (xs_hi_done, xs_done, gu_full, silu_done, h_done, turned_full, hi_done, hT_done, down_full,
         added, stored) = (k.sem(ctx, n + t_) for n in (
             "xs_hi_done", "xs_done", "gu_full", "silu_done", "h_done", "turned_full", "hi_done",
             "hT_done", "down_full", "added", "stored"))
        gate = k.gates[:, 2 * layer + 1:2 * layer + 2]

        def tiles(g):
            return [(c, min(P, HID - c * P)) for c in range(4 * g, min(4 * g + 4, KT))]

        def plan(s, front, turn, down):
            for u in range(UNITS):
                if front:
                    front(u)
                if turn and u % 2 == 0 and u // 2 < NG:
                    turn(u // 2)
                if down and u % 2 == 0 and 1 <= u // 2 <= NG:
                    down(u // 2 - 1)

        def run(eng, body):
            body(0, 0, True, False)
            body(1, 1, True, True)
            with eng.Fori(0, B // 2 - 1) as pair:
                for j in range(2):
                    body(pair * 2 + (2 + j), j, True, True)
            body(B, 0, False, True)

        with nc.Block() as block:
            @block.tensor
            def _(pe):
                def body(s, j, has_front, has_down):
                    i = 1 - j

                    def front(u):
                        if u == 0:
                            pe.wait_ge(xs_done, s + 1)
                        if late(s, 1) or u >= RING:
                            pe.wait_ge(h_done, s * UNITS + u - RING + 1)
                        for t in range(DT):
                            w0 = t * UNITS * GU + u * GU
                            for n, (a, w) in enumerate(((xs_hi, k.w_hi), (xs_hi, k.w_lo), (xs_lo, k.w_hi))):
                                mm = pe.matmul(gu[:, u % RING, 0:GU], a[:, j, t], w[:, w0:w0 + GU],
                                               start=(t == 0 and n == 0), stop=(t == DT - 1 and n == 2))
                        mm.then_inc(gu_full, 1)

                    def turn(g):
                        if g == 0:
                            pe.wait_ge(h_done, s * UNITS)
                        half = (g + i * NG) % 2
                        if late(s, 2) or g >= 2:
                            k.after(pe, hT_done, (s - 1) * NG + g - 1)
                        for c, rows in tiles(g):
                            mm = pe.transpose(turned[0:rows, half, (c % 4) * P:(c % 4 + 1) * P],
                                              h[:, i, c * P:c * P + rows], k.ident[:])
                        mm.then_inc(turned_full, 1)

                    def down(g):
                        if g == 0 and late(s, 3):
                            pe.wait_ge(added, s - 2)
                        pe.wait_ge(hT_done, (s - 1) * NG + g + 1)
                        half = (g + i * NG) % 2
                        for c, rows in tiles(g):
                            for n, (a, w) in enumerate(((hT_hi, k.w_hi), (hT_hi, k.w_lo), (hT_lo, k.w_hi))):
                                mm = pe.matmul(out[:, i, 0:D], a[0:rows, half, c % 4], w[0:rows, GW + c * D:GW + (c + 1) * D],
                                               start=(c == 0 and n == 0), stop=(c == KT - 1 and n == 2))
                        mm.then_inc(down_full, 1)
                    plan(s, has_front and front, has_down and turn, has_down and down)
                run(pe, body)

            @block.scalar
            def _(act):
                def body(s, j, has_front, has_down):
                    i = 1 - j
                    if has_front:
                        if late(s, 2):
                            act.wait_ge(gu_full, (s - 1) * UNITS)
                        nc.scalar.copy(xs_hi[:, j], k.actT[:, :, s]).then_inc(xs_hi_done, 1)

                    def front(u):
                        act.wait_ge(gu_full, s * UNITS + u + 1)
                        if late(s, 1) or u >= RING:
                            act.wait_ge(h_done, s * UNITS + u - RING + 1)
                        nc.scalar.activation(silu[:, u % RING], gu[:, u % RING, 0:UNIT], ACT.Silu).then_inc(silu_done, 1)

                    def turn(g):
                        half = (g + i * NG) % 2
                        act.wait_ge(turned_full, (s - 1) * NG + g + 1)
                        if late(s, 2) or g >= 2:
                            act.wait_ge(down_full, (s - 1) * NG + g - 1)
                        n, rows = len(tiles(g)), tiles(g)[0][1]
                        nc.scalar.copy(hT_hi[0:rows, half, 0:n],
                                       turned[0:rows, half, 0:n * P].rearrange("p (c n) -> p c n", n=P)).then_inc(hi_done, 1)
                    plan(s, has_front and front, has_down and turn, None)
                run(act, body)

            @block.vector
            def _(dve):
                def body(s, j, has_front, has_down):
                    i = 1 - j
                    if has_front:
                        dve.wait_ge(xs_hi_done, s + 1)
                        if late(s, 2):
                            dve.wait_ge(gu_full, (s - 1) * UNITS)
                        nc.vector.tensor_tensor(xs_lo[:, j], k.actT[:, :, s], xs_hi[:, j].bitcast(F32),
                                                ALU.subtract).then_inc(xs_done, 1)

                    def front(u):
                        dve.wait_ge(silu_done, s * UNITS + u + 1)
                        if u == 0 and late(s, 2):
                            dve.wait_ge(turned_full, (s - 1) * NG)
                        nc.vector.scalar_tensor_tensor(
                            h[:, j, u * UNIT:(u + 1) * UNIT], gu[:, u % RING, UNIT:GU],
                            k.w_unit[:, s, u:u + 1], silu[:, u % RING], ALU.mult, ALU.mult).then_inc(h_done, 1)

                    def turn(g):
                        half = (g + i * NG) % 2
                        dve.wait_ge(hi_done, (s - 1) * NG + g + 1)
                        if late(s, 2) or g >= 2:
                            dve.wait_ge(down_full, (s - 1) * NG + g - 1)
                        n, rows = len(tiles(g)), tiles(g)[0][1]
                        nc.vector.tensor_tensor(hT_lo[0:rows, half, 0:n],
                                                turned[0:rows, half, 0:n * P].rearrange("p (c n) -> p c n", n=P),
                                                hT_hi[0:rows, half, 0:n].bitcast(F32), ALU.subtract).then_inc(hT_done, 1)
                    plan(s, has_front and front, has_down and turn, None)
                    if has_down:
                        dve.wait_ge(down_full, s * NG)
                        nc.vector.scalar_tensor_tensor(k.x[:, s - 1], out[:, i, 0:D], gate, k.x[:, s - 1],
                                                       ALU.mult, ALU.add).then_inc(added, 1)
                        if layer == 0:
                            k.after(dve, added, s)
                            nc.vector.bn_stats(k.stats[:, s - 1], k.x[:, s - 1])
                run(dve, body)

            if layer == 1:
                @block.sync
                def _(sp):
                    with sp.Fori(0, B) as b:
                        sp.wait_ge(added, b + 1)
                        sp.dma_start(io["out"][b], k.x[:, b]).then_inc(stored, 16)
                    sp.wait_ge(stored, 16 * B)

def phase_turn_rows(k):
    nc = k.nc
    with ExitStack() as ctx:
        xn = k.sb(ctx, "xn_q", [P, 2, D])
        turned = k.ps(ctx, "turned_q", [P, 2, 512])
        pool_coef, coef = norm_coefficients(k, ctx, "q")
        normed, turned_full, copied = (k.sem(ctx, n) for n in ("normed_q", "turned_full_q", "copied_q"))
        with nc.Block() as block:
            @block.gpsimd
            def _(pool):
                pool_coef(pool)

            @block.vector
            def _(dve):
                dve.wait_ge(coef, 9)

                def body(b, j):
                    if late(b, 2):
                        dve.wait_ge(turned_full, b - 1)
                    nc.vector.tensor_scalar(xn[:, j], k.x[:, b], k.mean[:, bass.ds(b, 1)], k.rstd[:, bass.ds(b, 1)],
                                            ALU.subtract, ALU.mult).then_inc(normed, 1)
                steps(dve, body, 0, B)

            @block.tensor
            def _(pe):
                def body(b, j):
                    pe.wait_ge(normed, b + 1)
                    if late(b, 2):
                        pe.wait_ge(copied, b - 1)
                    for t in range(DT):
                        mm = pe.transpose(turned[:, j, t * P:(t + 1) * P], xn[:, j, t * P:(t + 1) * P], k.ident[:])
                    mm.then_inc(turned_full, 1)
                steps(pe, body, 0, B)

            @block.scalar
            def _(act):
                def body(b, j):
                    act.wait_ge(turned_full, b + 1)
                    nc.scalar.copy(k.actT[:, :, b], turned[:, j, 0:D].rearrange("p (t n) -> p t n", t=DT)).then_inc(copied, 1)
                steps(act, body, 0, B)


def phase_attention(k):
    nc, io = k.nc, k.io
    T = G // 4
    SCALE = float(HD) ** -0.5
    with ExitStack() as ctx:
        wq = k.sb(ctx, "wq", [P, DT, T, HG, P])
        wk = k.sb(ctx, "wk", [P, DT, T, P])
        wv = k.sb(ctx, "wv", [P, DT, G * HD])
        wo = k.sb(ctx, "wo", [P, DT, D])
        bo = k.sb(ctx, "bo", [P, D])
        csel_in = k.sb(ctx, "csel_in", [2, 2, P])
        csel = k.sb(ctx, "csel", [2, 2, P], BF16)
        cfix = k.sb(ctx, "cfix", [2, 2])
        lomask = k.sb(ctx, "lomask", [P, 2])
        consts = k.sb(ctx, "consts", [2, B * P], BF16)
        ident16 = k.sb(ctx, "ident16", [P, P], BF16)
        causal = k.sb(ctx, "causal", [P, 2, HG, P], BF16)
        cst = k.sb(ctx, "cst", [P, 2, DT, P])
        k_hi = k.sb(ctx, "k_hi", [P, T, P], F32R)
        q_hi = k.sb(ctx, "q_hi", [P, HG, P], F32R)
        k_st = k.sb(ctx, "k_st", [P, 2, T, P], F32R)
        q_st = k.sb(ctx, "q_st", [P, 2, T, HG, P], F32R)
        vaug = k.sb(ctx, "vaug", [P, 2, G, SLOT])
        mx = k.sb(ctx, "mx", [P, 2, G * HG])
        negT = k.sb(ctx, "negT", [G * HG, P], F32R)
        probs = k.sb(ctx, "probs", [P, 4, HG * P])
        oT = k.sb(ctx, "oT", [P, T, HG, P])
        rinv = k.sb(ctx, "rinv", [P, T, HG, 4])
        attn = k.sb(ctx, "attn", [P, G, HG, HD])
        attnT = k.sb(ctx, "attnT", [P, DT, P])
        bankA = k.ps(ctx, "bankA", [P, 512])
        bankC = k.ps(ctx, "bankC", [P, 512])
        s1 = k.ps(ctx, "s1", [P, 2, 512])
        s2 = k.ps(ctx, "s2", [P, 2, 512])
        oP = k.ps(ctx, "oP", [P, T, 512])
        names = ("loaded", "made", "c_ready", "cst_done", "kv_full", "k_hi_done", "k_done", "v_done", "q_full",
                 "q_hi_done", "q_done", "s1_full", "max_done", "maxT_full", "neg_done", "neg_in", "s2_full",
                 "exp_done", "pv_full", "oT_done", "turn_full", "rinv_done", "attn_done", "attnT_full", "attnT_done",
                 "o_full", "bias_done", "added", "cmask")
        (loaded, made, c_ready, cst_done, kv_full, k_hi_done, k_done, v_done, q_full, q_hi_done, q_done, s1_full,
         max_done, maxT_full, neg_done, neg_in, s2_full, exp_done, pv_full, oT_done, turn_full, rinv_done, attn_done,
         attnT_full, attnT_done, o_full, bias_done, added, cmask) = (k.sem(ctx, n + "_t") for n in names)
        pool_weights = split_weights(k, 1, ctx)
        LOADS = 9
        mask_in = probs[0:2].rearrange("p q n -> p (q n)").bitcast(mybir.dt.int32)

        def run(eng, body):
            for s in range(2):
                body(s, s % 2, True, s >= 1, False)
            with eng.Fori(0, B // 2 - 1) as pair:
                for j in range(2):
                    body(pair * 2 + (2 + j), j, True, True, True)
            body(B, 0, False, True, True)
            body(B + 1, 1, False, False, True)

        def rows(buf, s):
            return buf[SLOT * s:SLOT * (s + 1)]

        with nc.Block() as block:
            @block.sync
            def _(sp):
                for dst, src in ((wq, io["wq"]), (wk, io["wk"]), (wv, io["wv"]), (wo, io["wo"]), (csel_in, io["csel"]),
                                 (cfix, io["cfix"]), (lomask, io["lomask"])):
                    sp.dma_start(dst[:], src).then_inc(loaded, 16)
                sp.dma_start(bo[:], bass.AP(io["bo"].tensor, 0, [[0, P], [1, D]])).then_inc(loaded, 16)
                sp.dma_start(mask_in, bass.AP(io["mask"].tensor, 0, [[0, 2], [1, B * P]])).then_inc(loaded, 16)

                def body(s, j, front, back, tail):
                    if front:
                        sp.wait_ge(neg_done, s + 1)
                        for g in range(G):
                            sp.dma_start(q_st[SLOT * (g % 4) + 24:SLOT * (g % 4) + 25, j, g // 4].bitcast(F32),
                                         negT[HG * g:HG * (g + 1), :].bitcast(F32)).then_inc(neg_in, 16)
                run(sp, body)

            @block.gpsimd
            def _(pool):
                nc.gpsimd.memset(vaug[:], 0.0).then_inc(made, 1)
                nc.gpsimd.memset(causal[:], 0.0).then_inc(made, 1)
                pool.wait_ge(made, 2)
                nc.gpsimd.memset(vaug[:, :, :, HD:HD + 1], 1.0).then_inc(made, 1)
                nc.gpsimd.affine_select(out=causal[:, 0], in_=causal[:, 0], compare_op=ALU.is_ge, fill=NEG,
                                        base=0, pattern=[[0, HG], [-1, P]], channel_multiplier=1).then_inc(made, 1)
                nc.gpsimd.affine_select(out=causal[:, 1], in_=causal[:, 1], compare_op=ALU.is_ge, fill=NEG,
                                        base=0, pattern=[[0, HG], [1, P]], channel_multiplier=-1).then_inc(made, 1)
                nc.gpsimd.tensor_copy(ident16[:], k.ident[:]).then_inc(made, 1)
                pool_weights(pool)

            @block.tensor
            def _(pe):
                pe.wait_ge(loaded, 16 * LOADS)
                pe.wait_ge(c_ready, 2)
                pe.wait_ge(made, 6)

                def body(s, j, front, back, tail):
                    i = 1 - j
                    row = (s - 1) if back else None
                    if front:
                        if late(s, 1):
                            pe.wait_ge(neg_done, s)
                        for t in range(T):
                            for d in range(DT):
                                pe.matmul(bankC[:, t * P:(t + 1) * P], wk[:, d, t], k.ctxT[:, d, s],
                                          start=(d == 0), stop=False)
                            pe.matmul(bankC[:, t * P:(t + 1) * P], csel[:, 0], consts[:, bass.ds(s * P, P)],
                                      start=False, stop=True)
                        pe.wait_ge(cst_done, s + 1)
                        for d in range(DT):
                            mm = pe.matmul(bankC[:, T * P:T * P + G * HD], cst[:, j, d], wv[:, d],
                                           start=(d == 0), stop=(d == DT - 1))
                        mm.then_inc(kv_full, 1)
                        for t in range(T):
                            if t == 0 and late(s, 3):
                                pe.wait_ge(attnT_done, s - 2)
                            if t == 1:
                                pe.wait_ge(q_done, 2 * s + 1)
                            for h in range(HG):
                                for d in range(DT):
                                    pe.matmul(bankA[:, h * P:(h + 1) * P], wq[:, d, t, h], k.actT[:, d, s],
                                              start=(d == 0), stop=False)
                                mm = pe.matmul(bankA[:, h * P:(h + 1) * P], csel[:, 1], consts[:, bass.ds(s * P, P)],
                                               start=False, stop=True)
                            mm.then_inc(q_full, 1)
                    for g in range(G):
                        t, slot = g // 4, g % 4
                        if front:
                            if g == 0:
                                pe.wait_ge(k_done, s + 1)
                            if slot == 0:
                                pe.wait_ge(q_done, 2 * s + t + 1)
                            if late(s, 1) or g >= 2:
                                pe.wait_ge(max_done, s * G + g - 1)
                            pe.matmul(s1[:, g % 2], ident16[:], causal[:, 0], start=True, stop=False, skip_group_check=True)
                            for h in range(HG):
                                mm = pe.matmul(s1[:, g % 2, h * P:(h + 1) * P], rows(q_st, slot)[:, j, t, h],
                                               rows(k_st, slot)[:, j, t], start=False, stop=(h == HG - 1),
                                               skip_group_check=True)
                            mm.then_inc(s1_full, 1)
                        if back:
                            if g == 0:
                                pe.wait_ge(neg_in, s * G * 16)
                            if late(s, 2) or g >= 2:
                                pe.wait_ge(exp_done, (s - 1) * G + g - 1)
                            pe.matmul(s2[:, g % 2], ident16[:], causal[:, 1], start=True, stop=False, skip_group_check=True)
                            pe.matmul(s2[:, g % 2], rows(k_st, slot)[:, i, t], rows(q_st, slot)[:, i, t],
                                      start=False, stop=True, skip_group_check=True).then_inc(s2_full, 1)
                            if slot == 3:
                                pe.wait_ge(exp_done, (s - 1) * G + g + 1)
                                if t == 0 and late(s, 2):
                                    pe.wait_ge(oT_done, (s - 1) * T)
                                for q in range(4):
                                    mm = pe.matmul(oP[SLOT * q:SLOT * (q + 1), t], vaug[:, i, 4 * t + q], probs[:, q],
                                                   start=True, stop=True)
                                mm.then_inc(pv_full, 1)
                        if tail and g == 1:
                            pe.wait_ge(oT_done, (s - 1) * T)
                            if front:
                                pe.wait_ge(q_done, 2 * s + 2)
                                pe.wait_ge(v_done, s + 1)
                                pe.wait_ge(k_done, s + 1)
                            if not front:
                                pe.wait_ge(attnT_done, s - 2)
                                pe.wait_ge(added, s - 2)
                                pe.wait_ge(neg_done, B)
                            for t_ in range(T):
                                for h in range(HG):
                                    mm = pe.transpose((bankA, bankC)[t_][:, h * P:(h + 1) * P], oT[:, t_, h], k.ident[:])
                            mm.then_inc(turn_full, 1)
                        if tail and g == 3:
                            pe.wait_ge(attn_done, (s - 1) * T)
                            for d in range(DT):
                                mm = pe.transpose(bankA[:, d * P:(d + 1) * P],
                                                  attn[:].rearrange("p g h d -> p (g h d)")[:, d * P:(d + 1) * P], k.ident[:])
                            mm.then_inc(attnT_full, 1)
                        if tail and g == 5:
                            pe.wait_ge(attnT_done, s - 1)
                            for d in range(DT):
                                mm = pe.matmul(bankC[:, 0:D], attnT[:, d], wo[:, d], start=(d == 0), stop=(d == DT - 1))
                            mm.then_inc(o_full, 1)
                    if front:
                        pe.wait_ge(max_done, (s + 1) * G)
                        pe.wait_ge(v_done, s + 1)
                        if tail:
                            pe.wait_ge(added, s - 1)
                        pe.transpose(bankC[0:G * HG, 0:P], mx[:, j], k.ident[:]).then_inc(maxT_full, 1)
                run(pe, body)

            @block.scalar
            def _(act):
                def body(s, j, front, back, tail):
                    i = 1 - j
                    if front:
                        act.wait_ge(kv_full, s + 1)
                        if late(s, 1):
                            act.wait_ge(k_done, s)
                        nc.scalar.copy(k_hi[:], bankC[:, 0:T * P].rearrange("p (t n) -> p t n", t=T)).then_inc(k_hi_done, 1)
                        if late(s, 2):
                            act.wait_ge(pv_full, (s - 1) * T)
                        if isinstance(s, int) and s < 2:
                            act.wait_ge(made, 3)
                        nc.scalar.copy(vaug[:, j, :, 0:HD], bankC[:, T * P:T * P + G * HD].rearrange("p (g d) -> p g d", g=G)).then_inc(v_done, 1)
                        for t in range(T):
                            act.wait_ge(q_full, 2 * s + t + 1)
                            if late(s, 1) or t == 1:
                                act.wait_ge(q_done, 2 * s + t)
                            nc.scalar.copy(q_hi[:], bankA[:].rearrange("p (h n) -> p h n", h=HG)).then_inc(q_hi_done, 1)
                    for g in range(G):
                        if back:
                            act.wait_ge(s2_full, (s - 1) * G + g + 1)
                            if late(s, 2) or g >= 4:
                                act.wait_ge(pv_full, (s - 1) * T + g // 4 - (0 if g >= 4 else 0))
                            nc.scalar.activation(probs[:, g % 4], s2[:, g % 2], ACT.Exp, scale=SCALE).then_inc(exp_done, 1)
                        if tail and g == 4:
                            act.wait_ge(attnT_full, s - 1)
                            nc.scalar.copy(attnT[:], bankA[:, 0:D].rearrange("p (t n) -> p t n", t=DT)).then_inc(attnT_done, 1)
                    if back:
                        for t in range(T):
                            act.wait_ge(pv_full, (s - 1) * T + t + 1)
                            if t == 0 and late(s, 2):
                                act.wait_ge(turn_full, s - 1)
                            nc.scalar.copy(oT[:, t], oP[:, t].rearrange("p (h n) -> p h n", h=HG)).then_inc(oT_done, 1)
                    if front:
                        act.wait_ge(maxT_full, s + 1)
                        if late(s, 1):
                            act.wait_ge(neg_in, s * G * 16)
                        nc.scalar.mul(negT[:], bankC[0:G * HG, 0:P], -1.0).then_inc(neg_done, 1)
                run(act, body)

            @block.vector
            def _(dve):
                dve.wait_ge(loaded, 16 * LOADS)
                nc.vector.tensor_copy(csel[:], csel_in[:]).then_inc(c_ready, 1)
                nc.vector.tensor_scalar(consts[:], mask_in, 0.0, NEG, ALU.is_equal, ALU.mult).then_inc(cmask, 1)
                dve.wait_ge(cmask, 1)
                nc.vector.tensor_scalar(consts[:], consts[:], cfix[:, 0:1], cfix[:, 1:2], ALU.mult, ALU.add).then_inc(c_ready, 1)

                def body(s, j, front, back, tail):
                    if front:
                        if late(s, 2):
                            dve.wait_ge(kv_full, s - 1)
                        nc.vector.tensor_copy(cst[:, j], k.ctxT[:, :, s]).then_inc(cst_done, 1)
                        dve.wait_ge(k_hi_done, s + 1)
                        dve.wait_ge(v_done, s + 1)
                        if late(s, 2):
                            dve.wait_ge(s2_full, (s - 1) * G)
                        nc.vector.scalar_tensor_tensor(k_st[:, j], k_hi[:].bitcast(F32), lomask[:, 1:2],
                                                       bankC[:, 0:T * P].rearrange("p (t n) -> p t n", t=T),
                                                       ALU.mult, ALU.add).then_inc(k_done, 1)
                        for t in range(T):
                            dve.wait_ge(q_hi_done, 2 * s + t + 1)
                            nc.vector.scalar_tensor_tensor(q_st[:, j, t], q_hi[:].bitcast(F32), lomask[:, 0:1],
                                                           bankA[:].rearrange("p (h n) -> p h n", h=HG),
                                                           ALU.mult, ALU.add).then_inc(q_done, 1)
                    for g in range(G):
                        if front:
                            dve.wait_ge(s1_full, s * G + g + 1)
                            if g == 0 and late(s, 2):
                                dve.wait_ge(maxT_full, s - 1)
                            nc.vector.tensor_reduce(mx[:, j, HG * g:HG * (g + 1)],
                                                    s1[:, g % 2].rearrange("p (h n) -> p h n", h=HG), AX,
                                                    ALU.max).then_inc(max_done, 1)
                        if tail and g == 2:
                            dve.wait_ge(turn_full, s - 1)
                            for t in range(T):
                                src = (bankA, bankC)[t][:].rearrange("p (h q c) -> p h q c", h=HG, q=4)
                                if late(s, 3):
                                    dve.wait_ge(attnT_full, s - 2)
                                nc.vector.reciprocal(rinv[:, t], src[:, :, :, HD]).then_inc(rinv_done, 1)
                                dve.wait_ge(rinv_done, (s - 2) * T + t + 1)
                                nc.vector.tensor_tensor(attn[:, 4 * t:4 * t + 4].rearrange("p q h d -> p h q d"),
                                                        src[:, :, :, 0:HD],
                                                        rinv[:, t].unsqueeze(3).broadcast_to([P, HG, 4, HD]),
                                                        ALU.mult).then_inc(attn_done, 1)
                        if tail and g == 6:
                            dve.wait_ge(o_full, s - 1)
                            nc.vector.scalar_tensor_tensor(k.x[:, s - 2], bo[:], k.gates[:, 2:3], k.x[:, s - 2],
                                                           ALU.mult, ALU.add).then_inc(bias_done, 1)
                            dve.wait_ge(bias_done, s - 1)
                            nc.vector.scalar_tensor_tensor(k.x[:, s - 2], bankC[:, 0:D], k.gates[:, 2:3], k.x[:, s - 2],
                                                           ALU.mult, ALU.add).then_inc(added, 1)
                            k.after(dve, added, s - 1)
                            nc.vector.bn_stats(k.stats[:, s - 2], k.x[:, s - 2])
                run(dve, body)


def build(nc, io, stop=None):
    with ExitStack() as ctx:
        k = Kernel(nc, ctx, io)
        phase_setup(k)
        phase_turn(k)
        phase_conv(k)
        phase_residual(k)
        if stop != "conv":
            phase_route(k, 0)
            phase_experts(k, 0)
        if stop is None or stop == "attn":
            phase_turn_rows(k)
            phase_attention(k)
        if stop is None:
            phase_route(k, 1)
            phase_experts(k, 1)
        if stop:
            done = k.sem(ctx, "dbg")
            with nc.Block() as block:
                @block.sync
                def _(sp):
                    sp.dma_start(io["out"].rearrange("b t d -> t b d"), k.x[:]).then_inc(done, 16)
                    sp.wait_ge(done, 16)
            return


def layouts(v):
    import numpy as np
    one = {"x": v["x"], "ctx": v["ctx_2048"],
           "gates": np.stack([v["g_xattn"], v["g_ffn"]], axis=1).reshape(1, 4),
           "skip": v["L0_xattn_D"].reshape(1, HC)}
    taps = np.zeros((HC, P, D), np.float32)
    for p in range(P):
        taps[:, p, p:] = v["L0_xattn_ssm_kernel"][:, :D - p]
    one["taps"] = taps
    r0 = np.concatenate([v["L0_ffn_W_router"].T, v["L0_ffn_W_sgate"].T], axis=1)
    r1 = np.concatenate([v["L1_ffn_router"], np.zeros((D, 1), np.float32)], axis=1)
    one["routers"] = np.stack([r0, r1]).reshape(2, DT, P, E + 1).transpose(2, 0, 1, 3)
    for layer, (sg, sd, eg, ed) in enumerate((
            ("L0_ffn_Ws_gate_up", "L0_ffn_Ws_down", "L0_ffn_We_gate_up", "L0_ffn_We_down"),
            ("L1_ffn_shared_w_up_gate", "L1_ffn_shared_w_down", "L1_ffn_w_up_gate", "L1_ffn_w_down"))):
        shared = v[sg].reshape(D, 2, SHARED, UNIT).transpose(0, 2, 1, 3).reshape(D, SHARED, GU)
        gu = np.concatenate([shared, v[eg].transpose(1, 0, 2)], axis=1).reshape(DT, P, UNITS * GU)
        down = np.concatenate([v[sd], v[ed].reshape(E * UNIT, D), np.zeros((KT * P - HID, D), np.float32)])
        down = down.reshape(KT, P, D).transpose(1, 0, 2).reshape(P, KT * D)
        one[f"w{layer}"] = np.concatenate([gu.transpose(1, 0, 2).reshape(P, DT * UNITS * GU), down], axis=1)
    wq = v["L1_xattn_w_q"].reshape(2, 4, HG, HD, DT, P)
    wq = np.broadcast_to(wq.transpose(5, 4, 0, 2, 1, 3)[:, :, :, :, :, None], (P, DT, 2, HG, 4, 3, HD))
    wq = np.concatenate([wq, np.zeros((P, DT, 2, HG, 4, 1, HD), np.float32)], axis=5)
    one["wq"] = wq.reshape(P, DT, 2, HG, P)
    wk = v["L1_xattn_w_k"].reshape(2, 4, HD, DT, P)
    wk = np.broadcast_to(wk.transpose(4, 3, 0, 1, 2)[:, :, :, :, None], (P, DT, 2, 4, 3, HD))
    wk = np.concatenate([wk, np.zeros((P, DT, 2, 4, 1, HD), np.float32)], axis=4)
    one["wk"] = wk.reshape(P, DT, 2, P)
    one["wv"] = v["L1_xattn_w_v"].T.reshape(DT, P, G * HD).transpose(1, 0, 2)
    one["wo"] = v["L1_xattn_w_o"].T.reshape(DT, P, D).transpose(1, 0, 2)
    one["bo"] = v["L1_xattn_b_o"].reshape(1, D)
    one["mask"] = v["mask_BxS2_if1"].reshape(1, B * P)
    csel = np.zeros((2, 2, 4, SLOT), np.float32)
    csel[0, 0, :, 24] = 1.0
    csel[1, 0, :, 25] = 1.0
    csel[0, 1, :, 25] = 1.0
    one["csel"] = csel.reshape(2, 2, P)
    one["cfix"] = np.array([[0.0, 1.0], [1.0, 0.0]], np.float32)
    lomask = np.zeros((4, SLOT, 2), np.float32)
    lomask[:, 8:16, 0] = -1.0
    lomask[:, 16:24, 1] = -1.0
    one["lomask"] = lomask.reshape(P, 2)
    return one


def kernel(**inputs):
    import numpy as np
    import concourse.bacc as bacc
    from concourse.bass_utils import run_bass_kernel_spmd

    nc = bacc.Bacc("TRN2", target_bir_lowering=False, num_devices=1)
    arrays, io = {}, {}
    for name, a in layouts({n: np.asarray(a) for n, a in inputs.items()}).items():
        a = np.ascontiguousarray(a)
        arrays[f"in_{name}"] = a
        io[name] = nc.dram_tensor(f"in_{name}", a.shape, mybir.dt.from_np(a.dtype), kind="ExternalInput").ap()
    io["out"] = nc.dram_tensor("out_x", (B, P, D), F32, kind="ExternalOutput").ap()
    build(nc, io)
    return run_bass_kernel_spmd(nc, [arrays], core_ids=[0]).results[0]["out_x"]
```

```python
from contextlib import ExitStack

import concourse.bass as bass
from concourse import mybir

F32 = mybir.dt.float32
F32R = mybir.dt.float32r
BF16 = mybir.dt.bfloat16
ALU = mybir.AluOpType
ACT = mybir.ActivationFunctionType
AX = mybir.AxisListType.X

P = 128
B = 16
D = 256
DT = D // P
E = 8
UNIT = 176
SHARED = 4
UNITS = SHARED + E
GU = 2 * UNIT
HID = UNITS * UNIT
KT = (HID + P - 1) // P
WCOLS = DT * UNITS * GU + KT * D
WCHUNK = WCOLS // B
CAPACITY = 640
HC = 16
DC = 8
G, HG, HD = 8, 4, 8
SLOT = 32
EPS = 1e-5
NEG = -1.0e30


def steps(eng, body, first, end, peel=2):
    for s in range(first, first + peel):
        body(s, s % 2)
    pairs = (end - first - peel) // 2 * 2
    if pairs:
        with eng.Fori(0, pairs // 2) as pair:
            for j in range(2):
                body(pair * 2 + (first + peel + j), (first + peel + j) % 2)
    for s in range(first + peel + pairs, end):
        body(s, s % 2)


def late(step, n):
    return not isinstance(step, int) or step >= n


class Kernel:

    def __init__(self, nc, ctx, io):
        self.nc, self.io = nc, io
        self.sb_in(ctx)

    def sb(self, ctx, name, shape, dt=F32):
        return ctx.enter_context(self.nc.sbuf_tensor(name, shape, dt))

    def ps(self, ctx, name, shape, dt=F32):
        return ctx.enter_context(self.nc.psum_tensor(name, shape, dt))

    def sem(self, ctx, name):
        return ctx.enter_context(self.nc.semaphore(name))

    def after(self, eng, sem, value):
        eng.wait_ge(self.begun, 1)
        eng.wait_ge(sem, value)

    def sb_in(self, ctx):
        self.x = self.sb(ctx, "x_res", [P, B, D])
        self.ctxT = self.sb(ctx, "ctxT", [P, DT, B, P])
        self.actT = self.sb(ctx, "actT", [P, DT, B, P])
        self.w_hi = self.sb(ctx, "w_hi", [P, WCOLS], F32R)
        self.w_lo = self.sb(ctx, "w_lo", [P, WCOLS], F32R)
        self.ident = self.sb(ctx, "ident", [P, P])
        self.gates = self.sb(ctx, "gates", [P, 4])
        self.stats = self.sb(ctx, "stats", [P, B, 6])
        self.mean = self.sb(ctx, "mean", [P, B])
        self.rstd = self.sb(ctx, "rstd", [P, B])
        self.w_unit = self.sb(ctx, "w_unit", [P, B, UNITS])
        self.begun = self.sem(ctx, "begun")
        self.w_router = self.sb(ctx, "w_router", [P, 2, DT, E + 1])


class WeightSplit:

    def __init__(self, k, layer, ctx, halves):
        self.k, self.nc = k, k.nc
        self.halves = halves
        self.raw = k.sb(ctx, f"raw{layer}", [P, halves, WCHUNK])
        self.raw_in = [k.sem(ctx, f"raw_in{layer}_{j}") for j in range(2)]
        self.hi_done, self.lo_done = k.sem(ctx, f"hi_done{layer}"), k.sem(ctx, f"lo_done{layer}")
        self.src = k.io[f"w{layer}"]

    def load(self, eng, c, j):
        if late(c, self.halves):
            eng.wait_ge(self.lo_done, c + 1 - self.halves)
        eng.dma_start(self.raw[:, j % self.halves], self.src[:, bass.ds(c * WCHUNK, WCHUNK)]).then_inc(self.raw_in[j], 16)

    def hi(self, eng, copy, c, j):
        eng.wait_ge(self.raw_in[j], 8 * (c - j) + 16)
        copy(self.k.w_hi[:, bass.ds(c * WCHUNK, WCHUNK)], self.raw[:, j % self.halves]).then_inc(self.hi_done, 1)

    def lo(self, eng, c, j):
        cols = bass.ds(c * WCHUNK, WCHUNK)
        eng.wait_ge(self.hi_done, c + 1)
        eng.tensor_tensor(self.k.w_lo[:, cols], self.raw[:, j % self.halves], self.k.w_hi[:, cols].bitcast(F32),
                          ALU.subtract).then_inc(self.lo_done, 1)


def phase_setup(k):
    nc, io = k.nc, k.io
    with ExitStack() as ctx:
        x_in, small_in, made = (k.sem(ctx, n) for n in ("x_in", "small_in", "made"))
        stat_done, tanh_done = k.sem(ctx, "stat_done0"), k.sem(ctx, "tanh_done")
        raw_gates = k.sb(ctx, "raw_gates", [P, 4])
        with nc.Block() as block:
            @block.sync
            def _(sp):
                sp.dma_start(k.x[:], io["x"].rearrange("b t d -> t b d")).then_inc(x_in, 16)
                sp.dma_start(raw_gates[:, 0:4], bass.AP(io["gates"].tensor, 0, [[0, P], [1, 4]])).then_inc(small_in, 16)
                sp.dma_start(k.w_router[:], io["routers"]).then_inc(small_in, 16)
                sp.wait_ge(small_in, 32)

            @block.gpsimd
            def _(pool):
                nc.gpsimd.memset(k.ident[:], 0.0).then_inc(made, 1)
                pool.wait_ge(made, 1)
                nc.gpsimd.affine_select(out=k.ident[:], in_=k.ident[:], compare_op=ALU.not_equal, fill=1.0,
                                        base=0, pattern=[[-1, P]], channel_multiplier=1).then_inc(k.begun, 1)

            @block.scalar
            def _(act):
                act.wait_ge(small_in, 32)
                nc.scalar.activation(k.gates[:], raw_gates[:], ACT.Tanh).then_inc(tanh_done, 1)

            @block.vector
            def _(dve):
                dve.wait_ge(x_in, 16)
                with dve.Fori(0, B) as b:
                    nc.vector.bn_stats(k.stats[:, b], k.x[:, b]).then_inc(stat_done, 1)


def norm_coefficients(k, ctx, tag):
    nc = k.nc
    coef = k.sem(ctx, f"coef{tag}")
    dist = k.sb(ctx, f"dist{tag}", [P, B])
    var = k.sb(ctx, f"var{tag}", [P, B])
    expo = k.sb(ctx, f"expo{tag}", [P, B])

    def emit(pool):
        done = [0]

        def link(ins):
            done[0] += 1
            ins.then_inc(coef, 1)
            pool.wait_ge(coef, done[0])
        link(nc.gpsimd.memset(expo[:], -0.5))
        link(nc.gpsimd.tensor_tensor(k.mean[:], k.stats[:, :, 1], k.stats[:, :, 4], ALU.add))
        link(nc.gpsimd.tensor_scalar(k.mean[:], k.mean[:], 0.5, 0.0, ALU.mult, ALU.add))
        link(nc.gpsimd.tensor_tensor(dist[:], k.mean[:], k.stats[:, :, 1], ALU.subtract))
        link(nc.gpsimd.tensor_tensor(dist[:], dist[:], dist[:], ALU.mult))
        link(nc.gpsimd.tensor_tensor(var[:], k.stats[:, :, 2], k.stats[:, :, 5], ALU.add))
        link(nc.gpsimd.tensor_scalar(var[:], var[:], 1.0 / D, EPS, ALU.mult, ALU.add))
        link(nc.gpsimd.tensor_tensor(var[:], var[:], dist[:], ALU.add))
        link(nc.gpsimd.tensor_tensor(k.rstd[:], var[:], expo[:], ALU.pow))
    return emit, coef


def phase_turn(k):
    nc, io = k.nc, k.io
    with ExitStack() as ctx:
        xn = k.sb(ctx, "xn_a", [P, 2, D])
        cx = k.sb(ctx, "cx_a", [P, 2, D])
        turned = k.ps(ctx, "turned_a", [P, 2, 2 * DT, P])
        pool_coef, coef = norm_coefficients(k, ctx, "a")
        cx_in = [k.sem(ctx, f"cx_in{j}") for j in range(2)]
        normed, turned_full, copied = (k.sem(ctx, n) for n in ("normed_a", "turned_full_a", "copied_a"))
        with nc.Block() as block:
            @block.gpsimd
            def _(pool):
                pool_coef(pool)

            @block.sync
            def _(sp):
                def body(b, j):
                    if late(b, 2):
                        sp.wait_ge(turned_full, b - 1)
                    sp.dma_start(cx[:, j], io["ctx"][b]).then_inc(cx_in[j], 16)
                steps(sp, body, 0, B)

            @block.vector
            def _(dve):
                dve.wait_ge(coef, 9)

                def body(b, j):
                    if late(b, 2):
                        dve.wait_ge(turned_full, b - 1)
                    nc.vector.tensor_scalar(xn[:, j], k.x[:, b], k.mean[:, bass.ds(b, 1)], k.rstd[:, bass.ds(b, 1)],
                                            ALU.subtract, ALU.mult).then_inc(normed, 1)
                steps(dve, body, 0, B)

            @block.tensor
            def _(pe):
                def body(b, j):
                    pe.wait_ge(normed, b + 1)
                    pe.wait_ge(cx_in[j], 8 * (b - j) + 16)
                    if late(b, 2):
                        pe.wait_ge(copied, 2 * b - 2)
                    for t in range(DT):
                        pe.transpose(turned[:, j, t], xn[:, j, t * P:(t + 1) * P], k.ident[:])
                    for t in range(DT):
                        mm = pe.transpose(turned[:, j, DT + t], cx[:, j, t * P:(t + 1) * P], k.ident[:])
                    mm.then_inc(turned_full, 1)
                steps(pe, body, 0, B)

            @block.scalar
            def _(act):
                def body(b, j):
                    act.wait_ge(turned_full, b + 1)
                    nc.scalar.copy(k.actT[:, :, b], turned[:, j, 0:DT]).then_inc(copied, 1)
                    nc.scalar.copy(k.ctxT[:, :, b], turned[:, j, DT:2 * DT]).then_inc(copied, 1)
                steps(act, body, 0, B)


def phase_conv(k):
    nc, io = k.nc, k.io
    NB2 = B // 2
    W = B * DC * DC
    with ExitStack() as ctx:
        kv = k.sb(ctx, "kv", [P, 2, DT, W])
        toep = k.sb(ctx, "toep", [P, 2, D])
        skip = k.sb(ctx, "skip", [P, HC])
        diag = k.sb(ctx, "diag", [P, P])
        diag_done = k.sem(ctx, "diag_done")
        prod = k.sb(ctx, "prod", [P, 2, W])
        conv = k.ps(ctx, "conv", [P, 4, W])
        toep_in = [k.sem(ctx, f"toep_in{j}") for j in range(2)]
        skip_in, toep_full, kv_full, conv_full = (k.sem(ctx, n) for n in ("skip_in", "toep_full", "kv_full", "conv_full"))
        prod_done, summed = k.sem(ctx, "prod_done"), k.sem(ctx, "summed")
        weights = WeightSplit(k, 0, ctx, 2)

        def head(buf, t, h):
            return buf[:, t, :, bass.ds(h * DC, DC)]

        with nc.Block() as block:
            @block.sync
            def _(sp):
                sp.dma_start(skip[:], bass.AP(io["skip"].tensor, 0, [[0, P], [1, HC]])).then_inc(skip_in, 16)

                def body(h, j):
                    if late(h, 2):
                        sp.wait_ge(conv_full, 2 * h - 2)
                    sp.dma_start(toep[:, j], io["taps"][h]).then_inc(toep_in[j], 16)
                    weights.load(sp, h, j)
                steps(sp, body, 0, HC)

            @block.gpsimd
            def _(pool):
                pool.wait_ge(skip_in, 16)

                def body(h, j):
                    if late(h, 1):
                        pool.wait_ge(toep_full, h)
                    nc.gpsimd.tensor_tensor(diag[:], k.ident[:], skip[:, bass.ds(h, 1)].broadcast_to([P, P]),
                                            ALU.mult).then_inc(diag_done, 1)
                    pool.wait_ge(diag_done, h + 1)
                    pool.wait_ge(toep_in[j], 8 * (h - j) + 16)
                    nc.gpsimd.tensor_tensor(toep[:, j, 0:P], toep[:, j, 0:P], diag[:], ALU.add).then_inc(toep_full, 1)
                    if late(h, 2):
                        pool.wait_ge(conv_full, 2 * h - 2)
                    for t in range(DT):
                        c = head(k.ctxT, t, h)
                        nc.gpsimd.tensor_tensor(
                            kv[:, j, t].rearrange("p (b j i) -> p b j i", j=DC, i=DC),
                            c.unsqueeze(3).broadcast_to([P, B, DC, DC]),
                            c.unsqueeze(2).broadcast_to([P, B, DC, DC]), ALU.mult).then_inc(kv_full, 1)
                steps(pool, body, 0, HC)

            @block.tensor
            def _(pe):
                def body(h, j):
                    pe.wait_ge(toep_full, h + 1)
                    pe.wait_ge(kv_full, 2 * h + 2)
                    for t in range(DT):
                        bank = 2 * j + t
                        if late(h, 2):
                            pe.wait_ge(prod_done, 2 * h - 3 + t)
                        for half in range(2):
                            cols = slice(half * (W // 2), (half + 1) * (W // 2))
                            for s in range(t + 1):
                                mm = pe.matmul(conv[:, bank, cols], toep[:, j, (t - s) * P:(t - s + 1) * P],
                                               kv[:, j, s, cols], start=(s == 0), stop=(s == t))
                        mm.then_inc(conv_full, 1)
                steps(pe, body, 0, HC)

            @block.vector
            def _(dve):
                def body(h, j):
                    for t in range(DT):
                        dve.wait_ge(conv_full, 2 * h + t + 1)
                        if late(h, 1):
                            dve.wait_ge(summed, 2 * h - 1 + t)
                        q = head(k.actT, t, h)
                        nc.vector.tensor_tensor(
                            prod[:, t].rearrange("p (b j i) -> p b j i", j=DC, i=DC),
                            conv[:, 2 * j + t].rearrange("p (b j i) -> p b j i", j=DC, i=DC),
                            q.unsqueeze(2).broadcast_to([P, B, DC, DC]), ALU.mult).then_inc(prod_done, 1)
                        k.after(dve, prod_done, 2 * h + t + 1)
                        nc.vector.tensor_reduce(q, prod[:, t].rearrange("p (b j i) -> p b j i", j=DC, i=DC),
                                                AX, ALU.add).then_inc(summed, 1)
                    weights.lo(dve, h, j)
                steps(dve, body, 0, HC)

            @block.scalar
            def _(act):
                def body(h, j):
                    weights.hi(act, nc.scalar.copy, h, j)
                steps(act, body, 0, HC)


def phase_residual(k):
    nc = k.nc
    with ExitStack() as ctx:
        stage = k.sb(ctx, "stage_c", [P, 2, DT, P])
        back = k.ps(ctx, "back_c", [P, 2, 512])
        staged, turned, added = (k.sem(ctx, n) for n in ("staged_c", "turned_c", "added_c"))
        with nc.Block() as block:
            @block.scalar
            def _(act):
                def body(b, j):
                    if late(b, 2):
                        act.wait_ge(turned, b - 1)
                    nc.scalar.copy(stage[:, j], k.actT[:, :, b]).then_inc(staged, 1)
                steps(act, body, 0, B)

            @block.tensor
            def _(pe):
                def body(b, j):
                    pe.wait_ge(staged, b + 1)
                    if late(b, 2):
                        pe.wait_ge(added, b - 1)
                    for t in range(DT):
                        mm = pe.transpose(back[:, j, t * P:(t + 1) * P], stage[:, j, t], k.ident[:])
                    mm.then_inc(turned, 1)
                steps(pe, body, 0, B)

            @block.vector
            def _(dve):
                def body(b, j):
                    dve.wait_ge(turned, b + 1)
                    nc.vector.scalar_tensor_tensor(k.x[:, b], back[:, j, 0:D], k.gates[:, 0:1], k.x[:, b],
                                                   ALU.mult, ALU.add).then_inc(added, 1)
                    k.after(dve, added, b + 1)
                    nc.vector.bn_stats(k.stats[:, b], k.x[:, b])
                steps(dve, body, 0, B)


def phase_route(k, layer):
    nc = k.nc
    cols = E + 1 if layer == 0 else E
    with ExitStack() as ctx:
        xn = k.sb(ctx, f"xn_r{layer}", [P, 2, D])
        logT = k.sb(ctx, f"logT{layer}", [E + 1, B * P])
        lg = k.sb(ctx, f"lg{layer}", [P, B, E + 1])
        rev = k.sb(ctx, f"rev{layer}", [P, B, E])
        tmp = {n: k.sb(ctx, f"{n}{layer}", [P, B, E]) for n in ("eq", "rank", "one1", "one2", "lg2", "ex", "sel", "valid")}
        row = {n: k.sb(ctx, f"{n}_row{layer}", [P, B]) for n in ("m1", "m2", "r1", "r2", "gap", "e2", "den", "inv")}
        gate9 = k.sb(ctx, f"gate9{layer}", [P, B])
        sel_pad = k.sb(ctx, f"sel_pad{layer}", [P, 2 * B, E], BF16)
        sel16 = sel_pad[:, B:]
        ones16 = k.sb(ctx, f"ones16{layer}", [P, P], BF16)
        tri16 = k.sb(ctx, f"tri16{layer}", [P, P], BF16)
        turned = k.ps(ctx, f"turned_r{layer}", [P, 2, 512])
        logP = k.ps(ctx, f"logP{layer}", [P, 2, 512])
        lgP = k.ps(ctx, f"lgP{layer}", [P, B * (E + 1)])
        posP = k.ps(ctx, f"posP{layer}", [P, B, E])
        pool_coef, coef = norm_coefficients(k, ctx, f"r{layer}")
        normed, turned_full, copied = (k.sem(ctx, f"{n}_r{layer}") for n in ("normed", "turned_full", "copied"))
        logits_full, logits_out, back_full, chain = (k.sem(ctx, f"{n}_r{layer}") for n in
                                                     ("logits_full", "logits_out", "back_full", "chain"))
        consts, ex_in, ex_out, pos_in, pos_out = (k.sem(ctx, f"{n}_r{layer}") for n in
                                                  ("consts", "ex_in", "ex_out", "pos_in", "pos_out"))
        with nc.Block() as block:
            @block.gpsimd
            def _(pool):
                pool_coef(pool)
                for e in range(E):
                    nc.gpsimd.memset(rev[:, :, e], float(E - e)).then_inc(consts, 1)
                nc.gpsimd.memset(ones16[:], 1.0).then_inc(consts, 1)
                pool.wait_ge(consts, E + 1)
                nc.gpsimd.affine_select(out=tri16[:], in_=ones16[:], compare_op=ALU.is_gt, fill=0.0,
                                        base=0, pattern=[[1, P]], channel_multiplier=-1).then_inc(consts, 1)

            @block.vector
            def _(dve):
                dve.wait_ge(coef, 9)

                def body(b, j):
                    if late(b, 2):
                        dve.wait_ge(turned_full, b - 1)
                    nc.vector.tensor_scalar(xn[:, j], k.x[:, b], k.mean[:, bass.ds(b, 1)], k.rstd[:, bass.ds(b, 1)],
                                            ALU.subtract, ALU.mult).then_inc(normed, 1)
                steps(dve, body, 0, B)
                count = [0]

                def link(ins):
                    count[0] += 1
                    ins.then_inc(chain, 1)
                    dve.wait_ge(chain, count[0])

                def bc(r):
                    return r[:].unsqueeze(2).broadcast_to([P, B, E])

                def best(logits, m, r, one):
                    link(nc.vector.tensor_reduce(row[m][:], logits, AX, ALU.max))
                    link(nc.vector.tensor_tensor(tmp["eq"][:], logits, bc(row[m]), ALU.is_equal))
                    link(nc.vector.tensor_tensor(tmp["rank"][:], tmp["eq"][:], rev[:], ALU.mult))
                    link(nc.vector.tensor_reduce(row[r][:], tmp["rank"][:], AX, ALU.max))
                    link(nc.vector.tensor_tensor(tmp[one][:], tmp["rank"][:], bc(row[r]), ALU.is_equal))

                dve.wait_ge(back_full, 1)
                dve.wait_ge(consts, E + 2)
                link(nc.vector.tensor_copy(lg[:, :, 0:cols], lgP[:, 0:B * cols].rearrange("p (b e) -> p b e", e=cols)))
                logits = lg[:, :, 0:E]
                best(logits, "m1", "r1", "one1")
                link(nc.vector.scalar_tensor_tensor(tmp["lg2"][:], tmp["one1"][:], NEG, logits, ALU.mult, ALU.add))
                best(tmp["lg2"][:], "m2", "r2", "one2")
                if layer == 0:
                    link(nc.vector.tensor_tensor(tmp["ex"][:], logits, bc(row["m1"]), ALU.subtract))
                    nc.vector.tensor_copy(gate9[:], lg[:, :, E]).then_inc(ex_in, 1)
                    dve.wait_ge(ex_out, 2)
                    link(nc.vector.tensor_reduce(row["den"][:], tmp["ex"][:], AX, ALU.add))
                    link(nc.vector.reciprocal(row["inv"][:], row["den"][:]))
                    link(nc.vector.tensor_tensor(tmp["sel"][:], tmp["one1"][:], tmp["one2"][:], ALU.add))
                    link(nc.vector.tensor_tensor(tmp["ex"][:], tmp["ex"][:], tmp["sel"][:], ALU.mult))
                    link(nc.vector.tensor_tensor(k.w_unit[:, :, SHARED:], tmp["ex"][:], bc(row["inv"]), ALU.mult))
                    link(nc.vector.tensor_scalar(gate9[:], gate9[:], 1.0, None, ALU.add))
                    link(nc.vector.reciprocal(row["gap"][:], gate9[:]))
                    link(nc.vector.tensor_copy(k.w_unit[:, :, 0:SHARED],
                                               row["gap"][:].unsqueeze(2).broadcast_to([P, B, SHARED])))
                else:
                    link(nc.vector.tensor_tensor(sel16, tmp["one1"][:], tmp["one2"][:], ALU.add))
                    nc.vector.memset(sel_pad[:, 0:B], 0.0).then_inc(pos_in, 1)
                    nc.vector.tensor_tensor(row["gap"][:], row["m2"][:], row["m1"][:], ALU.subtract).then_inc(ex_in, 1)
                    dve.wait_ge(ex_out, 1)
                    link(nc.vector.tensor_scalar(row["den"][:], row["e2"][:], 1.0, None, ALU.add))
                    link(nc.vector.reciprocal(row["inv"][:], row["den"][:]))
                    link(nc.vector.tensor_tensor(tmp["ex"][:], tmp["one2"][:], bc(row["e2"]), ALU.mult))
                    link(nc.vector.tensor_tensor(tmp["ex"][:], tmp["ex"][:], tmp["one1"][:], ALU.add))
                    link(nc.vector.tensor_tensor(tmp["ex"][:], tmp["ex"][:], bc(row["inv"]), ALU.mult))
                    dve.wait_ge(pos_out, 1)
                    link(nc.vector.tensor_scalar(tmp["valid"][:], posP[:], float(CAPACITY), None, ALU.is_lt))
                    link(nc.vector.tensor_tensor(k.w_unit[:, :, SHARED:], tmp["ex"][:], tmp["valid"][:], ALU.mult))
                    link(nc.vector.memset(k.w_unit[:, :, 0:SHARED], 1.0))

            @block.scalar
            def _(act):
                def body(b, j):
                    act.wait_ge(turned_full, b + 1)
                    nc.scalar.copy(k.actT[:, :, b], turned[:, j, 0:D].rearrange("p (t n) -> p t n", t=DT)).then_inc(copied, 1)
                steps(act, body, 0, B)
                for c in range(4):
                    act.wait_ge(logits_full, c + 1)
                    nc.scalar.copy(logT[0:cols, c * 512:(c + 1) * 512], logP[0:cols, c % 2]).then_inc(logits_out, 1)
                act.wait_ge(ex_in, 1)
                if layer == 0:
                    act.wait_ge(chain, 13)
                    nc.scalar.activation(tmp["ex"][:], tmp["ex"][:], ACT.Exp).then_inc(ex_out, 1)
                    nc.scalar.activation(gate9[:], gate9[:], ACT.Exp, scale=-1.0).then_inc(ex_out, 1)
                else:
                    nc.scalar.activation(row["e2"][:], row["gap"][:], ACT.Exp).then_inc(ex_out, 1)

            @block.tensor
            def _(pe):
                def body(b, j):
                    pe.wait_ge(normed, b + 1)
                    if late(b, 2):
                        pe.wait_ge(copied, b - 1)
                    for t in range(DT):
                        mm = pe.transpose(turned[:, j, t * P:(t + 1) * P], xn[:, j, t * P:(t + 1) * P], k.ident[:])
                    mm.then_inc(turned_full, 1)
                steps(pe, body, 0, B)
                pe.wait_ge(copied, B)
                for c in range(4):
                    if c >= 2:
                        pe.wait_ge(logits_out, c - 1)
                    for t in range(DT):
                        mm = pe.matmul(logP[0:cols, c % 2], k.w_router[:, layer, t, 0:cols],
                                       k.actT[:, t, 4 * c:4 * c + 4], start=(t == 0), stop=(t == DT - 1))
                    mm.then_inc(logits_full, 1)
                pe.wait_ge(logits_out, 4)
                for b in range(B):
                    mm = pe.transpose(lgP[:, b * cols:(b + 1) * cols], logT[0:cols, b * P:(b + 1) * P],
                                      k.ident[0:cols, 0:cols])
                mm.then_inc(back_full, 1)
                if layer == 1:
                    pe.wait_ge(pos_in, 1)
                    pe.wait_ge(consts, E + 2)
                    for back in range(1, B):
                        pe.matmul(posP[:], ones16[:], sel_pad[:, B - back:2 * B - back], start=(back == 1), stop=False)
                    mm = pe.matmul(posP[:], tri16[:], sel16, start=False, stop=True)
                    mm.then_inc(pos_out, 1)


def phase_experts(k, layer):
    nc, io = k.nc, k.io
    GW = DT * UNITS * GU
    RING = 4
    NG = (KT + 3) // 4
    with ExitStack() as ctx:
        t_ = f"_e{layer}"
        xs_hi = k.sb(ctx, "xs_hi" + t_, [P, 2, DT, P], F32R)
        xs_lo = k.sb(ctx, "xs_lo" + t_, [P, 2, DT, P], F32R)
        silu = k.sb(ctx, "silu" + t_, [P, RING, UNIT])
        h = k.sb(ctx, "h" + t_, [P, 2, HID])
        hT_hi = k.sb(ctx, "hT_hi" + t_, [P, 2, 4, P], F32R)
        hT_lo = k.sb(ctx, "hT_lo" + t_, [P, 2, 4, P], F32R)
        gu = k.ps(ctx, "gu" + t_, [P, RING, 512])
        turned = k.ps(ctx, "turned" + t_, [P, 2, 512])
        out = k.ps(ctx, "out" + t_, [P, 2, 512])
        (xs_hi_done, xs_done, gu_full, silu_done, h_done, turned_full, hi_done, hT_done, down_full,
         added, stored) = (k.sem(ctx, n + t_) for n in (
             "xs_hi_done", "xs_done", "gu_full", "silu_done", "h_done", "turned_full", "hi_done",
             "hT_done", "down_full", "added", "stored"))
        gate = k.gates[:, 2 * layer + 1:2 * layer + 2]

        def tiles(g):
            return [(c, min(P, HID - c * P)) for c in range(4 * g, min(4 * g + 4, KT))]

        def plan(s, front, turn, down, split=None):
            for u in range(UNITS):
                if split and front and u == 5 and not (isinstance(s, int) and s == B - 1):
                    split(s + 1)
                if front:
                    front(u)
                if turn and u % 2 == 0 and u // 2 < NG:
                    turn(u // 2)
                if down and u % 2 == 0 and 1 <= u // 2 <= NG:
                    down(u // 2 - 1)

        def run(eng, body):
            body(0, 0, True, False)
            body(1, 1, True, True)
            with eng.Fori(0, B // 2 - 2) as pair:
                for j in range(2):
                    body(pair * 2 + (2 + j), j, True, True)
            body(B - 2, 0, True, True)
            body(B - 1, 1, True, True)
            body(B, 0, False, True)

        with nc.Block() as block:
            @block.tensor
            def _(pe):
                def body(s, j, has_front, has_down):
                    i = 1 - j

                    def front(u):
                        if u == 0:
                            pe.wait_ge(xs_done, s + 1)
                        if late(s, 1) or u >= RING:
                            pe.wait_ge(h_done, s * UNITS + u - RING + 1)
                        for t in range(DT):
                            w0 = t * UNITS * GU + u * GU
                            for n, (a, w) in enumerate(((xs_hi, k.w_hi), (xs_hi, k.w_lo), (xs_lo, k.w_hi))):
                                mm = pe.matmul(gu[:, u % RING, 0:GU], a[:, j, t], w[:, w0:w0 + GU],
                                               start=(t == 0 and n == 0), stop=(t == DT - 1 and n == 2))
                        mm.then_inc(gu_full, 1)

                    def turn(g):
                        if g == 0:
                            pe.wait_ge(h_done, s * UNITS)
                        half = (g + i * NG) % 2
                        if late(s, 2) or g >= 2:
                            k.after(pe, hT_done, (s - 1) * NG + g - 1)
                        for c, rows in tiles(g):
                            mm = pe.transpose(turned[0:rows, half, (c % 4) * P:(c % 4 + 1) * P],
                                              h[:, i, c * P:c * P + rows], k.ident[:])
                        mm.then_inc(turned_full, 1)

                    def down(g):
                        if g == 0 and late(s, 3):
                            pe.wait_ge(added, s - 1)
                        pe.wait_ge(hT_done, (s - 1) * NG + g + 1)
                        half = (g + i * NG) % 2
                        for c, rows in tiles(g):
                            for n, (a, w) in enumerate(((hT_hi, k.w_hi), (hT_hi, k.w_lo), (hT_lo, k.w_hi))):
                                mm = pe.matmul(out[:, i, 0:D], a[0:rows, half, c % 4], w[0:rows, GW + c * D:GW + (c + 1) * D],
                                               start=(c == 0 and n == 0), stop=(c == KT - 1 and n == 2))
                        mm.then_inc(down_full, 1)
                    plan(s, has_front and front, has_down and turn, has_down and down)
                run(pe, body)

            @block.scalar
            def _(act):
                def body(s, j, has_front, has_down):
                    i = 1 - j

                    def split(e):
                        half = j if e is s else i
                        if late(s, 1):
                            act.wait_ge(gu_full, s * UNITS)
                        nc.scalar.copy(xs_hi[:, half], k.actT[:, :, e]).then_inc(xs_hi_done, 1)
                    if isinstance(s, int) and s == 0:
                        split(s)

                    def front(u):
                        act.wait_ge(gu_full, s * UNITS + u + 1)
                        if late(s, 1) or u >= RING:
                            act.wait_ge(h_done, s * UNITS + u - RING + 1)
                        nc.scalar.activation(silu[:, u % RING], gu[:, u % RING, 0:UNIT], ACT.Silu).then_inc(silu_done, 1)

                    def turn(g):
                        half = (g + i * NG) % 2
                        act.wait_ge(turned_full, (s - 1) * NG + g + 1)
                        if late(s, 2) or g >= 2:
                            act.wait_ge(down_full, (s - 1) * NG + g - 1)
                        n, rows = len(tiles(g)), tiles(g)[0][1]
                        nc.scalar.copy(hT_hi[0:rows, half, 0:n],
                                       turned[0:rows, half, 0:n * P].rearrange("p (c n) -> p c n", n=P)).then_inc(hi_done, 1)
                    plan(s, has_front and front, has_down and turn, None, split)
                run(act, body)

            @block.vector
            def _(dve):
                dve.sem_inc(added, 1)

                def body(s, j, has_front, has_down):
                    i = 1 - j

                    def split(e):
                        half = j if e is s else i
                        dve.wait_ge(xs_hi_done, e + 1)
                        if late(s, 1):
                            dve.wait_ge(gu_full, s * UNITS)
                        nc.vector.tensor_tensor(xs_lo[:, half], k.actT[:, :, e], xs_hi[:, half].bitcast(F32),
                                                ALU.subtract).then_inc(xs_done, 1)
                    if isinstance(s, int) and s == 0:
                        split(s)

                    def front(u):
                        dve.wait_ge(silu_done, s * UNITS + u + 1)
                        if u == 0 and late(s, 2):
                            dve.wait_ge(turned_full, (s - 1) * NG)
                        nc.vector.scalar_tensor_tensor(
                            h[:, j, u * UNIT:(u + 1) * UNIT], gu[:, u % RING, UNIT:GU],
                            k.w_unit[:, s, u:u + 1], silu[:, u % RING], ALU.mult, ALU.mult).then_inc(h_done, 1)

                    def turn(g):
                        half = (g + i * NG) % 2
                        dve.wait_ge(hi_done, (s - 1) * NG + g + 1)
                        if late(s, 2) or g >= 2:
                            dve.wait_ge(down_full, (s - 1) * NG + g - 1)
                        n, rows = len(tiles(g)), tiles(g)[0][1]
                        nc.vector.tensor_tensor(hT_lo[0:rows, half, 0:n],
                                                turned[0:rows, half, 0:n * P].rearrange("p (c n) -> p c n", n=P),
                                                hT_hi[0:rows, half, 0:n].bitcast(F32), ALU.subtract).then_inc(hT_done, 1)
                    plan(s, has_front and front, has_down and turn, None, split)
                    if has_down:
                        dve.wait_ge(down_full, s * NG)
                        nc.vector.scalar_tensor_tensor(k.x[:, s - 1], out[:, i, 0:D], gate, k.x[:, s - 1],
                                                       ALU.mult, ALU.add).then_inc(added, 1)
                        if layer == 0:
                            k.after(dve, added, s + 1)
                            nc.vector.bn_stats(k.stats[:, s - 1], k.x[:, s - 1])
                run(dve, body)

            if layer == 1:
                @block.sync
                def _(sp):
                    with sp.Fori(0, B) as b:
                        sp.wait_ge(added, b + 2)
                        sp.dma_start(io["out"][b], k.x[:, b]).then_inc(stored, 16)
                    sp.wait_ge(stored, 16 * B)

def phase_turn_rows(k):
    nc = k.nc
    with ExitStack() as ctx:
        xn = k.sb(ctx, "xn_q", [P, 2, D])
        turned = k.ps(ctx, "turned_q", [P, 2, 512])
        pool_coef, coef = norm_coefficients(k, ctx, "q")
        normed, turned_full, copied = (k.sem(ctx, n) for n in ("normed_q", "turned_full_q", "copied_q"))
        with nc.Block() as block:
            @block.gpsimd
            def _(pool):
                pool_coef(pool)

            @block.vector
            def _(dve):
                dve.wait_ge(coef, 9)

                def body(b, j):
                    if late(b, 2):
                        dve.wait_ge(turned_full, b - 1)
                    nc.vector.tensor_scalar(xn[:, j], k.x[:, b], k.mean[:, bass.ds(b, 1)], k.rstd[:, bass.ds(b, 1)],
                                            ALU.subtract, ALU.mult).then_inc(normed, 1)
                steps(dve, body, 0, B)

            @block.tensor
            def _(pe):
                def body(b, j):
                    pe.wait_ge(normed, b + 1)
                    if late(b, 2):
                        pe.wait_ge(copied, b - 1)
                    for t in range(DT):
                        mm = pe.transpose(turned[:, j, t * P:(t + 1) * P], xn[:, j, t * P:(t + 1) * P], k.ident[:])
                    mm.then_inc(turned_full, 1)
                steps(pe, body, 0, B)

            @block.scalar
            def _(act):
                def body(b, j):
                    act.wait_ge(turned_full, b + 1)
                    nc.scalar.copy(k.actT[:, :, b], turned[:, j, 0:D].rearrange("p (t n) -> p t n", t=DT)).then_inc(copied, 1)
                steps(act, body, 0, B)


PLAN = (("project", 0), ("exps", 0), ("spread", 0), ("exps", 1), ("exps", 2), ("turn", 0), ("exps", 3),
        ("maxima", 0), ("maxima", 1), ("values", 0), ("turn", 1), ("maxima", 2), ("maxima", 3), ("exps", 4),
        ("maxima", 4), ("exps", 5), ("maxima", 5), ("output", 0), ("exps", 6), ("exps", 7), ("maxima", 6),
        ("maxima", 7), ("values", 1), ("negate", 0))


def phase_attention(k):
    nc, io = k.nc, k.io
    T = G // 4
    SCALE = float(HD) ** -0.5
    OF_FRONT, OF_BACK = ("project", "spread", "maxima", "negate"), ("exps", "values")
    with ExitStack() as ctx:
        wq = k.sb(ctx, "wq", [P, DT, T * P])
        wk = k.sb(ctx, "wk", [P, DT, T, P])
        wv = k.sb(ctx, "wv", [P, DT, G * HD])
        wo = k.sb(ctx, "wo", [P, DT, D])
        bo = k.sb(ctx, "bo", [P, D])
        csel = k.sb(ctx, "csel", [2, P], BF16)
        cfix = k.sb(ctx, "cfix", [2, 2])
        rowfix = k.sb(ctx, "rowfix", [P, 2])
        consts = k.sb(ctx, "consts", [2, B * P], BF16)
        spread = k.sb(ctx, "spread", [P, 2, HG, P], F32R)
        ident16 = k.sb(ctx, "ident16", [P, P], BF16)
        causal = k.sb(ctx, "causal", [P, 2, P], BF16)
        cst = k.sb(ctx, "cst", [P, 2, DT, P])
        k_hi = k.sb(ctx, "k_hi", [P, T, P], F32R)
        q_part = k.sb(ctx, "q_part", [P, 2, T * P], F32R)
        k_st = k.sb(ctx, "k_st", [P, 2, T, 4, P], F32R)
        q_st = k.sb(ctx, "q_st", [P, 2, HG, T, P], F32R)
        vaug = k.sb(ctx, "vaug", [P, 2, G, SLOT])
        mx = k.sb(ctx, "mx", [P, 2, 4, HG, T])
        negT = k.sb(ctx, "negT", [G * HG, P], F32R)
        probs = k.sb(ctx, "probs", [P, 4, HG * P])
        oT = k.sb(ctx, "oT", [P, T, HG, P])
        rinv = k.sb(ctx, "rinv", [P, T, HG, 4])
        attn = k.sb(ctx, "attn", [P, G, HG, HD])
        attnT = k.sb(ctx, "attnT", [P, DT, P])
        bankA = k.ps(ctx, "bankA", [P, 512])
        bankC = k.ps(ctx, "bankC", [P, 512])
        s1 = k.ps(ctx, "s1", [P, 2, 512])
        s2 = k.ps(ctx, "s2", [P, 2, 512])
        oP = k.ps(ctx, "oP", [P, T, 512])
        names = ("loaded", "made", "c_ready", "cst_done", "kv_full", "k_hi_done", "k_done", "v_done", "q_full",
                 "q_hi_done", "q_lo_done", "spread_full", "q0_done", "q1_done", "s1_full", "max_done", "maxT_full",
                 "neg_done", "neg_in", "s2_full", "exp_done", "pv_full", "oT_done", "turn_full", "rinv_done",
                 "attn_done", "attnT_full", "attnT_done", "o_full", "bias_done", "added", "cmask")
        (loaded, made, c_ready, cst_done, kv_full, k_hi_done, k_done, v_done, q_full,
         q_hi_done, q_lo_done, spread_full, q0_done, q1_done, s1_full, max_done, maxT_full,
         neg_done, neg_in, s2_full, exp_done, pv_full, oT_done, turn_full, rinv_done,
         attn_done, attnT_full, attnT_done, o_full, bias_done, added, cmask) = (k.sem(ctx, n + "_t") for n in names)
        weights = WeightSplit(k, 1, ctx, 1)
        mask_in = probs[0:2].rearrange("p q n -> p (q n)").bitcast(mybir.dt.int32)
        csel_in = attnT[0:2, 0, :]
        spread_in = oT[:].rearrange("p t h n -> p (t h n)")
        LOADS = 10

        def run(eng, emit):
            def body(s, j, front, back, tail):
                for part, arg in PLAN:
                    if front if part in OF_FRONT else back if part in OF_BACK else tail:
                        emit(s, j, part, arg)
            body(0, 0, True, False, False)
            body(1, 1, True, True, False)
            with eng.Fori(0, B // 2 - 1) as pair:
                for j in range(2):
                    body(pair * 2 + (2 + j), j, True, True, True)
            body(B, 0, False, True, True)
            body(B + 1, 1, False, False, True)

        def four(mask):
            return mask.unsqueeze(1).broadcast_to([P, 4, P])

        def rows(buf, s):
            return buf[SLOT * s:SLOT * (s + 1)]

        with nc.Block() as block:
            @block.sync
            def _(sp):
                for dst, src in ((wq, io["wq"]), (wk, io["wk"]), (wv, io["wv"]), (wo, io["wo"]), (attnT[0:2, 0], io["csel"]),
                                 (cfix, io["cfix"]), (rowfix, io["rowfix"])):
                    sp.dma_start(dst[:], src).then_inc(loaded, 16)
                sp.dma_start(spread_in, io["spread"]).then_inc(loaded, 16)
                sp.dma_start(bo[:], bass.AP(io["bo"].tensor, 0, [[0, P], [1, D]])).then_inc(loaded, 16)
                sp.dma_start(mask_in, bass.AP(io["mask"].tensor, 0, [[0, 2], [1, B * P]])).then_inc(loaded, 16)

                def emit(s, j, part, arg):
                    if part == "project":
                        weights.load(sp, s, j)
                    if part == "negate":
                        sp.wait_ge(neg_done, s + 1)
                        sp.dma_start(q_st[24:P:SLOT, j].bitcast(F32).rearrange("s h t n -> s (h t) n"),
                                     negT[:].bitcast(F32)).then_inc(neg_in, 16)
                run(sp, emit)

            @block.gpsimd
            def _(pool):
                nc.gpsimd.memset(vaug[:], 0.0).then_inc(made, 1)
                nc.gpsimd.memset(causal[:], 0.0).then_inc(made, 1)
                nc.gpsimd.memset(k_st[:].bitcast(F32), 0.0).then_inc(made, 1)
                pool.wait_ge(made, 3)
                nc.gpsimd.memset(vaug[:, :, :, HD:HD + 1], 1.0).then_inc(made, 1)
                nc.gpsimd.affine_select(out=causal[:, 0], in_=causal[:, 0], compare_op=ALU.is_ge, fill=NEG,
                                        base=0, pattern=[[-1, P]], channel_multiplier=1).then_inc(made, 1)
                nc.gpsimd.affine_select(out=causal[:, 1], in_=causal[:, 1], compare_op=ALU.is_ge, fill=NEG,
                                        base=0, pattern=[[1, P]], channel_multiplier=-1).then_inc(made, 1)
                nc.gpsimd.tensor_copy(ident16[:], k.ident[:]).then_inc(made, 1)

                def body(c, j):
                    weights.hi(pool, nc.gpsimd.tensor_copy, c, j)
                    weights.lo(pool, c, j)
                steps(pool, body, 0, B)

            @block.tensor
            def _(pe):
                pe.sem_inc(attnT_full, 1)
                pe.wait_ge(loaded, 16 * LOADS)
                pe.wait_ge(c_ready, 3)
                pe.wait_ge(made, 7)

                def emit(s, j, part, arg):
                    i, g, t, slot = 1 - j, arg, arg // 4, arg % 4
                    if part == "project":
                        if late(s, 3):
                            pe.wait_ge(attnT_done, s - 1)
                        for t in range(T):
                            for d in range(DT):
                                mm = pe.matmul(bankA[:, t * P:(t + 1) * P], wq[:, d, t * P:(t + 1) * P], k.actT[:, d, s],
                                               start=(d == 0), stop=(d == DT - 1))
                        mm.then_inc(q_full, 1)
                        if late(s, 1):
                            pe.wait_ge(neg_done, s)
                        for t in range(T):
                            for d in range(DT):
                                pe.matmul(bankC[:, t * P:(t + 1) * P], wk[:, d, t], k.ctxT[:, d, s],
                                          start=(d == 0), stop=False)
                            pe.matmul(bankC[:, t * P:(t + 1) * P], csel[:], consts[:, bass.ds(s * P, P)],
                                      start=False, stop=True)
                        pe.wait_ge(cst_done, s + 1)
                        for d in range(DT):
                            mm = pe.matmul(bankC[:, T * P:T * P + G * HD], cst[:, j, d], wv[:, d],
                                           start=(d == 0), stop=(d == DT - 1))
                        mm.then_inc(kv_full, 1)
                    elif part == "spread":
                        pe.wait_ge(q_hi_done, s + 1)
                        pe.wait_ge(q_lo_done, s + 1)
                        for h in range(HG):
                            for n in range(2):
                                mm = pe.matmul(s1[:, h // 2, h % 2 * T * P:(h % 2 + 1) * T * P], spread[:, n, h],
                                               q_part[:, n], start=(n == 0), stop=(n == 1))
                            if h % 2:
                                mm.then_inc(spread_full, 1)
                    elif part == "maxima":
                        if g == 0:
                            pe.wait_ge(k_done, 4 * s + 4)
                            pe.wait_ge(q0_done, s + 1)
                            pe.wait_ge(q1_done, s + 1)
                        if g >= 2:
                            pe.wait_ge(max_done, s * G + g - 1)
                        pe.matmul(s1[:, g % 2], ident16[:], four(causal[:, 0]), start=True, stop=False, skip_group_check=True)
                        h, t = g // T, g % T
                        pe.matmul(s1[:, g % 2], q_st[:, j, h, t], k_st[:, j, t], start=False, stop=True,
                                  skip_group_check=True).then_inc(s1_full, 1)
                    elif part == "exps":
                        if g == 0:
                            pe.wait_ge(neg_in, s * 16)
                        if late(s, 2) or g >= 2:
                            pe.wait_ge(exp_done, (s - 1) * G + g - 1)
                        pe.matmul(s2[:, g % 2], ident16[:], four(causal[:, 1]), start=True, stop=False, skip_group_check=True)
                        pe.matmul(s2[:, g % 2], k_st[:, i, t, slot], q_st[:, i, :, t],
                                  start=False, stop=True, skip_group_check=True).then_inc(s2_full, 1)
                    elif part == "values":
                        t = arg
                        pe.wait_ge(exp_done, (s - 1) * G + 4 * t + 4)
                        if late(s, 2):
                            pe.wait_ge(oT_done, (s - 2) * T + t + 1)
                        for q in range(4):
                            mm = pe.matmul(oP[SLOT * q:SLOT * (q + 1), t], vaug[:, i, 4 * t + q], probs[:, q],
                                           start=True, stop=True)
                        mm.then_inc(pv_full, 1)
                    elif part == "turn" and arg == 0:
                        pe.wait_ge(oT_done, (s - 1) * T)
                        if late(s, B) and isinstance(s, int):
                            pe.wait_ge(attnT_done, s - 1)
                            pe.wait_ge(added, s - 2)
                            pe.wait_ge(neg_done, B)
                        else:
                            pe.wait_ge(q_lo_done, s + 1)
                            pe.wait_ge(v_done, s + 1)
                            pe.wait_ge(k_done, 4 * s + 4)
                        for t in range(T):
                            for h in range(HG):
                                mm = pe.transpose((bankA, bankC)[t][:, h * P:(h + 1) * P], oT[:, t, h], k.ident[:])
                        mm.then_inc(turn_full, 1)
                    elif part == "turn":
                        pe.wait_ge(attn_done, (s - 1) * T)
                        for d in range(DT):
                            mm = pe.transpose(bankA[:, d * P:(d + 1) * P],
                                              attn[:].rearrange("p g h d -> p (g h d)")[:, d * P:(d + 1) * P], k.ident[:])
                        mm.then_inc(attnT_full, 1)
                    elif part == "output":
                        pe.wait_ge(attnT_done, s)
                        for d in range(DT):
                            mm = pe.matmul(bankC[:, 0:D], attnT[:, d], wo[:, d], start=(d == 0), stop=(d == DT - 1))
                        mm.then_inc(o_full, 1)
                    elif part == "negate":
                        pe.wait_ge(max_done, (s + 1) * G)
                        if late(s, 2):
                            pe.wait_ge(added, s - 1)
                        else:
                            pe.wait_ge(v_done, s + 1)
                        pe.transpose(bankC[0:G * HG, 0:P], mx[:, j].rearrange("p s h t -> p (s h t)"), k.ident[:]).then_inc(maxT_full, 1)
                run(pe, emit)

            @block.scalar
            def _(act):
                act.sem_inc(attnT_done, 1)
                act.wait_ge(loaded, 16 * LOADS)
                nc.scalar.copy(spread[:].rearrange("p a h n -> p (a h n)"), spread_in).then_inc(c_ready, 1)

                def emit(s, j, part, arg):
                    g = arg
                    if part == "project":
                        act.wait_ge(q_full, s + 1)
                        if late(s, 1):
                            act.wait_ge(spread_full, s * T)
                        nc.scalar.copy(q_part[:, 0], bankA[:, 0:T * P]).then_inc(q_hi_done, 1)
                        act.wait_ge(kv_full, s + 1)
                        if late(s, 1):
                            act.wait_ge(k_done, 4 * s)
                        nc.scalar.copy(k_hi[:], bankC[:, 0:T * P].rearrange("p (t n) -> p t n", t=T)).then_inc(k_hi_done, 1)
                        if late(s, 2):
                            act.wait_ge(pv_full, (s - 1) * T)
                        else:
                            act.wait_ge(made, 4)
                        nc.scalar.copy(vaug[:, j, :, 0:HD], bankC[:, T * P:T * P + G * HD].rearrange("p (g d) -> p g d", g=G)).then_inc(v_done, 1)
                    elif part == "spread":
                        act.wait_ge(spread_full, s * T + 1)
                        if late(s, 2):
                            act.wait_ge(s2_full, (s - 1) * G)
                        nc.scalar.activation(q_st[:, j, 0:2], s1[:, 0].rearrange("p (h t n) -> p h t n", h=2, t=T), ACT.Identity,
                                             bias=rowfix[:, 1:2]).then_inc(q0_done, 1)
                    elif part == "exps":
                        act.wait_ge(s2_full, (s - 1) * G + g + 1)
                        if late(s, 2) or g >= 4:
                            act.wait_ge(pv_full, (s - 1) * T + g // 4)
                        nc.scalar.activation(probs[:, g % 4], s2[:, g % 2], ACT.Exp, scale=SCALE).then_inc(exp_done, 1)
                    elif part == "values":
                        t = arg
                        act.wait_ge(pv_full, (s - 1) * T + t + 1)
                        if late(s, 2):
                            act.wait_ge(turn_full, s - 1)
                        nc.scalar.copy(oT[:, t], oP[:, t].rearrange("p (h n) -> p h n", h=HG)).then_inc(oT_done, 1)
                    elif part == "turn" and arg == 1:
                        act.wait_ge(attnT_full, s)
                        nc.scalar.copy(attnT[:], bankA[:, 0:D].rearrange("p (t n) -> p t n", t=DT)).then_inc(attnT_done, 1)
                    elif part == "negate":
                        act.wait_ge(maxT_full, s + 1)
                        if late(s, 1):
                            act.wait_ge(neg_in, s * 16)
                        nc.scalar.mul(negT[:], bankC[0:G * HG, 0:P], -1.0).then_inc(neg_done, 1)
                run(act, emit)

            @block.vector
            def _(dve):
                dve.wait_ge(loaded, 16 * LOADS)
                nc.vector.tensor_copy(csel[:], csel_in).then_inc(c_ready, 1)
                nc.vector.tensor_scalar(consts[:], mask_in, 0.0, NEG, ALU.is_equal, ALU.mult).then_inc(cmask, 1)
                dve.wait_ge(cmask, 1)
                nc.vector.tensor_scalar(consts[:], consts[:], cfix[:, 0:1], cfix[:, 1:2], ALU.mult, ALU.add).then_inc(c_ready, 1)

                def emit(s, j, part, arg):
                    g = arg
                    if part == "project":
                        if late(s, 2):
                            dve.wait_ge(kv_full, s - 1)
                        nc.vector.tensor_copy(cst[:, j], k.ctxT[:, :, s]).then_inc(cst_done, 1)
                        dve.wait_ge(q_hi_done, s + 1)
                        if late(s, 1):
                            dve.wait_ge(spread_full, s * T)
                        nc.vector.tensor_tensor(q_part[:, 1], bankA[:, 0:T * P], q_part[:, 0].bitcast(F32),
                                                ALU.subtract).then_inc(q_lo_done, 1)
                        dve.wait_ge(k_hi_done, s + 1)
                        dve.wait_ge(v_done, s + 1)
                        if late(s, 2):
                            dve.wait_ge(s2_full, (s - 1) * G)
                        if not late(s, 1):
                            dve.wait_ge(made, 3)
                        for q in range(4):
                            nc.vector.scalar_tensor_tensor(
                                rows(k_st, q)[:, j, :, q], rows(k_hi, q)[:].bitcast(F32), rows(rowfix, q)[:, 0:1],
                                rows(bankC, q)[:, 0:T * P].rearrange("p (t n) -> p t n", t=T),
                                ALU.mult, ALU.add).then_inc(k_done, 1)
                    elif part == "spread":
                        dve.wait_ge(spread_full, s * T + 2)
                        if late(s, 2):
                            dve.wait_ge(s2_full, (s - 1) * G)
                        nc.vector.tensor_scalar(q_st[:, j, 2:4], s1[:, 1].rearrange("p (h t n) -> p h t n", h=2, t=T),
                                                rowfix[:, 1:2], None, ALU.add).then_inc(q1_done, 1)
                    elif part == "maxima":
                        dve.wait_ge(s1_full, s * G + g + 1)
                        if g == 0 and late(s, 2):
                            dve.wait_ge(maxT_full, s - 1)
                        nc.vector.tensor_reduce(mx[:, j, :, g // T, g % T],
                                                s1[:, g % 2].rearrange("p (q n) -> p q n", q=4), AX,
                                                ALU.max).then_inc(max_done, 1)
                    elif part == "turn" and arg == 0:
                        dve.wait_ge(turn_full, s - 1)
                        for t in range(T):
                            src = (bankA, bankC)[t][:].rearrange("p (h q c) -> p h q c", h=HG, q=4)
                            if late(s, 3):
                                dve.wait_ge(attnT_full, s - 1)
                            nc.vector.reciprocal(rinv[:, t], src[:, :, :, HD]).then_inc(rinv_done, 1)
                            dve.wait_ge(rinv_done, (s - 2) * T + t + 1)
                            nc.vector.tensor_tensor(attn[:, 4 * t:4 * t + 4].rearrange("p q h d -> p h q d"),
                                                    src[:, :, :, 0:HD],
                                                    rinv[:, t].unsqueeze(3).broadcast_to([P, HG, 4, HD]),
                                                    ALU.mult).then_inc(attn_done, 1)
                    elif part == "output":
                        nc.vector.scalar_tensor_tensor(k.x[:, s - 2], bo[:], k.gates[:, 2:3], k.x[:, s - 2],
                                                       ALU.mult, ALU.add).then_inc(bias_done, 1)
                        dve.wait_ge(o_full, s - 1)
                        dve.wait_ge(bias_done, s - 1)
                        nc.vector.scalar_tensor_tensor(k.x[:, s - 2], bankC[:, 0:D], k.gates[:, 2:3], k.x[:, s - 2],
                                                       ALU.mult, ALU.add).then_inc(added, 1)
                        k.after(dve, added, s - 1)
                        nc.vector.bn_stats(k.stats[:, s - 2], k.x[:, s - 2])
                run(dve, emit)


def build(nc, io, stop=None):
    with ExitStack() as ctx:
        k = Kernel(nc, ctx, io)
        phase_setup(k)
        phase_turn(k)
        phase_conv(k)
        phase_residual(k)
        if stop != "conv":
            phase_route(k, 0)
            phase_experts(k, 0)
        if stop is None or stop == "attn":
            phase_turn_rows(k)
            phase_attention(k)
        if stop is None:
            phase_route(k, 1)
            phase_experts(k, 1)
        if stop:
            done = k.sem(ctx, "dbg")
            with nc.Block() as block:
                @block.sync
                def _(sp):
                    sp.dma_start(io["out"].rearrange("b t d -> t b d"), k.x[:]).then_inc(done, 16)
                    sp.wait_ge(done, 16)
            return


def layouts(v):
    import numpy as np
    one = {"x": v["x"], "ctx": v["ctx_2048"],
           "gates": np.stack([v["g_xattn"], v["g_ffn"]], axis=1).reshape(1, 4),
           "skip": v["L0_xattn_D"].reshape(1, HC)}
    taps = np.zeros((HC, P, D), np.float32)
    for p in range(P):
        taps[:, p, p:] = v["L0_xattn_ssm_kernel"][:, :D - p]
    one["taps"] = taps
    r0 = np.concatenate([v["L0_ffn_W_router"].T, v["L0_ffn_W_sgate"].T], axis=1)
    r1 = np.concatenate([v["L1_ffn_router"], np.zeros((D, 1), np.float32)], axis=1)
    one["routers"] = np.stack([r0, r1]).reshape(2, DT, P, E + 1).transpose(2, 0, 1, 3)
    for layer, (sg, sd, eg, ed) in enumerate((
            ("L0_ffn_Ws_gate_up", "L0_ffn_Ws_down", "L0_ffn_We_gate_up", "L0_ffn_We_down"),
            ("L1_ffn_shared_w_up_gate", "L1_ffn_shared_w_down", "L1_ffn_w_up_gate", "L1_ffn_w_down"))):
        shared = v[sg].reshape(D, 2, SHARED, UNIT).transpose(0, 2, 1, 3).reshape(D, SHARED, GU)
        gu = np.concatenate([shared, v[eg].transpose(1, 0, 2)], axis=1).reshape(DT, P, UNITS * GU)
        down = np.concatenate([v[sd], v[ed].reshape(E * UNIT, D), np.zeros((KT * P - HID, D), np.float32)])
        down = down.reshape(KT, P, D).transpose(1, 0, 2).reshape(P, KT * D)
        one[f"w{layer}"] = np.concatenate([gu.transpose(1, 0, 2).reshape(P, DT * UNITS * GU), down], axis=1)
    one["wq"] = v["L1_xattn_w_q"].T.reshape(DT, P, D).transpose(1, 0, 2)
    wk = v["L1_xattn_w_k"].reshape(2, 4, HD, DT, P)
    wk = np.broadcast_to(wk.transpose(4, 3, 0, 1, 2)[:, :, :, :, None], (P, DT, 2, 4, 3, HD))
    wk = np.concatenate([wk, np.zeros((P, DT, 2, 4, 1, HD), np.float32)], axis=4)
    one["wk"] = wk.reshape(P, DT, 2, P)
    one["wv"] = v["L1_xattn_w_v"].T.reshape(DT, P, G * HD).transpose(1, 0, 2)
    one["wo"] = v["L1_xattn_w_o"].T.reshape(DT, P, D).transpose(1, 0, 2)
    one["bo"] = v["L1_xattn_b_o"].reshape(1, D)
    one["mask"] = v["mask_BxS2_if1"].reshape(1, B * P)
    csel = np.zeros((2, 4, SLOT), np.float32)
    csel[0, :, 24] = 1.0
    csel[1, :, 25] = 1.0
    one["csel"] = csel.reshape(2, P)
    one["cfix"] = np.array([[0.0, 1.0], [1.0, 0.0]], np.float32)
    rowfix = np.zeros((4, SLOT, 2), np.float32)
    rowfix[:, 16:24, 0] = -1.0
    rowfix[:, 25, 1] = 1.0
    one["rowfix"] = rowfix.reshape(P, 2)
    spread = np.zeros((4, HG, HD, 2, HG, 4, SLOT), np.float32)
    for slot in range(4):
        for h in range(HG):
            for d in range(HD):
                spread[slot, h, d, 0, h, slot, [d, 16 + d]] = 1.0
                spread[slot, h, d, 1, h, slot, 8 + d] = 1.0
    one["spread"] = spread.reshape(P, 2 * HG * P)
    return one


def kernel(**inputs):
    import numpy as np
    import concourse.bacc as bacc
    from concourse.bass_utils import run_bass_kernel_spmd

    nc = bacc.Bacc("TRN2", target_bir_lowering=False, num_devices=1)
    arrays, io = {}, {}
    for name, a in layouts({n: np.asarray(a) for n, a in inputs.items()}).items():
        a = np.ascontiguousarray(a)
        arrays[f"in_{name}"] = a
        io[name] = nc.dram_tensor(f"in_{name}", a.shape, mybir.dt.from_np(a.dtype), kind="ExternalInput").ap()
    io["out"] = nc.dram_tensor("out_x", (B, P, D), F32, kind="ExternalOutput").ap()
    build(nc, io)
    return run_bass_kernel_spmd(nc, [arrays], core_ids=[0]).results[0]["out_x"]
```

```python
from contextlib import ExitStack

import concourse.bass as bass
from concourse import mybir

F32 = mybir.dt.float32
F32R = mybir.dt.float32r
I32 = mybir.dt.int32
BF16 = mybir.dt.bfloat16
ALU = mybir.AluOpType
ACT = mybir.ActivationFunctionType
AX = mybir.AxisListType.X

P = 128
B = 16
D = 256
DT = D // P
E = 8
UNIT = 176
SHARED = 4
UNITS = SHARED + E
GU = 2 * UNIT
HID = SHARED * UNIT
KT = (HID + P - 1) // P
ET = (UNIT + P - 1) // P
WCOLS = DT * UNITS * GU + KT * D
ECOLS = E * ET * D
CHOICES = 2
GT = 4
GROUPS = (CHOICES * B + E) // GT
TILES = GROUPS * GT
NUMBERS = B + E * E + TILES + GT
WCHUNK = WCOLS // B
CAPACITY = 640
HC = 16
DC = 8
G, HG, HD = 8, 4, 8
SLOT = 32
EPS = 1e-5
NEG = -1.0e30


def steps(eng, body, first, end, peel=2):
    for s in range(first, first + peel):
        body(s, s % 2)
    pairs = (end - first - peel) // 2 * 2
    if pairs:
        with eng.Fori(0, pairs // 2) as pair:
            for j in range(2):
                body(pair * 2 + (first + peel + j), (first + peel + j) % 2)
    for s in range(first + peel + pairs, end):
        body(s, s % 2)


def quads(eng, body):
    for b in range(4):
        body(b, b)
    with eng.Fori(0, B // 4 - 1) as quad:
        for j in range(4):
            body(quad * 4 + (4 + j), j)


def late(step, n):
    return not isinstance(step, int) or step >= n


class Kernel:

    def __init__(self, nc, ctx, io):
        self.nc, self.io = nc, io
        self.sb_in(ctx)

    def sb(self, ctx, name, shape, dt=F32):
        return ctx.enter_context(self.nc.sbuf_tensor(name, shape, dt))

    def ps(self, ctx, name, shape, dt=F32):
        return ctx.enter_context(self.nc.psum_tensor(name, shape, dt))

    def sem(self, ctx, name):
        return ctx.enter_context(self.nc.semaphore(name))

    def after(self, eng, sem, value):
        eng.wait_ge(self.begun, 1)
        eng.wait_ge(sem, value)

    def sb_in(self, ctx):
        self.x = self.sb(ctx, "x_res", [P, B, D])
        self.ctxT = self.sb(ctx, "ctxT", [P, DT, B, P])
        self.actT = self.sb(ctx, "actT", [P, DT, B, P])
        self.w_hi = self.sb(ctx, "w_hi", [P, WCOLS], F32R)
        self.w_lo = self.sb(ctx, "w_lo", [P, WCOLS], F32R)
        self.ident = self.sb(ctx, "ident", [P, P])
        self.gates = self.sb(ctx, "gates", [P, 4])
        self.stats = self.sb(ctx, "stats", [P, B, 6])
        self.mean = self.sb(ctx, "mean", [P, B])
        self.rstd = self.sb(ctx, "rstd", [P, B])
        self.w_shared = self.sb(ctx, "w_shared", [P, B])
        self.numbers = self.sb(ctx, "numbers", [P, NUMBERS])
        self.routed = self.nc.dram_tensor("routed_rows", (TILES * P, D), F32).ap()
        self.returned = self.nc.dram_tensor("returned_rows", (TILES * P, D), F32).ap()
        self.begun = self.sem(ctx, "begun")
        self.cleared = self.sem(ctx, "cleared")
        self.w_router = self.sb(ctx, "w_router", [P, 2, DT, E + 1])


class WeightSplit:

    def __init__(self, k, layer, ctx, halves):
        self.k, self.nc = k, k.nc
        self.halves = halves
        self.raw = k.sb(ctx, f"raw{layer}", [P, halves, WCHUNK])
        self.raw_in = [k.sem(ctx, f"raw_in{layer}_{j}") for j in range(2)]
        self.hi_done, self.lo_done = k.sem(ctx, f"hi_done{layer}"), k.sem(ctx, f"lo_done{layer}")
        self.src = k.io[f"w{layer}"]

    def load(self, eng, c, j):
        if late(c, self.halves):
            eng.wait_ge(self.lo_done, c + 1 - self.halves)
        eng.dma_start(self.raw[:, j % self.halves], self.src[:, bass.ds(c * WCHUNK, WCHUNK)]).then_inc(self.raw_in[j], 16)

    def hi(self, eng, copy, c, j):
        eng.wait_ge(self.raw_in[j], 8 * (c - j) + 16)
        copy(self.k.w_hi[:, bass.ds(c * WCHUNK, WCHUNK)], self.raw[:, j % self.halves]).then_inc(self.hi_done, 1)

    def lo(self, eng, c, j):
        cols = bass.ds(c * WCHUNK, WCHUNK)
        eng.wait_ge(self.hi_done, c + 1)
        eng.tensor_tensor(self.k.w_lo[:, cols], self.raw[:, j % self.halves], self.k.w_hi[:, cols].bitcast(F32),
                          ALU.subtract).then_inc(self.lo_done, 1)


def norm_coefficients(k, ctx, tag):
    nc = k.nc
    coef = k.sem(ctx, f"coef_{tag}")
    dist = k.sb(ctx, f"dist{tag}", [P, B])
    var = k.sb(ctx, f"var{tag}", [P, B])
    expo = k.sb(ctx, f"expo{tag}", [P, B])

    def emit(pool):
        done = [0]

        def link(ins):
            done[0] += 1
            ins.then_inc(coef, 1)
            pool.wait_ge(coef, done[0])
        link(nc.gpsimd.memset(expo[:], -0.5))
        link(nc.gpsimd.tensor_tensor(k.mean[:], k.stats[:, :, 1], k.stats[:, :, 4], ALU.add))
        link(nc.gpsimd.tensor_scalar(k.mean[:], k.mean[:], 0.5, 0.0, ALU.mult, ALU.add))
        link(nc.gpsimd.tensor_tensor(dist[:], k.mean[:], k.stats[:, :, 1], ALU.subtract))
        link(nc.gpsimd.tensor_tensor(dist[:], dist[:], dist[:], ALU.mult))
        link(nc.gpsimd.tensor_tensor(var[:], k.stats[:, :, 2], k.stats[:, :, 5], ALU.add))
        link(nc.gpsimd.tensor_scalar(var[:], var[:], 1.0 / D, EPS, ALU.mult, ALU.add))
        link(nc.gpsimd.tensor_tensor(var[:], var[:], dist[:], ALU.add))
        link(nc.gpsimd.tensor_tensor(k.rstd[:], var[:], expo[:], ALU.pow))
    return emit, coef


class NormTurn:

    def __init__(self, k, ctx, tag):
        self.k, self.nc = k, k.nc
        self.xn = k.sb(ctx, f"xn{tag}", [P, 4, D])
        self.turned = k.ps(ctx, f"turned{tag}", [P, 4, 512])
        self.coefficients, self.coef = norm_coefficients(k, ctx, tag)
        self.normed, self.turned_full, self.copied = (k.sem(ctx, n + tag) for n in ("normed", "turned_full", "copied"))

    def normalise(self, dve, kept=False):
        k = self.k
        dve.wait_ge(self.coef, 9)

        def body(b, j):
            if late(b, 4):
                dve.wait_ge(self.turned_full, b - 3)
                if kept:
                    dve.wait_ge(self.copied, b - 3)
            self.nc.vector.tensor_scalar(self.xn[:, j], k.x[:, b], k.mean[:, bass.ds(b, 1)], k.rstd[:, bass.ds(b, 1)],
                                         ALU.subtract, ALU.mult).then_inc(self.normed, 1)
        quads(dve, body)

    def turn_one(self, pe, b, j):
        pe.wait_ge(self.normed, b + 1)
        if late(b, 4):
            pe.wait_ge(self.copied, b - 3)
        for t in range(DT):
            mm = pe.transpose(self.turned[:, j, t * P:(t + 1) * P], self.xn[:, j, t * P:(t + 1) * P], self.k.ident[:])
        mm.then_inc(self.turned_full, 1)

    def turn(self, pe):
        quads(pe, lambda b, j: self.turn_one(pe, b, j))

    def copy_one(self, act, b, j):
        act.wait_ge(self.turned_full, b + 1)
        self.nc.scalar.copy(self.k.actT[:, :, b],
                            self.turned[:, j, 0:D].rearrange("p (t n) -> p t n", t=DT)).then_inc(self.copied, 1)

    def copy(self, act):
        quads(act, lambda b, j: self.copy_one(act, b, j))


def phase_start(k):
    nc, io = k.nc, k.io
    with ExitStack() as ctx:
        nt = NormTurn(k, ctx, "_a")
        raw_gates = k.sb(ctx, "raw_gates", [P, 4])
        cx = k.sb(ctx, "cx", [P, 2, 4, D])
        cx_turned = k.ps(ctx, "cx_turned", [P, 4, 512])
        small_in, made, stat_done = (k.sem(ctx, n) for n in ("small_in", "made", "stat_done"))
        x_in = [k.sem(ctx, f"x_in{j}") for j in range(2)]
        cx_in = [k.sem(ctx, f"cx_in{j}") for j in range(2)]
        cx_full, cx_copied = k.sem(ctx, "cx_full"), k.sem(ctx, "cx_copied")
        x_rows = io["x"].rearrange("b t d -> t b d")
        cx_rows = io["ctx"].rearrange("b t d -> t b d")
        with nc.Block() as block:
            @block.sync
            def _(sp):
                for q in range(2):
                    sp.dma_start(k.x[:, 8 * q:8 * q + 8], x_rows[:, 8 * q:8 * q + 8]).then_inc(x_in[q], 16)
                for q in range(4):
                    if q >= 2:
                        sp.wait_ge(cx_full, 4 * (q - 1))
                    sp.dma_start(cx[:, q % 2], cx_rows[:, 4 * q:4 * q + 4]).then_inc(cx_in[q % 2], 16)

            @block.gpsimd
            def _(pool):
                nc.gpsimd.memset(k.ident[:], 0.0).then_inc(made, 1)
                pool.wait_ge(made, 1)
                nc.gpsimd.affine_select(out=k.ident[:], in_=k.ident[:], compare_op=ALU.not_equal, fill=1.0,
                                        base=0, pattern=[[-1, P]], channel_multiplier=1).then_inc(k.begun, 1)
                pool.wait_ge(stat_done, B)
                nt.coefficients(pool)

            @block.tensor
            def _(pe):
                pe.wait_ge(k.begun, 1)

                def body(b, j, half, come):
                    if j == 0:
                        pe.wait_ge(cx_in[half], come)
                    if late(b, 4):
                        pe.wait_ge(cx_copied, b - 3)
                    for t in range(DT):
                        mm = pe.transpose(cx_turned[:, j, t * P:(t + 1) * P], cx[:, half, j, t * P:(t + 1) * P], k.ident[:])
                    mm.then_inc(cx_full, 1)
                for q in range(4):
                    for j in range(4):
                        body(4 * q + j, j, q % 2, 16 * (q // 2 + 1))
                nt.turn(pe)

            @block.scalar
            def _(act):
                act.dma_start(raw_gates[:], bass.AP(io["gates"].tensor, 0, [[0, P], [1, 4]])).then_inc(small_in, 16)
                act.dma_start(k.w_router[:], io["routers"]).then_inc(small_in, 16)
                act.dma_start(k.numbers[:], bass.AP(io["numbers"].tensor, 0, [[0, P], [1, NUMBERS]])).then_inc(small_in, 16)
                act.wait_ge(small_in, 48)
                nc.scalar.activation(k.gates[:], raw_gates[:], ACT.Tanh)

                def body(b, j):
                    act.wait_ge(cx_full, b + 1)
                    nc.scalar.copy(k.ctxT[:, :, b], cx_turned[:, j, 0:D].rearrange("p (t n) -> p t n", t=DT)).then_inc(cx_copied, 1)
                quads(act, body)
                nt.copy(act)

            @block.vector
            def _(dve):
                for q in range(2):
                    dve.wait_ge(x_in[q], 16)
                    for b in range(8 * q, 8 * q + 8):
                        nc.vector.bn_stats(k.stats[:, b], k.x[:, b]).then_inc(stat_done, 1)
                nt.normalise(dve)


def phase_conv(k):
    nc, io = k.nc, k.io
    W = B * DC * DC
    with ExitStack() as ctx:
        kv = k.sb(ctx, "kv", [P, 2, DT, W])
        toep = k.sb(ctx, "toep", [P, 2, D])
        skip = k.sb(ctx, "skip", [P, HC])
        diag = k.sb(ctx, "diag", [P, P])
        diag_done = k.sem(ctx, "diag_done")
        prod = k.sb(ctx, "prod", [P, 2, W])
        conv = k.ps(ctx, "conv", [P, 4, W])
        toep_in = [k.sem(ctx, f"toep_in{j}") for j in range(2)]
        skip_in, toep_full, kv_full, conv_full = (k.sem(ctx, n) for n in ("skip_in", "toep_full", "kv_full", "conv_full"))
        prod_done, summed = k.sem(ctx, "prod_done"), k.sem(ctx, "summed")
        weights = WeightSplit(k, 0, ctx, 2)
        ZCOLS = TILES * D // HC
        zero = k.sb(ctx, "zero", [P, ZCOLS])
        zeroed = k.sem(ctx, "zeroed")

        cleared_rows = k.routed.rearrange("(p r) d -> p (r d)", p=P)

        def head(buf, t, h):
            return buf[:, t, :, bass.ds(h * DC, DC)]

        with nc.Block() as block:
            @block.sync
            def _(sp):
                sp.dma_start(skip[:], bass.AP(io["skip"].tensor, 0, [[0, P], [1, HC]])).then_inc(skip_in, 16)

                def body(h, j):
                    if late(h, 2):
                        sp.wait_ge(conv_full, 2 * h - 2)
                    sp.dma_start(toep[:, j], io["taps"][h]).then_inc(toep_in[j], 16)
                    weights.load(sp, h, j)
                    if not late(h, 1):
                        sp.wait_ge(zeroed, 1)
                    sp.dma_start(cleared_rows[:, bass.ds(h * ZCOLS, ZCOLS)], zero[:]).then_inc(k.cleared, 16)
                steps(sp, body, 0, HC)
                sp.wait_ge(k.cleared, 16 * HC)

            @block.gpsimd
            def _(pool):
                nc.gpsimd.memset(zero[:], 0.0).then_inc(zeroed, 1)
                pool.wait_ge(skip_in, 16)

                def body(h, j):
                    if late(h, 2):
                        pool.wait_ge(conv_full, 2 * h - 2)
                    for t in range(DT):
                        c = head(k.ctxT, t, h)
                        nc.gpsimd.tensor_tensor(
                            kv[:, j, t].rearrange("p (b j i) -> p b j i", j=DC, i=DC),
                            c.unsqueeze(3).broadcast_to([P, B, DC, DC]),
                            c.unsqueeze(2).broadcast_to([P, B, DC, DC]), ALU.mult).then_inc(kv_full, 1)
                    if late(h, 1):
                        pool.wait_ge(toep_full, h)
                    nc.gpsimd.tensor_tensor(diag[:], k.ident[:], skip[:, bass.ds(h, 1)].broadcast_to([P, P]),
                                            ALU.mult).then_inc(diag_done, 1)
                    pool.wait_ge(diag_done, h + 1)
                    pool.wait_ge(toep_in[j], 8 * (h - j) + 16)
                    nc.gpsimd.tensor_tensor(toep[:, j, 0:P], toep[:, j, 0:P], diag[:], ALU.add).then_inc(toep_full, 1)
                steps(pool, body, 0, HC)

            @block.tensor
            def _(pe):
                def body(h, j):
                    pe.wait_ge(toep_full, h + 1)
                    pe.wait_ge(kv_full, 2 * h + 2)
                    for t in range(DT):
                        bank = 2 * j + t
                        if late(h, 2):
                            pe.wait_ge(prod_done, 2 * h - 3 + t)
                        for half in range(2):
                            cols = slice(half * (W // 2), (half + 1) * (W // 2))
                            for s in range(t + 1):
                                mm = pe.matmul(conv[:, bank, cols], toep[:, j, (t - s) * P:(t - s + 1) * P],
                                               kv[:, j, s, cols], start=(s == 0), stop=(s == t))
                        mm.then_inc(conv_full, 1)
                steps(pe, body, 0, HC)

            @block.vector
            def _(dve):
                def body(h, j):
                    for t in range(DT):
                        dve.wait_ge(conv_full, 2 * h + t + 1)
                        if late(h, 1):
                            dve.wait_ge(summed, 2 * h - 1 + t)
                        nc.vector.tensor_tensor(
                            prod[:, t].rearrange("p (b j i) -> p b j i", j=DC, i=DC),
                            conv[:, 2 * j + t].rearrange("p (b j i) -> p b j i", j=DC, i=DC),
                            head(k.actT, t, h).unsqueeze(2).broadcast_to([P, B, DC, DC]), ALU.mult).then_inc(prod_done, 1)
                    for t in range(DT):
                        k.after(dve, prod_done, 2 * h + t + 1)
                        nc.vector.tensor_reduce(head(k.actT, t, h), prod[:, t].rearrange("p (b j i) -> p b j i", j=DC, i=DC),
                                                AX, ALU.add).then_inc(summed, 1)
                    weights.lo(dve, h, j)
                steps(dve, body, 0, HC)

            @block.scalar
            def _(act):
                def body(h, j):
                    weights.hi(act, nc.scalar.copy, h, j)
                steps(act, body, 0, HC)


def phase_residual(k):
    nc = k.nc
    with ExitStack() as ctx:
        stage = k.sb(ctx, "stage_c", [P, 4, DT, P])
        back = k.ps(ctx, "back_c", [P, 4, 512])
        staged, turned, added = (k.sem(ctx, n) for n in ("staged_c", "turned_c", "added_c"))
        with nc.Block() as block:
            @block.scalar
            def _(act):
                def body(b, j):
                    if late(b, 4):
                        act.wait_ge(turned, b - 3)
                    nc.scalar.copy(stage[:, j], k.actT[:, :, b]).then_inc(staged, 1)
                quads(act, body)

            @block.tensor
            def _(pe):
                def body(b, j):
                    pe.wait_ge(staged, b + 1)
                    if late(b, 4):
                        pe.wait_ge(added, b - 3)
                    for t in range(DT):
                        mm = pe.transpose(back[:, j, t * P:(t + 1) * P], stage[:, j, t], k.ident[:])
                    mm.then_inc(turned, 1)
                quads(pe, body)

            @block.vector
            def _(dve):
                def body(b, j):
                    dve.wait_ge(turned, b + 1)
                    nc.vector.scalar_tensor_tensor(k.x[:, b], back[:, j, 0:D], k.gates[:, 0:1], k.x[:, b],
                                                   ALU.mult, ALU.add).then_inc(added, 1)
                    if j == 3:
                        for e in range(4):
                            k.after(dve, added, b - 2 + e)
                            nc.vector.bn_stats(k.stats[:, b - 3 + e], k.x[:, b - 3 + e])
                quads(dve, body)


class Mixture:

    def __init__(self, k, layer, ctx):
        self.spare = {}
        self.rows = k.sb(ctx, f"rows{layer}", [P, B, D])
        self.down_hi = k.sb(ctx, f"down_hi{layer}", [P, ECOLS], F32R)
        self.down_lo = k.sb(ctx, f"down_lo{layer}", [P, ECOLS], F32R)
        self.slot = k.sb(ctx, f"slot{layer}", [P, CHOICES, B], I32)
        self.share = k.sb(ctx, f"share{layer}", [P, CHOICES, B])
        self.owner = k.sb(ctx, f"owner{layer}", [P, GROUPS], I32)
        self.working = ExitStack()
        k.sb(self.working, f"first_tiles{layer}", [P, 2 * DT * P])
        spare = k.sb(self.working, f"spare{layer}", [P, 2 * (GT - 1) * DT * P])
        for name, rows, cols in (("one1", B, E), ("one2", B, E), ("weight", B, E), ("before", B + 1, E),
                                 ("slotf", CHOICES, B), ("ownerf", GROUPS, GT), ("packed", GROUPS, 1),
                                 ("tiles", E, 1), ("end", E, 1), ("start", E, 1), ("mine", B, E), ("part", B, E),
                                 ("place", B, E), ("over", E, B), ("upto", E, E), ("past", TILES, E)):
            view = spare[:, 0:rows * cols]
            self.spare[name] = view if cols == 1 else view.rearrange("p (r c) -> p r c", r=rows)
            spare = spare[:, rows * cols:]


def phase_mixture(k, layer):
    with ExitStack() as ctx:
        m = Mixture(k, layer, ctx)
        phase_route(k, layer, m)
        m.working.close()
        phase_experts(k, layer, m)


def phase_route(k, layer, m):
    nc, io = k.nc, k.io
    DCHUNK = ECOLS // E
    BY_POOL = 5
    cols = E + 1 if layer == 0 else E
    with ExitStack() as ctx:
        nt = NormTurn(k, ctx, f"_r{layer}")
        raw = k.sb(ctx, f"raw_r{layer}", [P, 3, DCHUNK])
        logT = k.sb(ctx, f"logT{layer}", [E + 1, B * P])
        lg = k.sb(ctx, f"lg{layer}", [P, B, E + 1])
        rev = k.sb(ctx, f"rev{layer}", [P, B, E])
        tmp = {n: k.sb(ctx, f"{n}{layer}", [P, B, E]) for n in ("eq", "rank", "lg2")}
        tmp.update(one1=m.spare["one1"], one2=m.spare["one2"], ex=m.spare["weight"])
        row = {n: k.sb(ctx, f"{n}_row{layer}", [P, B]) for n in ("m1", "m2", "r1", "r2", "gap", "e2", "den", "inv")}
        gate9 = k.sb(ctx, f"gate9{layer}", [P, B])
        sel_pad = k.sb(ctx, f"sel_pad{layer}", [P, 2 * B, E], BF16)
        sel16 = sel_pad[:, B:]
        ones16 = k.sb(ctx, f"ones16{layer}", [P, P], BF16)
        tri16 = k.sb(ctx, f"tri16{layer}", [P, P], BF16)
        logP = k.ps(ctx, f"logP{layer}", [P, 2, 512])
        lgP = k.ps(ctx, f"lgP{layer}", [P, B * (E + 1)])
        posP = k.ps(ctx, f"posP{layer}", [P, B + 1, E])
        logits_full, logits_out, back_full, chain = (k.sem(ctx, f"{n}_r{layer}") for n in
                                                     ("logits_full", "logits_out", "back_full", "chain"))
        consts, ex_in, ex_out, pos_in, pos_out = (k.sem(ctx, f"{n}_r{layer}") for n in
                                                  ("consts", "ex_in", "ex_out", "pos_in", "pos_out"))
        raw_in = [k.sem(ctx, f"down_in{j}_r{layer}") for j in range(3)]
        down_hi_done, down_lo_done = k.sem(ctx, f"down_hi_r{layer}"), k.sem(ctx, f"down_lo_r{layer}")
        with nc.Block() as block:
            @block.sync
            def _(sp):
                for c in range(E):
                    if c >= 3:
                        sp.wait_ge(down_lo_done, c - 2)
                    sp.dma_start(raw[:, c % 3], io[f"down{layer}"][:, c * DCHUNK:(c + 1) * DCHUNK]).then_inc(raw_in[c % 3], 16)

            @block.gpsimd
            def _(pool):
                nt.coefficients(pool)

                for e in range(E):
                    nc.gpsimd.memset(rev[:, :, e], float(E - e)).then_inc(consts, 1)
                nc.gpsimd.memset(sel_pad[:, 0:B], 0.0).then_inc(consts, 1)
                nc.gpsimd.memset(ones16[:], 1.0).then_inc(consts, 1)
                pool.wait_ge(consts, E + 2)
                nc.gpsimd.affine_select(out=tri16[:], in_=ones16[:], compare_op=ALU.is_gt, fill=0.0,
                                        base=0, pattern=[[1, P]], channel_multiplier=-1).then_inc(consts, 1)
                for c in range(E):
                    cols = slice(c * DCHUNK, (c + 1) * DCHUNK)
                    pool.wait_ge(raw_in[c % 3], 16 * (c // 3 + 1))
                    if c < BY_POOL:
                        nc.gpsimd.tensor_copy(m.down_hi[:, cols], raw[:, c % 3]).then_inc(down_hi_done, 1)
                    pool.wait_ge(down_hi_done, c + 1)
                    nc.gpsimd.tensor_tensor(m.down_lo[:, cols], raw[:, c % 3], m.down_hi[:, cols].bitcast(F32),
                                            ALU.subtract).then_inc(down_lo_done, 1)

            @block.vector
            def _(dve):
                nt.normalise(dve, kept=True)
                count = [0]

                def link(ins):
                    count[0] += 1
                    ins.then_inc(chain, 1)
                    dve.wait_ge(chain, count[0])

                def bc(r):
                    return r[:].unsqueeze(2).broadcast_to([P, B, E])

                def best(logits, m, r, one):
                    link(nc.vector.tensor_reduce(row[m][:], logits, AX, ALU.max))
                    link(nc.vector.tensor_tensor(tmp["eq"][:], logits, bc(row[m]), ALU.is_equal))
                    link(nc.vector.tensor_tensor(tmp["rank"][:], tmp["eq"][:], rev[:], ALU.mult))
                    link(nc.vector.tensor_reduce(row[r][:], tmp["rank"][:], AX, ALU.max))
                    link(nc.vector.tensor_tensor(tmp[one][:], tmp["rank"][:], bc(row[r]), ALU.is_equal))

                dve.wait_ge(back_full, 1)
                dve.wait_ge(consts, E + 3)
                link(nc.vector.tensor_copy(lg[:, :, 0:cols], lgP[:, 0:B * cols].rearrange("p (b e) -> p b e", e=cols)))
                logits = lg[:, :, 0:E]
                best(logits, "m1", "r1", "one1")
                link(nc.vector.scalar_tensor_tensor(tmp["lg2"][:], tmp["one1"][:], NEG, logits, ALU.mult, ALU.add))
                best(tmp["lg2"][:], "m2", "r2", "one2")
                nc.vector.tensor_tensor(sel16, tmp["one1"][:], tmp["one2"][:], ALU.add).then_inc(pos_in, 1)
                if layer == 0:
                    link(nc.vector.tensor_tensor(tmp["ex"][:], logits, bc(row["m1"]), ALU.subtract))
                    nc.vector.tensor_copy(gate9[:], lg[:, :, E]).then_inc(ex_in, 1)
                    dve.wait_ge(ex_out, 2)
                    link(nc.vector.tensor_reduce(row["den"][:], tmp["ex"][:], AX, ALU.add))
                    link(nc.vector.reciprocal(row["inv"][:], row["den"][:]))
                    link(nc.vector.tensor_tensor(tmp["ex"][:], tmp["ex"][:], bc(row["inv"]), ALU.mult))
                    link(nc.vector.tensor_scalar(gate9[:], gate9[:], 1.0, None, ALU.add))
                    link(nc.vector.reciprocal(k.w_shared[:], gate9[:]))
                else:
                    nc.vector.tensor_tensor(row["gap"][:], row["m2"][:], row["m1"][:], ALU.subtract).then_inc(ex_in, 1)
                    link(nc.vector.memset(k.w_shared[:], 1.0))
                    dve.wait_ge(ex_out, 1)
                    link(nc.vector.tensor_scalar(row["den"][:], row["e2"][:], 1.0, None, ALU.add))
                    link(nc.vector.reciprocal(row["inv"][:], row["den"][:]))
                    link(nc.vector.tensor_tensor(tmp["ex"][:], tmp["one2"][:], bc(row["e2"]), ALU.mult))
                    link(nc.vector.tensor_tensor(tmp["ex"][:], tmp["ex"][:], tmp["one1"][:], ALU.add))
                    link(nc.vector.tensor_tensor(tmp["ex"][:], tmp["ex"][:], bc(row["inv"]), ALU.mult))

            @block.scalar
            def _(act):
                for c in range(5):
                    for j in range(4 if c < 4 else 0):
                        act.wait_ge(nt.normed, 4 * c + j + 1)
                        nc.scalar.copy(m.rows[:, 4 * c + j], nt.xn[:, j])
                        nt.copy_one(act, 4 * c + j, j)
                    if c >= 1:
                        act.wait_ge(logits_full, c)
                        nc.scalar.copy(logT[0:cols, (c - 1) * 512:c * 512], logP[0:cols, (c - 1) % 2]).then_inc(logits_out, 1)
                for c in range(BY_POOL, E):
                    act.wait_ge(down_hi_done, c)
                    act.wait_ge(raw_in[c % 3], 16 * (c // 3 + 1))
                    nc.scalar.copy(m.down_hi[:, c * DCHUNK:(c + 1) * DCHUNK], raw[:, c % 3]).then_inc(down_hi_done, 1)
                act.wait_ge(ex_in, 1)
                if layer == 0:
                    nc.scalar.activation(tmp["ex"][:], tmp["ex"][:], ACT.Exp).then_inc(ex_out, 1)
                    nc.scalar.activation(gate9[:], gate9[:], ACT.Exp, scale=-1.0).then_inc(ex_out, 1)
                else:
                    nc.scalar.activation(row["e2"][:], row["gap"][:], ACT.Exp).then_inc(ex_out, 1)
                act.wait_ge(pos_out, 1)
                nc.scalar.copy(m.spare["before"], posP[:])

            @block.tensor
            def _(pe):
                for c in range(5):
                    for j in range(4 if c < 4 else 0):
                        nt.turn_one(pe, 4 * c + j, j)
                    if c >= 1:
                        pe.wait_ge(nt.copied, 4 * c)
                        if c >= 3:
                            pe.wait_ge(logits_out, c - 2)
                        for t in range(DT):
                            mm = pe.matmul(logP[0:cols, (c - 1) % 2], k.w_router[:, layer, t, 0:cols],
                                           k.actT[:, t, 4 * c - 4:4 * c], start=(t == 0), stop=(t == DT - 1))
                        mm.then_inc(logits_full, 1)
                pe.wait_ge(logits_out, 4)
                for b in range(B):
                    mm = pe.transpose(lgP[:, b * cols:(b + 1) * cols], logT[0:cols, b * P:(b + 1) * P],
                                      k.ident[0:cols, 0:cols])
                mm.then_inc(back_full, 1)
                pe.wait_ge(pos_in, 1)
                pe.wait_ge(consts, E + 3)
                for back in range(1, B + 1):
                    pe.matmul(posP[:], ones16[:], sel_pad[:, B - back:2 * B + 1 - back], start=(back == 1), stop=False)
                mm = pe.matmul(posP[:, 0:B], tri16[:], sel16, start=False, stop=True)
                mm.then_inc(pos_out, 1)


def phase_experts(k, layer, m):
    nc, io = k.nc, k.io
    GW = DT * UNITS * GU
    ONE, MANY = "one element", "many tiles"
    FIRST = B // 2
    END_MANY = FIRST + GROUPS
    STEPS = B + GROUPS
    RETURN = END_MANY + 2
    PAIR = 2
    with ExitStack() as ctx:
        t_ = f"_e{layer}"
        xs_hi = k.sb(ctx, "xs_hi" + t_, [P, GT, 2, DT, P], F32R)
        xs_lo = k.sb(ctx, "xs_lo" + t_, [P, GT, 2, DT, P], F32R)
        silu = k.sb(ctx, "silu" + t_, [P, 2, UNIT])
        h = k.sb(ctx, "h" + t_, [P, 2, HID])
        hT_hi = k.sb(ctx, "hT_hi" + t_, [P, 2, 4, P], F32R)
        hT_lo = k.sb(ctx, "hT_lo" + t_, [P, 2, 4, P], F32R)
        gu = k.ps(ctx, "gu" + t_, [P, GT, 512])
        turned = k.ps(ctx, "turned" + t_, [P, 2, 512])
        out = k.ps(ctx, "out" + t_, [P, 2, 512])
        (xs_hi_done, xs_done, gu_full, silu_done, h_done, turned_full, hi_done, hT_done, down_full,
         added, rows_turned, returned_out, sent, mixed, stored, placing, sharing) = (k.sem(ctx, n + t_) for n in (
             "xs_hi_done", "xs_done", "gu_full", "silu_done", "h_done", "turned_full", "hi_done",
             "hT_done", "down_full", "added", "rows_turned", "returned_out", "sent", "mixed", "stored", "placing", "sharing"))
        rows_in = [k.sem(ctx, f"rows_in{j}{t_}") for j in range(2)]
        rows_out = [k.sem(ctx, f"rows_out{j}{t_}") for j in range(2)]
        back_in = [k.sem(ctx, f"back_in{j}{t_}") for j in range(2)]
        placed = []
        gate = k.gates[:, 2 * layer + 1:2 * layer + 2]
        thresholds = k.numbers[:, 0:B]
        triangle = k.numbers[:, B:B + E * E].rearrange("p (a b) -> p a b", a=E)
        tile_number = k.numbers[:, B + E * E:B + E * E + TILES]
        powers = k.numbers[:, B + E * E + TILES:]

        def row_tiles(j):
            return m.rows[:, GT * j:GT * (j + 1)]

        def out_tiles(j):
            return m.rows[:, GT * (2 + j):GT * (3 + j)]

        def group_in_dram(buf, g):
            return buf[bass.ds(g * (GT * P), GT * P)].rearrange("(t p) d -> p t d", p=P)

        def hidden(kind, g):
            if kind == ONE:
                return [(min(c * P, HID - P), 0, c) for c in range(4 * g, min(4 * g + 4, KT))]
            return [(u * UNIT + min(c * P, UNIT - P), u, c) for u in (2 * g, 2 * g + 1) for c in range(ET)]

        def run(eng, emit):
            def pairs(first, n, skip, kind):
                with eng.Fori(0, n) as pair:
                    for j in range(2):
                        emit(pair * 2 + (first + j), j, skip, kind, kind, kind)
            emit(0, 0, 0, ONE, None, ONE)
            emit(1, 1, 0, ONE, ONE, ONE)
            pairs(2, FIRST // 2 - 2, 0, ONE)
            emit(FIRST - 2, 0, 0, ONE, ONE, ONE)
            emit(FIRST - 1, 1, 0, ONE, ONE, MANY)
            emit(FIRST, 0, 0, MANY, ONE, MANY)
            emit(FIRST + 1, 1, 0, MANY, MANY, MANY)
            pairs(FIRST + 2, GROUPS // 2 - 2, 0, MANY)
            emit(END_MANY - 2, 0, 0, MANY, MANY, MANY)
            emit(END_MANY - 1, 1, GROUPS, MANY, MANY, ONE)
            emit(END_MANY, 0, GROUPS, ONE, MANY, ONE)
            emit(END_MANY + 1, 1, GROUPS, ONE, ONE, ONE)
            pairs(END_MANY + 2, (STEPS - END_MANY) // 2 - 2, GROUPS, ONE)
            emit(STEPS - 2, 0, GROUPS, ONE, ONE, ONE)
            emit(STEPS - 1, 1, GROUPS, ONE, ONE, None)
            emit(STEPS, 0, GROUPS, None, ONE, None)

        def order(front, back, after, front_, turn_, down_, split_, rows_, out_):
            for part, arg in (("front", 0), ("turn", 0), ("front", 1), ("turn", 1), ("split", 0), ("front", 2),
                              ("down", 0), ("rows", 0), ("out", 0), ("front", 3), ("down", 1), ("rows", 1), ("out", 1)):
                fn, on = {"front": (front_, front), "turn": (turn_, back), "down": (down_, back),
                          "split": (split_, after == ONE), "rows": (rows_, after == MANY),
                          "out": (out_, back == MANY)}[part]
                if fn and on:
                    fn(arg)

        with nc.Block() as block:
            @block.gpsimd
            def _(pool):
                count = [0]

                def link(ins):
                    count[0] += 1
                    ins.then_inc(placing, 1)
                    pool.wait_ge(placing, count[0])

                def total(dst, parts, n):
                    while n > 2:
                        n //= 2
                        link(nc.gpsimd.tensor_tensor(parts[:, :, 0:n], parts[:, :, 0:n], parts[:, :, n:2 * n], ALU.add))
                    link(nc.gpsimd.tensor_tensor(dst, parts[:, :, 0], parts[:, :, 1], ALU.add))
                t = m.spare
                link(nc.gpsimd.tensor_tensor(t["over"], t["before"][:, B].unsqueeze(2).broadcast_to([P, E, B]),
                                             thresholds.unsqueeze(1).broadcast_to([P, E, B]), ALU.subtract))
                link(nc.gpsimd.tensor_scalar(t["over"], t["over"], 0.0, 0.0, ALU.is_gt, ALU.add))
                total(t["tiles"], t["over"], B)
                link(nc.gpsimd.tensor_tensor(t["upto"], t["tiles"].unsqueeze(1).broadcast_to([P, E, E]), triangle, ALU.mult))
                total(t["end"], t["upto"], E)
                link(nc.gpsimd.tensor_tensor(t["start"], t["end"], t["tiles"], ALU.subtract))
                link(nc.gpsimd.tensor_scalar(t["start"], t["start"], float(P), 0.0, ALU.mult, ALU.add))
                link(nc.gpsimd.tensor_tensor(t["place"], t["before"][:, 0:B],
                                             t["start"].unsqueeze(1).broadcast_to([P, B, E]), ALU.add))
                for c, one in enumerate(("one1", "one2")):
                    link(nc.gpsimd.tensor_tensor(t["mine"], t[one], t["place"], ALU.mult))
                    total(t["slotf"][:, c], t["mine"], E)
                link(nc.gpsimd.tensor_copy(m.slot[:], t["slotf"]))
                pool.wait_ge(k.cleared, 16 * HC)
                for b in range(B):
                    for c in range(CHOICES):
                        nc.gpsimd.indirect_dma_start(
                            k.routed, bass.IndirectOffsetOnAxis(ap=m.slot[:, c, b:b + 1], axis=0),
                            m.rows[:, b], None).then_inc(sent, 16)
                digits = t["ownerf"]
                link(nc.gpsimd.tensor_tensor(t["past"], tile_number.unsqueeze(2).broadcast_to([P, TILES, E]),
                                             t["end"].unsqueeze(1).broadcast_to([P, TILES, E]), ALU.subtract))
                link(nc.gpsimd.tensor_scalar(t["past"], t["past"], 0.0, 0.0, ALU.is_ge, ALU.add))
                total(digits.rearrange("p g t -> p (g t)"), t["past"], E)
                link(nc.gpsimd.tensor_scalar(digits, digits, float(E - 1), 0.0, ALU.min, ALU.add))
                link(nc.gpsimd.tensor_tensor(digits, digits, powers.unsqueeze(1).broadcast_to([P, GROUPS, GT]), ALU.mult))
                total(t["packed"], digits, GT)
                link(nc.gpsimd.tensor_copy(m.owner[:], t["packed"]))
                placed.append(count[0])
                pool.wait_ge(rows_turned, 2 * GROUPS)
                for j in range(2):
                    pool.wait_ge(rows_out[j], 16 * (GROUPS // 2))
                for pair in range(B // PAIR):
                    if pair >= 2:
                        pool.wait_ge(mixed, PAIR * CHOICES * (pair - 1))
                    for c in range(CHOICES):
                        for e in range(PAIR):
                            b = PAIR * pair + e
                            nc.gpsimd.indirect_dma_start(
                                row_tiles(pair % 2)[:, PAIR * c + e], None, k.returned,
                                bass.IndirectOffsetOnAxis(ap=m.slot[:, c, b:b + 1], axis=0)).then_inc(back_in[pair % 2], 16)

            @block.sync
            def _(sp):
                def load(g, j):
                    if late(g, 2):
                        sp.wait_ge(rows_turned, 2 * g - 2)
                    sp.dma_start(row_tiles(j), group_in_dram(k.routed, g)).then_inc(rows_in[j], 16)

                def store(g, j):
                    sp.wait_ge(returned_out, 2 * g + 2)
                    sp.dma_start(group_in_dram(k.returned, g), out_tiles(j)).then_inc(rows_out[j], 16)
                sp.wait_ge(placing, placed[0])
                sp.wait_ge(sent, 16 * B * CHOICES)
                for g in range(4):
                    load(g, g % 2)
                with sp.Fori(0, GROUPS // 2 - 2) as pair:
                    for j in range(2):
                        store(pair * 2 + j, j)
                        load(pair * 2 + (4 + j), j)
                for g in range(GROUPS - 4, GROUPS):
                    store(g, g % 2)
                if layer == 1:
                    with sp.Fori(0, B // PAIR) as pair:
                        sp.wait_ge(mixed, pair * (PAIR * CHOICES) + PAIR * CHOICES)
                        sp.wait_ge(added, pair * PAIR + (PAIR + 1))
                        sp.dma_start(io["out"][bass.ds(pair * PAIR, PAIR)].rearrange("b t d -> t b d"),
                                     k.x[:, bass.ds(pair * PAIR, PAIR)]).then_inc(stored, 16)
                    sp.wait_ge(stored, 16 * (B // PAIR))
                for j in range(2):
                    sp.wait_ge(rows_out[j], 16 * (GROUPS // 2))

            @block.tensor
            def _(pe):
                def experts(g):
                    packed = pe.value_load(m.owner[0:1, bass.ds(g, 1)], min_val=0, max_val=E ** GT - 1)
                    return [pe.snap((packed // E ** u) % E) for u in range(GT)]

                def emit(s, j, skip, front, back, after):
                    i = 1 - j
                    owners = {}

                    def front_(u):
                        if front == MANY and u == 0:
                            owners["front"] = experts(s - FIRST)
                        pe.wait_ge(xs_done, 2 * s + u // 2 + 1)
                        if late(s, 1):
                            k.after(pe, h_done, 4 * s + u - 3)
                        for t in range(DT):
                            w0 = t * UNITS * GU + ((SHARED + owners["front"][u]) if front == MANY else u) * GU
                            x = u if front == MANY else 0
                            for n, (a, w) in enumerate(((xs_hi, k.w_hi), (xs_hi, k.w_lo), (xs_lo, k.w_hi))):
                                mm = pe.matmul(gu[:, u, 0:GU], a[:, x, j, t], w[:, bass.ds(w0, GU)],
                                               start=(t == 0 and n == 0), stop=(t == DT - 1 and n == 2))
                        mm.then_inc(gu_full, 1)

                    def turn_(g):
                        if g == 0:
                            pe.wait_ge(h_done, 4 * s)
                        if front == MANY:
                            pe.wait_ge(xs_done, 2 * s + g + 1)
                        if late(s, 2):
                            pe.wait_ge(hT_done, 2 * s - 3 + g)
                        for n, (c0, _, _) in enumerate(hidden(back, g)):
                            mm = pe.transpose(turned[:, g, n * P:(n + 1) * P], h[:, i, c0:c0 + P], k.ident[:])
                        mm.then_inc(turned_full, 1)

                    def down_(g):
                        if back == ONE:
                            pe.wait_ge(hT_done, 2 * s - 1 + g)
                            if g == 0:
                                if not isinstance(s, int) or s - 1 - skip >= 2:
                                    pe.wait_ge(added, s - 1 - skip)
                                if isinstance(s, int) and s == END_MANY + 1:
                                    pe.wait_ge(returned_out, 2 * GROUPS)
                            for n, (_, _, c) in enumerate(hidden(back, g)):
                                w0 = GW + c * D
                                for q, (a, w) in enumerate(((hT_hi, k.w_hi), (hT_hi, k.w_lo), (hT_lo, k.w_hi))):
                                    mm = pe.matmul(out[:, i, 0:D], a[:, g, n], w[:, w0:w0 + D],
                                                   start=(c == 0 and q == 0), stop=(c == KT - 1 and q == 2))
                            mm.then_inc(down_full, 1)
                        else:
                            r = s - 1 - FIRST
                            if g == 0:
                                owners["back"] = experts(r)
                            if late(s, FIRST + 2):
                                pe.wait_ge(returned_out, 2 * r - 1 + g)
                            elif g == 0:
                                pe.wait_ge(added, FIRST + 1)
                            pe.wait_ge(hT_done, 2 * s - 1 + g)
                            for n, (_, u, c) in enumerate(hidden(back, g)):
                                w0 = owners["back"][u] * (ET * D) + c * D
                                for q, (a, w) in enumerate(((hT_hi, m.down_hi), (hT_hi, m.down_lo), (hT_lo, m.down_hi))):
                                    mm = pe.matmul(out[:, g, u % 2 * D:(u % 2 + 1) * D], a[:, g, n], w[:, bass.ds(w0, D)],
                                                   start=(c == 0 and q == 0), stop=(c == ET - 1 and q == 2))
                            mm.then_inc(down_full, 1)

                    def rows_(g):
                        r = s + 1 - FIRST
                        if g == 0:
                            if isinstance(s, int) and s == FIRST - 1:
                                pe.wait_ge(placing, placed[0])
                            pe.wait_ge(rows_in[i], 8 * (r - i) + 16)
                        for n in range(4):
                            u, t = 2 * g + n // 2, n % 2
                            mm = pe.transpose(turned[:, g, n * P:(n + 1) * P], row_tiles(i)[:, u, t * P:(t + 1) * P], k.ident[:])
                        mm.then_inc(rows_turned, 1)
                    order(front, back, after, front_, turn_, down_, None, rows_, None)
                run(pe, emit)

            @block.scalar
            def _(act):
                def emit(s, j, skip, front, back, after):
                    i = 1 - j

                    def split_(_):
                        if late(s, 1):
                            act.wait_ge(gu_full, 4 * s)
                        nc.scalar.copy(xs_hi[:, 0, i], k.actT[:, :, s + 1 - skip]).then_inc(xs_hi_done, 2)
                    if isinstance(s, int) and s == 0:
                        nc.scalar.copy(xs_hi[:, 0, 0], k.actT[:, :, 0]).then_inc(xs_hi_done, 2)

                    def front_(u):
                        act.wait_ge(gu_full, 4 * s + u + 1)
                        if late(s, 1) or u >= 2:
                            act.wait_ge(h_done, 4 * s + u - 1)
                        nc.scalar.activation(silu[:, u % 2], gu[:, u, 0:UNIT], ACT.Silu).then_inc(silu_done, 1)

                    def turn_(g):
                        act.wait_ge(turned_full, 2 * s - 1 + g)
                        if late(s, 2):
                            act.wait_ge(down_full, 2 * s - 3 + g)
                        n = len(hidden(back, g))
                        nc.scalar.copy(hT_hi[:, g, 0:n], turned[:, g, 0:n * P].rearrange("p (c n) -> p c n", n=P)).then_inc(hi_done, 1)

                    def rows_(g):
                        r = s + 1 - FIRST
                        act.wait_ge(rows_turned, 2 * r + g + 1)
                        if g == 0:
                            act.wait_ge(gu_full, 4 * s)
                        nc.scalar.copy(xs_hi[:, 2 * g:2 * g + 2, i],
                                       turned[:, g].rearrange("p (u t n) -> p u t n", u=2, t=DT)).then_inc(xs_hi_done, 1)

                    def out_(g):
                        r = s - 1 - FIRST
                        act.wait_ge(down_full, 2 * s - 1 + g)
                        if late(s, FIRST + 3):
                            act.wait_ge(rows_out[i], 8 * (r - i))
                        nc.scalar.copy(out_tiles(i)[:, 2 * g:2 * g + 2], out[:, g].rearrange("p (u d) -> p u d", u=2)).then_inc(returned_out, 1)
                    order(front, back, after, front_, turn_, None, split_, rows_, out_)
                run(act, emit)

            @block.vector
            def _(dve):
                dve.sem_inc(added, 1)
                count = [0]

                def link(ins):
                    count[0] += 1
                    ins.then_inc(sharing, 1)
                    dve.wait_ge(sharing, count[0])

                def shares():
                    t = m.spare
                    if layer == 1:
                        link(nc.vector.tensor_scalar(t["part"], t["before"][:, 0:B], float(CAPACITY), None, ALU.is_lt))
                        link(nc.vector.tensor_tensor(t["weight"], t["weight"], t["part"], ALU.mult))
                    for c, one in enumerate(("one1", "one2")):
                        link(nc.vector.tensor_tensor(t["part"], t[one], t["weight"], ALU.mult))
                        link(nc.vector.tensor_reduce(m.share[:, c], t["part"], AX, ALU.add))
                    link(nc.vector.tensor_scalar(m.share[:], m.share[:], gate, None, ALU.mult))

                def emit(s, j, skip, front, back, after):
                    i = 1 - j
                    if isinstance(s, int) and s == 1:
                        shares()

                    def split_(_):
                        dve.wait_ge(xs_hi_done, 2 * s + 4)
                        if late(s, 1):
                            dve.wait_ge(gu_full, 4 * s)
                        nc.vector.tensor_tensor(xs_lo[:, 0, i], k.actT[:, :, s + 1 - skip], xs_hi[:, 0, i].bitcast(F32),
                                                ALU.subtract).then_inc(xs_done, 2)
                    if isinstance(s, int) and s == 0:
                        dve.wait_ge(xs_hi_done, 2)
                        nc.vector.tensor_tensor(xs_lo[:, 0, 0], k.actT[:, :, 0], xs_hi[:, 0, 0].bitcast(F32),
                                                ALU.subtract).then_inc(xs_done, 2)

                    def front_(u):
                        dve.wait_ge(silu_done, 4 * s + u + 1)
                        if u == 0 and late(s, 2):
                            dve.wait_ge(turned_full, 2 * s - 2)
                        dst = h[:, j, u * UNIT:(u + 1) * UNIT]
                        if front == ONE:
                            nc.vector.scalar_tensor_tensor(dst, gu[:, u, UNIT:GU], k.w_shared[:, bass.ds(s - skip, 1)],
                                                           silu[:, u % 2], ALU.mult, ALU.mult).then_inc(h_done, 1)
                        else:
                            nc.vector.tensor_tensor(dst, gu[:, u, UNIT:GU], silu[:, u % 2], ALU.mult).then_inc(h_done, 1)

                    def turn_(g):
                        dve.wait_ge(hi_done, 2 * s - 1 + g)
                        if late(s, 2):
                            dve.wait_ge(down_full, 2 * s - 3 + g)
                        n = len(hidden(back, g))
                        nc.vector.tensor_tensor(hT_lo[:, g, 0:n], turned[:, g, 0:n * P].rearrange("p (c n) -> p c n", n=P),
                                                hT_hi[:, g, 0:n].bitcast(F32), ALU.subtract).then_inc(hT_done, 1)

                    def rows_(g):
                        dve.wait_ge(xs_hi_done, 2 * s + g + 3)
                        if g == 0:
                            dve.wait_ge(gu_full, 4 * s)
                        nc.vector.tensor_tensor(xs_lo[:, 2 * g:2 * g + 2, i], turned[:, g].rearrange("p (u t n) -> p u t n", u=2, t=DT),
                                                xs_hi[:, 2 * g:2 * g + 2, i].bitcast(F32), ALU.subtract).then_inc(xs_done, 1)
                    mixes = skip and late(s, RETURN)

                    def down_(g):
                        if mixes:
                            mix(s - RETURN, j, g)
                    order(front, back, after, front_, turn_, down_, split_, rows_, None)
                    if back == ONE:
                        e = s - 1 - skip
                        dve.wait_ge(down_full, 2 * s)
                        nc.vector.scalar_tensor_tensor(k.x[:, e], out[:, i, 0:D], gate, k.x[:, e],
                                                       ALU.mult, ALU.add).then_inc(added, 1)
                    if isinstance(s, int) and s == STEPS:
                        for c in range(CHOICES):
                            mix(STEPS + 1 - RETURN, 1, c)

                def mix(pair, j, c):
                    if c == 0:
                        dve.wait_ge(back_in[j], 32 * (pair - j) + 64)
                        k.after(dve, added, pair * PAIR + PAIR + 1)
                    else:
                        k.after(dve, mixed, pair * (PAIR * CHOICES) + PAIR)
                    for e in range(PAIR):
                        b = pair * PAIR + e
                        nc.vector.scalar_tensor_tensor(k.x[:, b], row_tiles(j)[:, PAIR * c + e], m.share[:, c, bass.ds(b, 1)],
                                                       k.x[:, b], ALU.mult, ALU.add).then_inc(mixed, 1)
                    if layer == 0 and c == CHOICES - 1:
                        k.after(dve, mixed, pair * (PAIR * CHOICES) + PAIR * CHOICES)
                        for e in range(PAIR):
                            b = pair * PAIR + e
                            nc.vector.bn_stats(k.stats[:, b], k.x[:, b])
                run(dve, emit)


PLAN = (("project", 0), ("exps", 0), ("exps", 1), ("spread", 0), ("exps", 2), ("exps", 3), ("turn", 0),
        ("maxima", 0), ("exps", 4), ("exps", 5), ("maxima", 1), ("values", 0), ("maxima", 2), ("exps", 6),
        ("maxima", 3), ("turn", 1), ("maxima", 4), ("exps", 7), ("maxima", 5), ("maxima", 6),
        ("maxima", 7), ("output", 0), ("values", 1), ("negate", 0))


def phase_attention(k):
    nc, io = k.nc, k.io
    T = G // 4
    SCALE = float(HD) ** -0.5
    OF_FRONT, OF_BACK = ("project", "spread", "maxima", "negate"), ("exps", "values")
    with ExitStack() as ctx:
        wq = k.sb(ctx, "wq", [P, DT, T * P])
        wk = k.sb(ctx, "wk", [P, DT, T, P])
        wv = k.sb(ctx, "wv", [P, DT, G * HD])
        wo = k.sb(ctx, "wo", [P, DT, D])
        bo = k.sb(ctx, "bo", [P, D])
        csel = k.sb(ctx, "csel", [2, P], BF16)
        cfix = k.sb(ctx, "cfix", [2, 2])
        rowfix = k.sb(ctx, "rowfix", [P, 2])
        consts = k.sb(ctx, "consts", [2, B * P], BF16)
        spread = k.sb(ctx, "spread", [P, 2, HG, P], F32R)
        ident16 = k.sb(ctx, "ident16", [P, P], BF16)
        causal = k.sb(ctx, "causal", [P, P], BF16)
        cst = k.sb(ctx, "cst", [P, 2, DT, P])
        k_hi = k.sb(ctx, "k_hi", [P, T, P], F32R)
        q_part = k.sb(ctx, "q_part", [P, 2, T * P], F32R)
        k_st = k.sb(ctx, "k_st", [P, 2, T, 4, P], F32R)
        q_st = k.sb(ctx, "q_st", [P, 2, HG, T, P], F32R)
        vaug = k.sb(ctx, "vaug", [P, 2, G, SLOT])
        mx = k.sb(ctx, "mx", [P, 2, 4, HG, T])
        negT = k.sb(ctx, "negT", [G * HG, P], F32R)
        probs = k.sb(ctx, "probs", [P, G, HG * P])
        oT = k.sb(ctx, "oT", [P, T, HG, P])
        rinv = k.sb(ctx, "rinv", [P, T, HG, 4])
        attn = k.sb(ctx, "attn", [P, G, HG, HD])
        attnT = k.sb(ctx, "attnT", [P, DT, P])
        names = ("loaded", "made", "c_ready", "cst_done", "kv_full", "k_hi_done", "k_done", "v_done", "q_full",
                 "q_hi_done", "q_lo_done", "spread_full", "q0_done", "q1_done", "s1_full", "max_done", "maxT_full",
                 "neg_done", "neg_in", "s2_full", "exp_done", "pv_full", "oT_done", "turn_full", "rinv_done",
                 "attn_done", "attnT_full", "attnT_done", "o_full", "bias_done", "added", "cmask", "masked", "seen")
        (loaded, made, c_ready, cst_done, kv_full, k_hi_done, k_done, v_done, q_full,
         q_hi_done, q_lo_done, spread_full, q0_done, q1_done, s1_full, max_done, maxT_full,
         neg_done, neg_in, s2_full, exp_done, pv_full, oT_done, turn_full, rinv_done,
         attn_done, attnT_full, attnT_done, o_full, bias_done, added, cmask, masked, seen) = (k.sem(ctx, n + "_t") for n in names)
        weights = WeightSplit(k, 1, ctx, 2)
        mask_in = probs[0:2, 0:4].rearrange("p q n -> p (q n)").bitcast(mybir.dt.int32)
        csel_in = attnT[0:2, 0, :]
        spread_in = oT[:].rearrange("p t h n -> p (t h n)")
        LOADS = 10

        with ExitStack() as first:
            nt = NormTurn(k, first, "_q")
            with nc.Block() as block:
                @block.sync
                def _(sp):
                    for dst, src in ((wq, io["wq"]), (wk, io["wk"]), (wv, io["wv"]), (wo, io["wo"]), (attnT[0:2, 0], io["csel"]),
                                     (cfix, io["cfix"]), (rowfix, io["rowfix"])):
                        sp.dma_start(dst[:], src).then_inc(loaded, 16)
                    sp.dma_start(spread_in, io["spread"]).then_inc(loaded, 16)
                    sp.dma_start(bo[:], bass.AP(io["bo"].tensor, 0, [[0, P], [1, D]])).then_inc(loaded, 16)
                    sp.dma_start(mask_in, bass.AP(io["mask"].tensor, 0, [[0, 2], [1, B * P]])).then_inc(loaded, 16)

                @block.gpsimd
                def _(pool):
                    nt.coefficients(pool)
                    nc.gpsimd.memset(vaug[:], 0.0).then_inc(made, 1)
                    nc.gpsimd.memset(causal[:], 0.0).then_inc(made, 1)
                    nc.gpsimd.memset(k_st[:].bitcast(F32), 0.0).then_inc(made, 1)
                    pool.wait_ge(made, 3)
                    nc.gpsimd.memset(vaug[:, :, :, HD:HD + 1], 1.0).then_inc(made, 1)
                    nc.gpsimd.affine_select(out=causal[:], in_=causal[:], compare_op=ALU.is_ge, fill=NEG,
                                            base=0, pattern=[[-1, P]], channel_multiplier=1).then_inc(made, 1)
                    nc.gpsimd.tensor_copy(ident16[:], k.ident[:]).then_inc(made, 1)

                @block.tensor
                def _(pe):
                    nt.turn(pe)

                @block.scalar
                def _(act):
                    nt.copy(act)
                    act.wait_ge(loaded, 16 * LOADS)
                    nc.scalar.copy(spread[:].rearrange("p a h n -> p (a h n)"), spread_in).then_inc(c_ready, 1)

                @block.vector
                def _(dve):
                    nt.normalise(dve)
                    dve.wait_ge(loaded, 16 * LOADS)
                    nc.vector.tensor_copy(csel[:], csel_in).then_inc(c_ready, 1)
                    nc.vector.tensor_scalar(consts[:], mask_in, 0.0, NEG, ALU.is_equal, ALU.mult).then_inc(cmask, 1)
                    dve.wait_ge(cmask, 1)
                    nc.vector.tensor_scalar(consts[:], consts[:], cfix[:, 0:1], cfix[:, 1:2], ALU.mult, ALU.add).then_inc(c_ready, 1)

        bankA = k.ps(ctx, "bankA", [P, 512])
        bankC = k.ps(ctx, "bankC", [P, 512])
        s1 = k.ps(ctx, "s1", [P, 2, 512])
        s2 = k.ps(ctx, "s2", [P, 2, 512])
        oP = k.ps(ctx, "oP", [P, T, 512])
        def run(eng, emit):
            def body(s, j, front, back, tail):
                for part, arg in PLAN:
                    if front if part in OF_FRONT else back if part in OF_BACK else tail:
                        emit(s, j, part, arg)
            body(0, 0, True, False, False)
            body(1, 1, True, True, False)
            with eng.Fori(0, B // 2 - 1) as pair:
                for j in range(2):
                    body(pair * 2 + (2 + j), j, True, True, True)
            body(B, 0, False, True, True)
            body(B + 1, 1, False, False, True)

        def four(mask):
            return mask.unsqueeze(1).broadcast_to([P, 4, P])

        def rows(buf, s):
            return buf[SLOT * s:SLOT * (s + 1)]

        with nc.Block() as block:
            @block.sync
            def _(sp):
                def emit(s, j, part, arg):
                    if part == "project":
                        weights.load(sp, s, j)
                    if part == "negate":
                        sp.wait_ge(neg_done, s + 1)
                        sp.dma_start(q_st[24:P:SLOT, j].bitcast(F32).rearrange("s h t n -> s (h t) n"),
                                     negT[:].bitcast(F32)).then_inc(neg_in, 16)
                run(sp, emit)

            @block.gpsimd
            def _(pool):
                def emit(s, j, part, arg):
                    g = arg
                    if part == "maxima" and g == 4:
                        weights.lo(pool, s, j)
                    elif part == "exps":
                        pool.wait_ge(exp_done, (s - 1) * G + g + 1)
                        pool.sem_inc(seen, 1)
                        nc.gpsimd.affine_select(out=probs[:, g], in_=probs[:, g], compare_op=ALU.is_ge, fill=0.0,
                                                base=0, pattern=[[0, HG], [1, P]], channel_multiplier=-1).then_inc(masked, 1)
                run(pool, emit)

            @block.tensor
            def _(pe):
                pe.sem_inc(attnT_full, 1)

                def emit(s, j, part, arg):
                    i, g, t, slot = 1 - j, arg, arg // 4, arg % 4
                    if part == "project":
                        if late(s, 3):
                            pe.wait_ge(attnT_done, s - 1)
                        for t in range(T):
                            for d in range(DT):
                                mm = pe.matmul(bankA[:, t * P:(t + 1) * P], wq[:, d, t * P:(t + 1) * P], k.actT[:, d, s],
                                               start=(d == 0), stop=(d == DT - 1))
                        mm.then_inc(q_full, 1)
                        if late(s, 1):
                            pe.wait_ge(neg_done, s)
                        for t in range(T):
                            for d in range(DT):
                                pe.matmul(bankC[:, t * P:(t + 1) * P], wk[:, d, t], k.ctxT[:, d, s],
                                          start=(d == 0), stop=False)
                            pe.matmul(bankC[:, t * P:(t + 1) * P], csel[:], consts[:, bass.ds(s * P, P)],
                                      start=False, stop=True)
                        pe.wait_ge(cst_done, s + 1)
                        for d in range(DT):
                            mm = pe.matmul(bankC[:, T * P:T * P + G * HD], cst[:, j, d], wv[:, d],
                                           start=(d == 0), stop=(d == DT - 1))
                        mm.then_inc(kv_full, 1)
                    elif part == "spread":
                        pe.wait_ge(q_hi_done, s + 1)
                        pe.wait_ge(q_lo_done, s + 1)
                        for h in range(HG):
                            for n in range(2):
                                mm = pe.matmul(s1[:, h // 2, h % 2 * T * P:(h % 2 + 1) * T * P], spread[:, n, h],
                                               q_part[:, n], start=(n == 0), stop=(n == 1))
                            if h % 2:
                                mm.then_inc(spread_full, 1)
                    elif part == "maxima":
                        if g == 0:
                            pe.wait_ge(k_done, 4 * s + 4)
                            pe.wait_ge(q0_done, s + 1)
                            pe.wait_ge(q1_done, s + 1)
                        if g >= 2:
                            pe.wait_ge(max_done, s * G + g - 1)
                        pe.matmul(s1[:, g % 2], ident16[:], four(causal[:]), start=True, stop=False, skip_group_check=True)
                        h, t = g // T, g % T
                        pe.matmul(s1[:, g % 2], q_st[:, j, h, t], k_st[:, j, t], start=False, stop=True,
                                  skip_group_check=True).then_inc(s1_full, 1)
                    elif part == "exps":
                        if g == 0:
                            pe.wait_ge(neg_in, s * 16)
                        if late(s, 2) or g >= 2:
                            pe.wait_ge(exp_done, (s - 1) * G + g - 1)
                        pe.matmul(s2[:, g % 2], k_st[:, i, t, slot], q_st[:, i, :, t],
                                  start=True, stop=True).then_inc(s2_full, 1)
                    elif part == "values":
                        t = arg
                        pe.wait_ge(masked, (s - 1) * G + 4 * t + 4)
                        if late(s, 2):
                            pe.wait_ge(oT_done, (s - 2) * T + t + 1)
                        for q in range(4):
                            mm = pe.matmul(oP[SLOT * q:SLOT * (q + 1), t], vaug[:, i, 4 * t + q], probs[:, 4 * t + q],
                                           start=True, stop=True)
                        mm.then_inc(pv_full, 1)
                    elif part == "turn" and arg == 0:
                        pe.wait_ge(oT_done, (s - 1) * T)
                        if late(s, B) and isinstance(s, int):
                            pe.wait_ge(attnT_done, s - 1)
                            pe.wait_ge(added, s - 2)
                            pe.wait_ge(neg_done, B)
                        else:
                            pe.wait_ge(q_lo_done, s + 1)
                            pe.wait_ge(v_done, s + 1)
                            pe.wait_ge(k_done, 4 * s + 4)
                        for t in range(T):
                            for h in range(HG):
                                mm = pe.transpose((bankA, bankC)[t][:, h * P:(h + 1) * P], oT[:, t, h], k.ident[:])
                        mm.then_inc(turn_full, 1)
                    elif part == "turn":
                        pe.wait_ge(attn_done, (s - 1) * T)
                        for d in range(DT):
                            mm = pe.transpose(bankA[:, d * P:(d + 1) * P],
                                              attn[:].rearrange("p g h d -> p (g h d)")[:, d * P:(d + 1) * P], k.ident[:])
                        mm.then_inc(attnT_full, 1)
                    elif part == "output":
                        pe.wait_ge(attnT_done, s)
                        for d in range(DT):
                            mm = pe.matmul(bankC[:, 0:D], attnT[:, d], wo[:, d], start=(d == 0), stop=(d == DT - 1))
                        mm.then_inc(o_full, 1)
                    elif part == "negate":
                        pe.wait_ge(max_done, (s + 1) * G)
                        if late(s, 2):
                            pe.wait_ge(added, s - 1)
                        else:
                            pe.wait_ge(v_done, s + 1)
                        pe.transpose(bankC[0:G * HG, 0:P], mx[:, j].rearrange("p s h t -> p (s h t)"), k.ident[:]).then_inc(maxT_full, 1)
                run(pe, emit)

            @block.scalar
            def _(act):
                act.sem_inc(attnT_done, 1)
                def emit(s, j, part, arg):
                    g = arg
                    if part == "project":
                        act.wait_ge(q_full, s + 1)
                        if late(s, 1):
                            act.wait_ge(spread_full, s * T)
                        nc.scalar.copy(q_part[:, 0], bankA[:, 0:T * P]).then_inc(q_hi_done, 1)
                        act.wait_ge(kv_full, s + 1)
                        if late(s, 1):
                            act.wait_ge(k_done, 4 * s)
                        nc.scalar.copy(k_hi[:], bankC[:, 0:T * P].rearrange("p (t n) -> p t n", t=T)).then_inc(k_hi_done, 1)
                        if late(s, 2):
                            act.wait_ge(pv_full, (s - 1) * T)
                        nc.scalar.copy(vaug[:, j, :, 0:HD], bankC[:, T * P:T * P + G * HD].rearrange("p (g d) -> p g d", g=G)).then_inc(v_done, 1)
                    elif part == "spread":
                        act.wait_ge(spread_full, s * T + 1)
                        if late(s, 2):
                            act.wait_ge(s2_full, (s - 1) * G)
                        nc.scalar.activation(q_st[:, j, 0:2], s1[:, 0].rearrange("p (h t n) -> p h t n", h=2, t=T), ACT.Identity,
                                             bias=rowfix[:, 1:2]).then_inc(q0_done, 1)
                    elif part == "maxima" and g == 3:
                        weights.hi(act, nc.scalar.copy, s, j)
                    elif part == "exps":
                        act.wait_ge(s2_full, (s - 1) * G + g + 1)
                        if late(s, 2):
                            act.wait_ge(pv_full, (s - 2) * T + g // 4 + 1)
                        nc.scalar.activation(probs[:, g], s2[:, g % 2], ACT.Exp, scale=SCALE).then_inc(exp_done, 1)
                    elif part == "values":
                        t = arg
                        act.wait_ge(pv_full, (s - 1) * T + t + 1)
                        if late(s, 2):
                            act.wait_ge(turn_full, s - 1)
                        nc.scalar.copy(oT[:, t], oP[:, t].rearrange("p (h n) -> p h n", h=HG)).then_inc(oT_done, 1)
                    elif part == "turn" and arg == 1:
                        act.wait_ge(attnT_full, s)
                        nc.scalar.copy(attnT[:], bankA[:, 0:D].rearrange("p (t n) -> p t n", t=DT)).then_inc(attnT_done, 1)
                    elif part == "negate":
                        act.wait_ge(maxT_full, s + 1)
                        if late(s, 1):
                            act.wait_ge(neg_in, s * 16)
                        nc.scalar.mul(negT[:], bankC[0:G * HG, 0:P], -1.0).then_inc(neg_done, 1)
                run(act, emit)

            @block.vector
            def _(dve):
                def emit(s, j, part, arg):
                    g = arg
                    if part == "project":
                        if late(s, 2):
                            dve.wait_ge(kv_full, s - 1)
                        nc.vector.tensor_copy(cst[:, j], k.ctxT[:, :, s]).then_inc(cst_done, 1)
                        dve.wait_ge(q_hi_done, s + 1)
                        if late(s, 1):
                            dve.wait_ge(spread_full, s * T)
                        nc.vector.tensor_tensor(q_part[:, 1], bankA[:, 0:T * P], q_part[:, 0].bitcast(F32),
                                                ALU.subtract).then_inc(q_lo_done, 1)
                        dve.wait_ge(k_hi_done, s + 1)
                        dve.wait_ge(v_done, s + 1)
                        if late(s, 2):
                            dve.wait_ge(s2_full, (s - 1) * G)
                        for q in range(4):
                            nc.vector.scalar_tensor_tensor(
                                rows(k_st, q)[:, j, :, q], rows(k_hi, q)[:].bitcast(F32), rows(rowfix, q)[:, 0:1],
                                rows(bankC, q)[:, 0:T * P].rearrange("p (t n) -> p t n", t=T),
                                ALU.mult, ALU.add).then_inc(k_done, 1)
                    elif part == "spread":
                        dve.wait_ge(spread_full, s * T + 2)
                        if late(s, 2):
                            dve.wait_ge(s2_full, (s - 1) * G)
                        nc.vector.tensor_scalar(q_st[:, j, 2:4], s1[:, 1].rearrange("p (h t n) -> p h t n", h=2, t=T),
                                                rowfix[:, 1:2], None, ALU.add).then_inc(q1_done, 1)
                    elif part == "maxima":
                        dve.wait_ge(s1_full, s * G + g + 1)
                        if g == 0 and late(s, 2):
                            dve.wait_ge(maxT_full, s - 1)
                        nc.vector.tensor_reduce(mx[:, j, :, g // T, g % T],
                                                s1[:, g % 2].rearrange("p (q n) -> p q n", q=4), AX,
                                                ALU.max).then_inc(max_done, 1)
                    elif part == "turn" and arg == 0:
                        dve.wait_ge(turn_full, s - 1)
                        for t in range(T):
                            src = (bankA, bankC)[t][:].rearrange("p (h q c) -> p h q c", h=HG, q=4)
                            if late(s, 3):
                                dve.wait_ge(attnT_full, s - 1)
                            nc.vector.reciprocal(rinv[:, t], src[:, :, :, HD]).then_inc(rinv_done, 1)
                            dve.wait_ge(rinv_done, (s - 2) * T + t + 1)
                            nc.vector.tensor_tensor(attn[:, 4 * t:4 * t + 4].rearrange("p q h d -> p h q d"),
                                                    src[:, :, :, 0:HD],
                                                    rinv[:, t].unsqueeze(3).broadcast_to([P, HG, 4, HD]),
                                                    ALU.mult).then_inc(attn_done, 1)
                    elif part == "output":
                        nc.vector.scalar_tensor_tensor(k.x[:, s - 2], bo[:], k.gates[:, 2:3], k.x[:, s - 2],
                                                       ALU.mult, ALU.add).then_inc(bias_done, 1)
                        dve.wait_ge(o_full, s - 1)
                        dve.wait_ge(bias_done, s - 1)
                        nc.vector.scalar_tensor_tensor(k.x[:, s - 2], bankC[:, 0:D], k.gates[:, 2:3], k.x[:, s - 2],
                                                       ALU.mult, ALU.add).then_inc(added, 1)
                        k.after(dve, added, s - 1)
                        nc.vector.bn_stats(k.stats[:, s - 2], k.x[:, s - 2])
                run(dve, emit)


def build(nc, io):
    with ExitStack() as ctx:
        k = Kernel(nc, ctx, io)
        phase_start(k)
        phase_conv(k)
        phase_residual(k)
        phase_mixture(k, 0)
        phase_attention(k)
        phase_mixture(k, 1)


def layouts(v):
    import numpy as np
    one = {"x": v["x"], "ctx": v["ctx_2048"],
           "gates": np.stack([v["g_xattn"], v["g_ffn"]], axis=1).reshape(1, 4),
           "skip": v["L0_xattn_D"].reshape(1, HC)}
    taps = np.zeros((HC, P, D), np.float32)
    for p in range(P):
        taps[:, p, p:] = v["L0_xattn_ssm_kernel"][:, :D - p]
    one["taps"] = taps
    r0 = np.concatenate([v["L0_ffn_W_router"].T, v["L0_ffn_W_sgate"].T], axis=1)
    r1 = np.concatenate([v["L1_ffn_router"], np.zeros((D, 1), np.float32)], axis=1)
    one["routers"] = np.stack([r0, r1]).reshape(2, DT, P, E + 1).transpose(2, 0, 1, 3)
    for layer, (sg, sd, eg, ed) in enumerate((
            ("L0_ffn_Ws_gate_up", "L0_ffn_Ws_down", "L0_ffn_We_gate_up", "L0_ffn_We_down"),
            ("L1_ffn_shared_w_up_gate", "L1_ffn_shared_w_down", "L1_ffn_w_up_gate", "L1_ffn_w_down"))):
        shared = v[sg].reshape(D, 2, SHARED, UNIT).transpose(0, 2, 1, 3).reshape(D, SHARED, GU)
        gu = np.concatenate([shared, v[eg].transpose(1, 0, 2)], axis=1).reshape(DT, P, UNITS * GU)
        down = np.zeros((KT, P, D), np.float32)
        down[:KT - 1] = v[sd][:(KT - 1) * P].reshape(KT - 1, P, D)
        down[KT - 1, KT * P - HID:] = v[sd][(KT - 1) * P:]
        down = down.transpose(1, 0, 2).reshape(P, KT * D)
        expert = np.zeros((E, ET, P, D), np.float32)
        expert[:, 0] = v[ed][:, :P]
        expert[:, 1, ET * P - UNIT:] = v[ed][:, P:]
        one[f"down{layer}"] = expert.transpose(2, 0, 1, 3).reshape(P, ECOLS)
        one[f"w{layer}"] = np.concatenate([gu.transpose(1, 0, 2).reshape(P, DT * UNITS * GU), down], axis=1)
    one["numbers"] = np.concatenate([np.arange(B) * P, np.tri(E).reshape(-1), np.arange(TILES),
                                     float(E) ** np.arange(GT)]).astype(np.float32).reshape(1, NUMBERS)
    one["wq"] = v["L1_xattn_w_q"].T.reshape(DT, P, D).transpose(1, 0, 2)
    wk = v["L1_xattn_w_k"].reshape(2, 4, HD, DT, P)
    wk = np.broadcast_to(wk.transpose(4, 3, 0, 1, 2)[:, :, :, :, None], (P, DT, 2, 4, 3, HD))
    wk = np.concatenate([wk, np.zeros((P, DT, 2, 4, 1, HD), np.float32)], axis=4)
    one["wk"] = wk.reshape(P, DT, 2, P)
    one["wv"] = v["L1_xattn_w_v"].T.reshape(DT, P, G * HD).transpose(1, 0, 2)
    one["wo"] = v["L1_xattn_w_o"].T.reshape(DT, P, D).transpose(1, 0, 2)
    one["bo"] = v["L1_xattn_b_o"].reshape(1, D)
    one["mask"] = v["mask_BxS2_if1"].reshape(1, B * P)
    csel = np.zeros((2, 4, SLOT), np.float32)
    csel[0, :, 24] = 1.0
    csel[1, :, 25] = 1.0
    one["csel"] = csel.reshape(2, P)
    one["cfix"] = np.array([[0.0, 1.0], [1.0, 0.0]], np.float32)
    rowfix = np.zeros((4, SLOT, 2), np.float32)
    rowfix[:, 16:24, 0] = -1.0
    rowfix[:, 25, 1] = 1.0
    one["rowfix"] = rowfix.reshape(P, 2)
    spread = np.zeros((4, HG, HD, 2, HG, 4, SLOT), np.float32)
    for slot in range(4):
        for h in range(HG):
            for d in range(HD):
                spread[slot, h, d, 0, h, slot, [d, 16 + d]] = 1.0
                spread[slot, h, d, 1, h, slot, 8 + d] = 1.0
    one["spread"] = spread.reshape(P, 2 * HG * P)
    return one


def kernel(**inputs):
    import numpy as np
    import concourse.bacc as bacc
    from concourse.bass_utils import run_bass_kernel_spmd

    nc = bacc.Bacc("TRN2", target_bir_lowering=False, num_devices=1)
    arrays, io = {}, {}
    for name, a in layouts({n: np.asarray(a) for n, a in inputs.items()}).items():
        a = np.ascontiguousarray(a)
        arrays[f"in_{name}"] = a
        io[name] = nc.dram_tensor(f"in_{name}", a.shape, mybir.dt.from_np(a.dtype), kind="ExternalInput").ap()
    io["out"] = nc.dram_tensor("out_x", (B, P, D), F32, kind="ExternalOutput").ap()
    build(nc, io)
    return run_bass_kernel_spmd(nc, [arrays], core_ids=[0]).results[0]["out_x"]
```
